# Optimizing a Trainium2 kernel written in Bass

```python
import numpy as np
import jax
import jax.numpy as jnp

def _softmax(x, axis=-1):
    return jax.nn.softmax(x, axis=axis)

def _gelu(x):
    return jax.nn.gelu(x, approximate=True)

def _silu(x):
    return jax.nn.silu(x)

def _sigmoid(x):
    return jax.nn.sigmoid(x)

def _layernorm(x, axis=-1, eps=1e-05):
    m = jnp.mean(x, axis=axis, keepdims=True)
    v = jnp.var(x, axis=axis, keepdims=True)
    return (x - m) / jnp.sqrt(v + eps)

def _scatter_add(tgt, idx, src, axis=0):
    return tgt.at[idx].add(src)

def _segment_sum(src, seg, n):
    return jax.ops.segment_sum(src, seg, n)
kernel_name = 'mk_perceiver_d1_seqx_r8_cf64cf'

def setup_inputs(seed: int=0):
    np.random.seed(seed)
    _w = jnp.asarray

    def _rec_inputs():
        import jax
        import jax.numpy as jnp
        _rk = jax.random.key(seed)
        x = 7.22e-05 + 1 * jax.random.normal(jax.random.fold_in(_rk, 1), (32, 64, 128), jnp.float32)
        _lenS = 64 - jax.random.randint(jax.random.fold_in(_rk, 7), (32,), 0, max(1, 64 // 4) + 1, jnp.int32)
        _lenS2 = 1601 - jax.random.randint(jax.random.fold_in(_rk, 8), (32,), 0, max(1, 1601 // 4) + 1, jnp.int32)
        _ctx_768P = jax.random.normal(jax.random.fold_in(_rk, 11), (32, 16, 96), jnp.float32)
        _ctx_768c = jax.random.dirichlet(jax.random.fold_in(_rk, 511), 0.3 * jnp.ones((16,), jnp.float32), (32, 1601))
        _ctx_768t = jnp.einsum('bsk,bkd->bsd', _ctx_768c, _ctx_768P)
        _ctx_768t = _ctx_768t * jax.lax.rsqrt(jnp.mean(jnp.square(_ctx_768t)) + 1e-12) * 0.953939
        ctx_768 = -0.000191848 + 0.999787 * (_ctx_768t + 0.3 * jax.random.normal(jax.random.fold_in(_rk, 611), (32, 1601, 96), jnp.float32))
        return (x, ctx_768)
    x, ctx_768 = _rec_inputs()

    def _L0_xattn_setup():
        import jax, jax.numpy as jnp
        import numpy as np
        NUM_HEADS = 16
        CLAMP = 10000.0
        key = jax.random.key(seed)
        ks = jax.random.split(key, 8)
        B, Nq, Nkv, Cq, Ckv = (4, 256, 256, 128, 96)
        s_q = 1.0 / np.sqrt(Cq)
        s_kv = 1.0 / np.sqrt(Ckv)
        return {'query': jax.random.normal(ks[0], (B, Nq, Cq), jnp.float32), 'key_value': jax.random.normal(ks[1], (B, Nkv, Ckv), jnp.float32), 'Wq': jax.random.normal(ks[2], (Cq, Cq), jnp.float32) * s_q, 'bq': jnp.zeros((Cq,), jnp.float32), 'Wk': jax.random.normal(ks[3], (Ckv, Cq), jnp.float32) * s_kv, 'bk': jnp.zeros((Cq,), jnp.float32), 'Wv': jax.random.normal(ks[4], (Ckv, Cq), jnp.float32) * s_kv, 'bv': jnp.zeros((Cq,), jnp.float32), 'Wo': jax.random.normal(ks[5], (Cq, Cq), jnp.float32) * s_q, 'bo': jnp.zeros((Cq,), jnp.float32)}
    _L0_xattn_all = _L0_xattn_setup()
    _L0_xattn_in = {k: v for k, v in _L0_xattn_all.items() if k in ('Wq', 'bq', 'Wk', 'bk', 'Wv', 'bv', 'Wo', 'bo')}
    del _L0_xattn_all

    def _L0_attn_setup():
        import jax, jax.numpy as jnp
        import numpy as np
        D_MODEL = 128
        N_HEADS = 16
        D_K = D_MODEL // N_HEADS
        D_HID = 4 * D_MODEL
        GATE_TEMP = 16.0
        RMS_EPS = 1e-06
        LN_EPS = 1e-05

        def _rmsnorm(x, scale):
            norm = jnp.sqrt(jnp.sum(x * x, axis=-1, keepdims=True))
            rms = norm / np.sqrt(x.shape[-1]).astype(np.float32)
            return x / (rms + RMS_EPS) * scale

        def _silu(x):
            return x * jax.nn.sigmoid(x)

        def _gla(x, wq, wk, wv, wg1, bg1, wg2, bg2, wog, bog, wo):
            xb = jnp.swapaxes(x, 0, 1)
            B, T, C = xb.shape
            H, dk = (N_HEADS, D_K)
            q = (xb @ wq.T).reshape(B, T, H, dk)
            k = (xb @ wk.T).reshape(B, T, H, dk)
            v = (xb @ wv.T).reshape(B, T, H, dk)
            gate_hidden = _silu(xb @ wg1.T + bg1)
            alpha = jax.nn.sigmoid((gate_hidden @ wg2.T + bg2) / GATE_TEMP).reshape(B, T, H, dk)
            qT, kT, vT, aT = (jnp.moveaxis(a, 1, 0) for a in (q, k, v, alpha))
            S0 = jnp.zeros((B, H, dk, dk), xb.dtype)

            def step(S, qkva):
                q_t, k_t, v_t, a_t = qkva
                S = a_t[..., None] * S + k_t[..., :, None] * v_t[..., None, :]
                o_t = jnp.einsum('bhk,bhkv->bhv', q_t, S)
                return (S, o_t)
            S_final, oT = jax.lax.scan(step, S0, (qT, kT, vT, aT))
            o = jnp.moveaxis(oT, 0, 1)
            mu = jnp.mean(o, axis=-1, keepdims=True)
            var = jnp.mean((o - mu) ** 2, axis=-1, keepdims=True)
            o = (o - mu) / jnp.sqrt(var + LN_EPS)
            o = o.reshape(B, T, H * dk)
            out_gate = _silu(xb @ wog.T + bog)
            out = o * out_gate @ wo.T
            return (jnp.swapaxes(out, 0, 1), S_final)

        def _reference_tuple_inner(x, scale1, scale2, wq, wk, wv, wg1, bg1, wg2, bg2, wog, bog, wo, w_gate, w_up, w_down):
            attn_out, new_cache = _gla(_rmsnorm(x, scale1), wq, wk, wv, wg1, bg1, wg2, bg2, wog, bog, wo)
            x = x + attn_out
            normed = _rmsnorm(x, scale2)
            ffn = _silu(normed @ w_gate.T) * (normed @ w_up.T) @ w_down.T
            x = x + ffn
            return (x, new_cache)
        key = jax.random.key(seed)
        ks = jax.random.split(key, 20)
        s = 0.02

        def w(k, shape):
            return jax.random.normal(k, shape, dtype=jnp.float32) * s
        inp = {'x': jax.random.normal(ks[0], (256, 4, D_MODEL), dtype=jnp.float32), 'scale1': jnp.ones((D_MODEL,), jnp.float32), 'scale2': jnp.ones((D_MODEL,), jnp.float32), 'wq': w(ks[1], (D_MODEL, D_MODEL)), 'wk': w(ks[2], (D_MODEL, D_MODEL)), 'wv': w(ks[3], (D_MODEL, D_MODEL)), 'wg1': w(ks[4], (16, D_MODEL)), 'bg1': jnp.zeros((16,), jnp.float32), 'wg2': w(ks[5], (D_MODEL, 16)), 'bg2': jnp.zeros((D_MODEL,), jnp.float32), 'wog': w(ks[6], (D_MODEL, D_MODEL)), 'bog': jnp.zeros((D_MODEL,), jnp.float32), 'wo': w(ks[7], (D_MODEL, D_MODEL)), 'w_gate': w(ks[8], (D_HID, D_MODEL)), 'w_up': w(ks[9], (D_HID, D_MODEL)), 'w_down': w(ks[10], (D_MODEL, D_HID))}
        return inp
    _L0_attn_all = _L0_attn_setup()
    _L0_attn_in = {k: v for k, v in _L0_attn_all.items() if k in ('scale1', 'scale2', 'wq', 'wk', 'wv', 'wg1', 'bg1', 'wg2', 'bg2', 'wog', 'bog', 'wo', 'w_gate', 'w_up', 'w_down')}
    del _L0_attn_all

    def _L0_ffn_setup():
        import jax, jax.numpy as jnp
        import numpy as np
        B, T, D = (8, 512, 128)
        NUM_SLOTS = 64
        TOP_K = 8
        DQ = D // 4
        DH = D // 2

        def _forward(x, slot_init, w1, b1, w2, b2, tau, Wih, Whh, bih, bhh, wq, bq, wk, bk, wv, bv, ln_g, ln_b, wvp, bvp, wo, bo):
            Bx, Tx, Dx = x.shape
            S = jnp.broadcast_to(slot_init[None], (Bx, NUM_SLOTS, Dx)).astype(x.dtype)
            slot_mean = jnp.broadcast_to(S.mean(axis=1, keepdims=True), (Bx, Tx, Dx))
            ctx = jnp.concatenate([x, slot_mean], axis=-1)
            h = jax.nn.gelu(ctx @ w1 + b1, approximate=False)
            route_logits = (h @ w2 + b2) / (jnp.abs(tau) + 0.1)
            topk_vals, topk_idx = jax.lax.top_k(route_logits, TOP_K)
            topk_w = jax.nn.softmax(topk_vals, axis=-1)
            alpha = (jax.nn.one_hot(topk_idx, NUM_SLOTS, dtype=x.dtype) * topk_w[..., None]).sum(axis=-2)
            slot_input = jnp.einsum('bts,btd->bsd', alpha, x)
            denom = alpha.sum(axis=1) + 1e-08
            si = slot_input / denom[..., None]
            gi = si @ Wih.T + bih
            gh = S @ Whh.T + bhh
            i_r, i_z, i_n = jnp.split(gi, 3, axis=-1)
            h_r, h_z, h_n = jnp.split(gh, 3, axis=-1)
            r = jax.nn.sigmoid(i_r + h_r)
            z = jax.nn.sigmoid(i_z + h_z)
            n = jnp.tanh(i_n + r * h_n)
            S_new = (1.0 - z) * n + z * S
            q = S_new @ wq + bq
            k = S_new @ wk + bk
            v = S_new @ wv + bv
            scale = DQ ** (-0.5)
            attn = jax.nn.softmax(jnp.einsum('bsq,btq->bst', q, k) * scale, axis=-1)
            S_comm = jnp.einsum('bst,btd->bsd', attn, v)
            y = S_new + S_comm
            mu = y.mean(axis=-1, keepdims=True)
            var = y.var(axis=-1, keepdims=True)
            y = (y - mu) * jax.lax.rsqrt(var + 1e-05) * ln_g + ln_b
            slot_values = y @ wvp + bvp
            out = jnp.einsum('bts,bsd->btd', alpha, slot_values)
            return out @ wo + bo
        key = jax.random.key(seed)
        ks = jax.random.split(key, 24)
        n = lambda k, shp, s=0.02: jax.random.normal(k, shp, dtype=jnp.float32) * s
        return {'x': jax.random.normal(ks[0], (B, T, D), dtype=jnp.float32), 'slot_init': n(ks[1], (NUM_SLOTS, D)), 'w1': n(ks[2], (2 * D, DH)), 'b1': jnp.zeros((DH,)), 'w2': n(ks[3], (DH, NUM_SLOTS)), 'b2': jnp.zeros((NUM_SLOTS,)), 'tau': jnp.ones((1,)), 'Wih': n(ks[4], (3 * D, D)), 'Whh': n(ks[5], (3 * D, D)), 'bih': jnp.zeros((3 * D,)), 'bhh': jnp.zeros((3 * D,)), 'wq': n(ks[6], (D, DQ)), 'bq': jnp.zeros((DQ,)), 'wk': n(ks[7], (D, DQ)), 'bk': jnp.zeros((DQ,)), 'wv': n(ks[8], (D, D)), 'bv': jnp.zeros((D,)), 'ln_g': jnp.ones((D,)), 'ln_b': jnp.zeros((D,)), 'wvp': n(ks[9], (D, D)), 'bvp': jnp.zeros((D,)), 'wo': n(ks[10], (D, D)), 'bo': jnp.zeros((D,))}
    _L0_ffn_all = _L0_ffn_setup()
    _L0_ffn_in = {k: v for k, v in _L0_ffn_all.items() if k in ('slot_init', 'w1', 'b1', 'w2', 'b2', 'tau', 'Wih', 'Whh', 'bih', 'bhh', 'wq', 'bq', 'wk', 'bk', 'wv', 'bv', 'ln_g', 'ln_b', 'wvp', 'bvp', 'wo', 'bo')}
    del _L0_ffn_all
    return {'x': x, 'ctx_768': ctx_768, 'L0_xattn_Wq': _L0_xattn_in['Wq'], 'L0_xattn_bq': _L0_xattn_in['bq'], 'L0_xattn_Wk': _L0_xattn_in['Wk'], 'L0_xattn_bk': _L0_xattn_in['bk'], 'L0_xattn_Wv': _L0_xattn_in['Wv'], 'L0_xattn_bv': _L0_xattn_in['bv'], 'L0_xattn_Wo': _L0_xattn_in['Wo'], 'L0_xattn_bo': _L0_xattn_in['bo'], 'L0_attn_scale1': _L0_attn_in['scale1'], 'L0_attn_scale2': _L0_attn_in['scale2'], 'L0_attn_wq': _L0_attn_in['wq'], 'L0_attn_wk': _L0_attn_in['wk'], 'L0_attn_wv': _L0_attn_in['wv'], 'L0_attn_wg1': _L0_attn_in['wg1'], 'L0_attn_bg1': _L0_attn_in['bg1'], 'L0_attn_wg2': _L0_attn_in['wg2'], 'L0_attn_bg2': _L0_attn_in['bg2'], 'L0_attn_wog': _L0_attn_in['wog'], 'L0_attn_bog': _L0_attn_in['bog'], 'L0_attn_wo': _L0_attn_in['wo'], 'L0_attn_w_gate': _L0_attn_in['w_gate'], 'L0_attn_w_up': _L0_attn_in['w_up'], 'L0_attn_w_down': _L0_attn_in['w_down'], 'L0_ffn_slot_init': _L0_ffn_in['slot_init'], 'L0_ffn_w1': _L0_ffn_in['w1'], 'L0_ffn_b1': _L0_ffn_in['b1'], 'L0_ffn_w2': _L0_ffn_in['w2'], 'L0_ffn_b2': _L0_ffn_in['b2'], 'L0_ffn_tau': _L0_ffn_in['tau'], 'L0_ffn_Wih': _L0_ffn_in['Wih'], 'L0_ffn_Whh': _L0_ffn_in['Whh'], 'L0_ffn_bih': _L0_ffn_in['bih'], 'L0_ffn_bhh': _L0_ffn_in['bhh'], 'L0_ffn_wq': _L0_ffn_in['wq'], 'L0_ffn_bq': _L0_ffn_in['bq'], 'L0_ffn_wk': _L0_ffn_in['wk'], 'L0_ffn_bk': _L0_ffn_in['bk'], 'L0_ffn_wv': _L0_ffn_in['wv'], 'L0_ffn_bv': _L0_ffn_in['bv'], 'L0_ffn_ln_g': _L0_ffn_in['ln_g'], 'L0_ffn_ln_b': _L0_ffn_in['ln_b'], 'L0_ffn_wvp': _L0_ffn_in['wvp'], 'L0_ffn_bvp': _L0_ffn_in['bvp'], 'L0_ffn_wo': _L0_ffn_in['wo'], 'L0_ffn_bo': _L0_ffn_in['bo']}

def reference(x, ctx_768, L0_xattn_Wq, L0_xattn_bq, L0_xattn_Wk, L0_xattn_bk, L0_xattn_Wv, L0_xattn_bv, L0_xattn_Wo, L0_xattn_bo, L0_attn_scale1, L0_attn_scale2, L0_attn_wq, L0_attn_wk, L0_attn_wv, L0_attn_wg1, L0_attn_bg1, L0_attn_wg2, L0_attn_bg2, L0_attn_wog, L0_attn_bog, L0_attn_wo, L0_attn_w_gate, L0_attn_w_up, L0_attn_w_down, L0_ffn_slot_init, L0_ffn_w1, L0_ffn_b1, L0_ffn_w2, L0_ffn_b2, L0_ffn_tau, L0_ffn_Wih, L0_ffn_Whh, L0_ffn_bih, L0_ffn_bhh, L0_ffn_wq, L0_ffn_bq, L0_ffn_wk, L0_ffn_bk, L0_ffn_wv, L0_ffn_bv, L0_ffn_ln_g, L0_ffn_ln_b, L0_ffn_wvp, L0_ffn_bvp, L0_ffn_wo, L0_ffn_bo):
    import jax
    import jax.numpy as jnp

    def _L0_xattn_ref(query, key_value, Wq, bq, Wk, bk, Wv, bv, Wo, bo):
        import jax, jax.numpy as jnp
        import numpy as np
        NUM_HEADS = 16
        CLAMP = 10000.0
        B, Nq, Cq = query.shape
        Nkv = key_value.shape[1]
        H = NUM_HEADS
        D = Cq // H
        scale = D ** (-0.5)
        q = (query @ Wq + bq).reshape(B, Nq, H, D).transpose(0, 2, 1, 3)
        k = (key_value @ Wk + bk).reshape(B, Nkv, H, D).transpose(0, 2, 1, 3)
        v = (key_value @ Wv + bv).reshape(B, Nkv, H, D).transpose(0, 2, 1, 3)
        attn = jnp.einsum('bhqd,bhkd->bhqk', q, k) * scale
        attn = jnp.clip(attn, -CLAMP, CLAMP)
        attn = jax.nn.softmax(attn, axis=-1)
        attn = jnp.where(jnp.any(jnp.isnan(attn)), jnp.asarray(1.0 / Nkv, attn.dtype), attn)
        x = jnp.einsum('bhqk,bhkd->bqhd', attn, v).reshape(B, Nq, Cq)
        return x @ Wo + bo

    def _L0_attn_ref(x, scale1, scale2, wq, wk, wv, wg1, bg1, wg2, bg2, wog, bog, wo, w_gate, w_up, w_down):
        import jax, jax.numpy as jnp
        import numpy as np
        D_MODEL = 128
        N_HEADS = 16
        D_K = D_MODEL // N_HEADS
        D_HID = 4 * D_MODEL
        GATE_TEMP = 16.0
        RMS_EPS = 1e-06
        LN_EPS = 1e-05

        def _rmsnorm(x, scale):
            norm = jnp.sqrt(jnp.sum(x * x, axis=-1, keepdims=True))
            rms = norm / np.sqrt(x.shape[-1]).astype(np.float32)
            return x / (rms + RMS_EPS) * scale

        def _silu(x):
            return x * jax.nn.sigmoid(x)

        def _gla(x, wq, wk, wv, wg1, bg1, wg2, bg2, wog, bog, wo):
            xb = jnp.swapaxes(x, 0, 1)
            B, T, C = xb.shape
            H, dk = (N_HEADS, D_K)
            q = (xb @ wq.T).reshape(B, T, H, dk)
            k = (xb @ wk.T).reshape(B, T, H, dk)
            v = (xb @ wv.T).reshape(B, T, H, dk)
            gate_hidden = _silu(xb @ wg1.T + bg1)
            alpha = jax.nn.sigmoid((gate_hidden @ wg2.T + bg2) / GATE_TEMP).reshape(B, T, H, dk)
            qT, kT, vT, aT = (jnp.moveaxis(a, 1, 0) for a in (q, k, v, alpha))
            S0 = jnp.zeros((B, H, dk, dk), xb.dtype)

            def step(S, qkva):
                q_t, k_t, v_t, a_t = qkva
                S = a_t[..., None] * S + k_t[..., :, None] * v_t[..., None, :]
                o_t = jnp.einsum('bhk,bhkv->bhv', q_t, S)
                return (S, o_t)
            S_final, oT = jax.lax.scan(step, S0, (qT, kT, vT, aT))
            o = jnp.moveaxis(oT, 0, 1)
            mu = jnp.mean(o, axis=-1, keepdims=True)
            var = jnp.mean((o - mu) ** 2, axis=-1, keepdims=True)
            o = (o - mu) / jnp.sqrt(var + LN_EPS)
            o = o.reshape(B, T, H * dk)
            out_gate = _silu(xb @ wog.T + bog)
            out = o * out_gate @ wo.T
            return (jnp.swapaxes(out, 0, 1), S_final)

        def _reference_tuple_inner(x, scale1, scale2, wq, wk, wv, wg1, bg1, wg2, bg2, wog, bog, wo, w_gate, w_up, w_down):
            attn_out, new_cache = _gla(_rmsnorm(x, scale1), wq, wk, wv, wg1, bg1, wg2, bg2, wog, bog, wo)
            x = x + attn_out
            normed = _rmsnorm(x, scale2)
            ffn = _silu(normed @ w_gate.T) * (normed @ w_up.T) @ w_down.T
            x = x + ffn
            return (x, new_cache)
        return _reference_tuple_inner(x, scale1, scale2, wq, wk, wv, wg1, bg1, wg2, bg2, wog, bog, wo, w_gate, w_up, w_down)[0]

    def _L0_ffn_ref(x, slot_init, w1, b1, w2, b2, tau, Wih, Whh, bih, bhh, wq, bq, wk, bk, wv, bv, ln_g, ln_b, wvp, bvp, wo, bo):
        import jax, jax.numpy as jnp
        import numpy as np
        B, T, D = (8, 512, 128)
        NUM_SLOTS = 64
        TOP_K = 8
        DQ = D // 4
        DH = D // 2

        def _forward(x, slot_init, w1, b1, w2, b2, tau, Wih, Whh, bih, bhh, wq, bq, wk, bk, wv, bv, ln_g, ln_b, wvp, bvp, wo, bo):
            Bx, Tx, Dx = x.shape
            S = jnp.broadcast_to(slot_init[None], (Bx, NUM_SLOTS, Dx)).astype(x.dtype)
            slot_mean = jnp.broadcast_to(S.mean(axis=1, keepdims=True), (Bx, Tx, Dx))
            ctx = jnp.concatenate([x, slot_mean], axis=-1)
            h = jax.nn.gelu(ctx @ w1 + b1, approximate=False)
            route_logits = (h @ w2 + b2) / (jnp.abs(tau) + 0.1)
            topk_vals, topk_idx = jax.lax.top_k(route_logits, TOP_K)
            topk_w = jax.nn.softmax(topk_vals, axis=-1)
            alpha = (jax.nn.one_hot(topk_idx, NUM_SLOTS, dtype=x.dtype) * topk_w[..., None]).sum(axis=-2)
            slot_input = jnp.einsum('bts,btd->bsd', alpha, x)
            denom = alpha.sum(axis=1) + 1e-08
            si = slot_input / denom[..., None]
            gi = si @ Wih.T + bih
            gh = S @ Whh.T + bhh
            i_r, i_z, i_n = jnp.split(gi, 3, axis=-1)
            h_r, h_z, h_n = jnp.split(gh, 3, axis=-1)
            r = jax.nn.sigmoid(i_r + h_r)
            z = jax.nn.sigmoid(i_z + h_z)
            n = jnp.tanh(i_n + r * h_n)
            S_new = (1.0 - z) * n + z * S
            q = S_new @ wq + bq
            k = S_new @ wk + bk
            v = S_new @ wv + bv
            scale = DQ ** (-0.5)
            attn = jax.nn.softmax(jnp.einsum('bsq,btq->bst', q, k) * scale, axis=-1)
            S_comm = jnp.einsum('bst,btd->bsd', attn, v)
            y = S_new + S_comm
            mu = y.mean(axis=-1, keepdims=True)
            var = y.var(axis=-1, keepdims=True)
            y = (y - mu) * jax.lax.rsqrt(var + 1e-05) * ln_g + ln_b
            slot_values = y @ wvp + bvp
            out = jnp.einsum('bts,bsd->btd', alpha, slot_values)
            return out @ wo + bo
        return _forward(x, slot_init, w1, b1, w2, b2, tau, Wih, Whh, bih, bhh, wq, bq, wk, bk, wv, bv, ln_g, ln_b, wvp, bvp, wo, bo)
    x = x + _L0_xattn_ref(_layernorm(x, axis=-1), ctx_768, L0_xattn_Wq, L0_xattn_bq, L0_xattn_Wk, L0_xattn_bk, L0_xattn_Wv, L0_xattn_bv, L0_xattn_Wo, L0_xattn_bo)
    x = x + _L0_attn_ref(_layernorm(x, axis=-1), L0_attn_scale1, L0_attn_scale2, L0_attn_wq, L0_attn_wk, L0_attn_wv, L0_attn_wg1, L0_attn_bg1, L0_attn_wg2, L0_attn_bg2, L0_attn_wog, L0_attn_bog, L0_attn_wo, L0_attn_w_gate, L0_attn_w_up, L0_attn_w_down)
    x = x + _L0_ffn_ref(_layernorm(x, axis=-1), L0_ffn_slot_init, L0_ffn_w1, L0_ffn_b1, L0_ffn_w2, L0_ffn_b2, L0_ffn_tau, L0_ffn_Wih, L0_ffn_Whh, L0_ffn_bih, L0_ffn_bhh, L0_ffn_wq, L0_ffn_bq, L0_ffn_wk, L0_ffn_bk, L0_ffn_wv, L0_ffn_bv, L0_ffn_ln_g, L0_ffn_ln_b, L0_ffn_wvp, L0_ffn_bvp, L0_ffn_wo, L0_ffn_bo)
    return x

_drawn_inputs = setup_inputs


def setup_inputs(seed=0):
    import zlib

    import numpy as np

    out = dict(_drawn_inputs(seed))
    spreads = {'L0_xattn_bq': (0.0, 0.355),
     'L0_xattn_bk': (0.0, 2.0),
     'L0_xattn_bv': (0.0, 0.1),
     'L0_xattn_bo': (0.0, 0.1),
     'L0_attn_scale1': (1.0, 0.6),
     'L0_attn_scale2': (1.0, 0.6),
     'L0_attn_bg1': (0.0, 2.0),
     'L0_attn_bg2': (0.0, 2.0),
     'L0_attn_bog': (0.0, 0.8),
     'L0_ffn_b1': (0.0, 2.0),
     'L0_ffn_b2': (0.0, 2.0),
     'L0_ffn_bih': (0.0, 2.0),
     'L0_ffn_bhh': (0.0, 2.0),
     'L0_ffn_bq': (0.0, 2.0),
     'L0_ffn_bk': (0.0, 2.0),
     'L0_ffn_bv': (0.0, 2.0),
     'L0_ffn_ln_g': (1.0, 0.6),
     'L0_ffn_ln_b': (0.0, 2.0),
     'L0_ffn_bvp': (0.0, 2.0),
     'L0_ffn_bo': (0.0, 0.8)}
    factors = {'L0_attn_wq': 4.339,
     'L0_attn_wk': 4.371,
     'L0_attn_wv': 4.377,
     'L0_attn_wg1': 8.0,
     'L0_attn_wg2': 8.0,
     'L0_attn_wog': 4.766,
     'L0_attn_wo': 4.316,
     'L0_attn_w_gate': 8.0,
     'L0_attn_w_up': 8.0,
     'L0_attn_w_down': 8.0,
     'L0_ffn_slot_init': 64.0,
     'L0_ffn_w1': 64.0,
     'L0_ffn_w2': 64.0,
     'L0_ffn_Wih': 41.104,
     'L0_ffn_Whh': 64.0,
     'L0_ffn_wq': 64.0,
     'L0_ffn_wk': 64.0,
     'L0_ffn_wv': 64.0,
     'L0_ffn_wvp': 8.0,
     'L0_ffn_wo': 5.154}
    for name, (base, spread) in spreads.items():
        noise = np.random.default_rng([zlib.crc32(name.encode()), seed]).standard_normal(out[name].shape)
        drawn = base * np.exp(spread * noise) if base else spread * noise
        out[name] = jnp.asarray(drawn.astype(out[name].dtype))
    for name, factor in factors.items():
        out[name] = (out[name] * factor).astype(out[name].dtype)
    return out
```

```python
from contextlib import ExitStack

import numpy as np

import concourse.bass as bass
from concourse import mybir

F32 = mybir.dt.float32
F16 = mybir.dt.float16
I32 = mybir.dt.int32
ALU = mybir.AluOpType
ACT = mybir.ActivationFunctionType
AX = mybir.AxisListType

P = 128
B, NQ, C = 32, 64, 128
NKV, CKV = 1601, 96
H, D = 16, 8
TOK = B * NQ
CH = 512
NC = TOK // CH
NB = -(-NKV // P)
PAIRS = H // 2
SCALE = D ** -0.5
CLAMP = 10000.0
HID = 4 * C
SLOTS = 64
TOPK = 8
DQ = C // 4
NT = TOK // P
PB = CH // NQ
KCH = [(c * CH, min(CH, NKV - c * CH)) for c in range(-(-NKV // CH))]
KBL = [(i * P, min(P, NKV - i * P)) for i in range(NB)]
NSTACK = 16
UNITS = len(KCH) + 4 + 1
SUM_LOW, SUM_HIGH = 1e-10, 1e30


def pack():
    first = [("x_wq", C, C), ("x_wk", CKV, C), ("x_wv", CKV, C), ("mean", P, P), ("head_mask", P, H), ("row_mask", P, 4),
             ("bias_a", P, 4), ("sel_num", P, 4 * P), ("sel_den", P, 4 * P), ("ident", P, P), ("ones", P, P),
             ("x_wo", C, C)]
    second = [("g_wq", C, C), ("g_wk", C, C), ("g_wv", C, D * C), ("g_wg1", C, 16), ("g_wg2", 16, C),
              ("g_wog", C, C), ("g_wo", C, C), ("w_gate", C, HID), ("w_up", C, HID), ("w_down", C, 4 * C),
              ("head_sum", P, D * P), ("head_mean", P, P), ("bias_b", P, 21), ("w1x", C, 64),
              ("w1s", C, 64), ("w2", 64, SLOTS), ("b2", P, SLOTS), ("wih", C, 3 * C), ("whh", C, 3 * C),
              ("s_wq", C, DQ), ("s_wk", C, DQ), ("s_wv", C, C), ("s_wvp", C, C), ("s_wo", C, C),
              ("slots", C, SLOTS)]
    where, widths = {}, []
    for a, group in enumerate((first, second)):
        col = 0
        for name, rows, cols in group:
            where[name] = (a, col, rows, cols)
            col += cols
        widths.append(col)
    return where, widths


WHERE, WIDTHS = pack()
BIAS_A = ["x_bq", "x_bk", "x_bv", "x_bo"]
BIAS_B = ["scale1", "scale2", "bg1", "bg2", "bog", "b1", "bih_r", "bih_z", "bih_n", "bhh_r", "bhh_z",
          "bhh_n", "s_bq", "s_bk", "s_bv", "ln_g", "ln_b", "s_bvp", "s_bo", "tau", "zero"]


def perceiver(nc, x_t, ctx_t, w_a, w_b, out_t, force_general=False):
    with ExitStack() as stack:
        def sb(name, shape, dt=F32):
            return stack.enter_context(nc.sbuf_tensor(name, shape, dt))

        def sem(name):
            return stack.enter_context(nc.semaphore(name))

        WA = sb("WA", [P, WIDTHS[0]])
        WB = sb("WB", [P, WIDTHS[1]])
        X = sb("X", [P, TOK])
        AT = sb("AT", [P, TOK])
        QT = sb("QT", [P, TOK])
        arena = sb("arena", [P, 14 * TOK])
        small = sb("small", [P, 1024])
        flag = sb("flag", [1, 2], I32)
        PS = stack.enter_context(nc.psum_tensor("PS", [P, 8, CH], F32))

        def w(name):
            a, col, rows, cols = WHERE[name]
            return (WA, WB)[a][0:rows, col:col + cols]

        def bias(name, rows=P):
            group, array, names = (("bias_a", WA, BIAS_A) if name in BIAS_A else ("bias_b", WB, BIAS_B))
            col = WHERE[group][1] + names.index(name)
            return array[0:rows, col:col + 1]

        def slot(k, n=1):
            return arena[:, k * TOK:(k + n) * TOK]

        def chunk(buf, c):
            return buf[:, c * CH:(c + 1) * CH]

        used = [0]

        def carve(cols):
            used[0] += cols
            assert used[0] <= 14 * TOK
            return arena[:, used[0] - cols:used[0]]

        def halves(cols):
            return carve(cols // 2).bitcast(F16)

        ctx_sb = [carve(NKV)[0:CKV, :] for _ in range(2)]
        k_parts = halves(2 * NKV).rearrange("p (a k) -> p a k", a=2)
        k_stack0 = used[0]
        k_stack = [halves(4 * NKV).rearrange("p (g k) -> p g k", g=4) for _ in range(2)]
        k_stack1 = used[0]
        v_sb = [carve(NB * PAIRS * 32).rearrange("p (n h m) -> p n h m", n=NB, h=PAIRS) for _ in range(2)]
        q_stack = halves(4 * TOK).rearrange("p (g t) -> p g t", g=4)
        q_bd = [halves(H * NQ).rearrange("p (g h q) -> p g h q", g=4, h=4) for _ in range(2)]
        p_sb = [carve(H * NQ) for _ in range(2)]
        o_sb = [carve(2 * P) for _ in range(2)]
        fast_end = used[0]
        q_parts = halves(2 * TOK).rearrange("p (a t) -> p a t", a=2)
        used[0] = k_stack0
        first_norm = [carve(TOK) for _ in range(2)]
        used[0] = k_stack0
        gk_sb = carve(NKV)
        gq_bd = carve(H * NQ)
        s_sb = carve(NKV)
        pt_sb = carve(NB * P).rearrange("p (n q) -> p n q", n=NB)
        assert used[0] <= k_stack1
        okay = small[:, 0:64]
        okay_a = small[:, 64:128]
        okay_b = small[:, 128:192]
        recip = small[:, 192:256]
        okay_min = small[:, 256:257]
        row_neg = small[:, 258:259]
        ctx_mean = small[0:CKV, 260:292]
        v_mean = small[:, 292:324]
        real = small[:, 324:388]
        real_all = small[:, 388:452]
        real_min = small[:, 452:453]

        class Signals(dict):

            def __missing__(self, name):
                self[name] = sem(name)
                return self[name]

        s = Signals()
        ctx_in = [sem("ctx_in0"), sem("ctx_in1")]
        PE, V, A, G = nc.tensor, nc.vector, nc.scalar, nc.gpsimd
        eps = sb("eps", [P, 1])
        ps = PS

        NORMS = {
            "norm1": (X, AT, first_norm[0], first_norm[1], "mean"),
            "norm2": (X, slot(0), slot(1), slot(2), "mean"),
            "normo": (slot(6), slot(6), slot(7), slot(11), "head_mean"),
            "norm3": (X, slot(0), slot(1), slot(2), "mean"),
            "norms": (slot(9), slot(9), slot(10), slot(11), "mean"),
        }

        ORDER = list(NORMS)

        def base(tag):
            return NC * ORDER.index(tag)

        def norm_ready(tag, c):
            return s["norm_ready"], base(tag) + c + 1

        def norm_pe(pe, tag, src_ready):
            src, dst, centred, square, weight = NORMS[tag]
            for c in range(NC):
                src_ready(c)
                PE.matmul(ps[:, c, :], w(weight), chunk(src, c), start=True, stop=True).then_inc(s["norm_mean"], 1)
            for c in range(NC):
                pe.wait_ge(s["norm_squared"], base(tag) + c + 1)
                PE.matmul(ps[:, c, :], w(weight), chunk(square, c), start=True, stop=True).then_inc(s["norm_var"], 1)

        def norm_act(act, tag):
            src, dst, centred, square, weight = NORMS[tag]
            for c in range(NC):
                act.wait_ge(s["norm_centred"], base(tag) + c + 1)
                A.activation(chunk(square, c), chunk(centred, c), ACT.Square).then_inc(s["norm_squared"], 1)
            for c in range(NC):
                act.wait_ge(s["norm_var"], base(tag) + c + 1)
                A.activation(chunk(square, c), ps[:, c, :], ACT.Sqrt, bias=eps[:, 0:1]).then_inc(s["norm_root"], 1)

        def norm_dve(dve, tag):
            src, dst, centred, square, weight = NORMS[tag]
            for c in range(NC):
                dve.wait_ge(s["norm_mean"], base(tag) + c + 1)
                V.tensor_tensor(chunk(centred, c), chunk(src, c), ps[:, c, :], ALU.subtract)\
                    .then_inc(s["norm_centred"], 1)
            for c in range(NC):
                dve.wait_ge(s["norm_root"], base(tag) + c + 1)
                V.reciprocal(chunk(square, c), chunk(square, c)).then_inc(s["norm_inverse"], 1)
                dve.wait_ge(s["norm_inverse"], base(tag) + c + 1)
                V.tensor_tensor(chunk(dst, c), chunk(centred, c), chunk(square, c), ALU.mult)\
                    .then_inc(s["norm_ready"], 1)

        RMS = {
            "rms1": (slot(0), slot(3), slot(1), "scale1"),
            "rms2": (slot(10), slot(3), slot(1), "scale2"),
        }

        def rms_base(tag):
            return NC * list(RMS).index(tag)

        def rms_pe(pe, tag):
            square = RMS[tag][2]
            for c in range(NC):
                pe.wait_ge(s["rms_squared"], rms_base(tag) + c + 1)
                PE.matmul(ps[:, 4 + c, :], w("mean"), chunk(square, c), start=True, stop=True)\
                    .then_inc(s["rms_mean"], 1)

        def rms_act(act, tag, src_ready):
            src, dst, square, scale = RMS[tag]
            for c in range(NC):
                act.wait_ge(*src_ready(c))
                A.activation(chunk(square, c), chunk(src, c), ACT.Square).then_inc(s["rms_squared"], 1)
            for c in range(NC):
                act.wait_ge(s["rms_mean"], rms_base(tag) + c + 1)
                A.activation(chunk(square, c), ps[:, 4 + c, :], ACT.Sqrt).then_inc(s["rms_root"], 1)

        def rms_dve(dve, tag):
            src, dst, square, scale = RMS[tag]
            for c in range(NC):
                dve.wait_ge(s["rms_root"], rms_base(tag) + c + 1)
                V.tensor_scalar(chunk(square, c), chunk(square, c), 1e-6, None, ALU.add).then_inc(s["rms_step"], 1)
                dve.wait_ge(s["rms_step"], 2 * (rms_base(tag) + c) + 1)
                V.reciprocal(chunk(square, c), chunk(square, c)).then_inc(s["rms_step"], 1)
                dve.wait_ge(s["rms_step"], 2 * (rms_base(tag) + c) + 2)
                V.scalar_tensor_tensor(chunk(dst, c), chunk(src, c), bias(scale), chunk(square, c),
                                       ALU.mult, ALU.mult).then_inc(s["rms_ready"], 1)

        def turn(b, i):
            return UNITS * b + 8 + i

        def pe_keys(u, c, bank):
            k0, n = KCH[c]
            return PE.matmul(ps[:, bank, 0:n], w("x_wk"), ctx_sb[u][:, k0:k0 + n], start=True, stop=True)

        def pe_values(u, g, bank):
            for i in range(4 * g, min(4 * g + 4, NB)):
                k0, n = KBL[i]
                o = (i - 4 * g) * P
                mm = PE.matmul(ps[0:n, bank, o:o + P], ctx_sb[u][:, k0:k0 + n], w("x_wv"), start=True, stop=True)
            return mm

        def dve_keys(dve, c, bank, stacked, high):
            k0, n = KCH[c]
            hi, lo = k_parts[:, 0, k0:k0 + n], k_parts[:, 1, k0:k0 + n]
            if stacked is not None and c == 0:
                dve.wait_ge(s["k_stacked"], stacked)
            V.tensor_scalar(hi, ps[:, bank, 0:n], bias("x_bk"), None, ALU.add).then_inc(s["k_high"], 1)
            dve.wait_ge(s["k_high"], high)
            V.scalar_tensor_tensor(lo, ps[:, bank, 0:n], bias("x_bk"), hi, ALU.add, ALU.subtract)\
                .then_inc(s["turn_out"], 1)

        def g_keys(c):
            k0, n = KCH[c]
            return V.tensor_scalar(gk_sb[:, k0:k0 + n], ps[:, c, 0:n], bias("x_bk"), None, ALU.add)

        def sp_stack(u):
            for g in range(4):
                for c in range(4):
                    nc.sync.dma_start(k_stack[u][32 * c:32 * c + 32, g, :], k_parts[32 * g:32 * g + 32, c % 2, :])\
                        .then_inc(s["k_stacked"], 16)

        def dve_values(u, g, bank):
            n, rows = (4, P) if g < 3 else (1, KBL[-1][1])
            return V.tensor_copy(v_sb[u][0:rows, 4 * g:4 * g + n, :, 0:16],
                                 ps[0:rows, bank, 0:n * P].rearrange("p (n h m) -> p n h m", n=n, h=PAIRS))

        def pe_finish(u, bank):
            for k, name in enumerate(("sel_num", "sel_den")):
                for i in range(4):
                    r, e = i // 2, i % 2
                    mm = PE.matmul(ps[:, bank, k * NQ:(k + 1) * NQ], w(name)[:, i * P:(i + 1) * P],
                                   o_sb[u][:, r * P + e * NQ:r * P + (e + 1) * NQ], start=(i == 0), stop=(i == 3))
            return mm

        def q_blocks(b, u):
            return G.tensor_tensor(q_bd[u], q_stack[:, :, bass.ds(b * NQ, NQ)].unsqueeze(2).broadcast_to([P, 4, 4, NQ]),
                                   w("row_mask").unsqueeze(1).unsqueeze(3).broadcast_to([P, 4, 4, NQ]), ALU.mult)

        def g_q_blocks(b):
            return G.tensor_tensor(gq_bd.rearrange("p (h q) -> p h q", h=H),
                                   QT[:, bass.ds(b * NQ, NQ)].unsqueeze(1).broadcast_to([P, H, NQ]),
                                   w("head_mask").unsqueeze(2).broadcast_to([P, H, NQ]), ALU.mult)

        def pe_pv(pe, b, u, i):
            n, par, rows = NB * b + i, (NB * u + i) % 2, KBL[i][1]
            pe.wait_ge(s["exp_done"], n + 3)
            if i == 0:
                pe.wait_ge(s["acc_out"], b + 1)
            for h in range(PAIRS):
                c, r = h % 4, h // 4
                mm = PE.matmul(ps[32 * c:32 * c + 32, 4 + u, r * P:(r + 1) * P], v_sb[u][0:rows, i, h, :],
                               p_sb[par][0:rows, h * P:(h + 1) * P], start=(i == 0 and r == 0),
                               stop=(i == NB - 1), skip_group_check=True)
                if i == NB - 1 and h == 0:
                    mm.then_inc(s["q_free"], 1)
            mm.then_inc(s["pv_done"], 1)

        def pe_next(pe, j, u, i):
            b = 2 * j + u
            if i == 0:
                pe.wait_ge(ctx_in[1 - u], 16 * (j + 1 + u))
            pe.wait_ge(s["turn_out"], turn(b, i) + 1)
            (pe_keys if i < 4 else pe_values)(1 - u, i % 4, 6 + (u + i) % 2).then_inc(s["turn_ps"], 1)

        def pe_batch(pe, j, u, last):
            b = 2 * j + u
            for i in range(NB + 1):
                if i < NB:
                    n, par = NB * b + i, (NB * u + i) % 2
                    if i == 0:
                        pe.wait_ge(s["q_ready"], b + 1)
                        pe.wait_ge(s["turn_out"], turn(b, 0) + 1)
                        pe.wait_ge(s["k_stacked"], 16 * NSTACK * (b + 1))
                    pe.wait_ge(s["exp_done"], n + 1)
                    k0, rows = KBL[i]
                    for g in range(4):
                        mm = PE.matmul(ps[0:rows, 2 * par + g // 2, (g % 2) * 256:(g % 2 + 1) * 256],
                                       k_stack[u][:, g, k0:k0 + rows],
                                       q_bd[u][:, g, :, :].rearrange("p h q -> p (h q)"), start=True, stop=True)
                    mm.then_inc(s["score_ps"], 1)
                if i == NB and not last:
                    pe_next(pe, j, u, 7)
                if i >= 1:
                    pe_pv(pe, b, u, i - 1)
                if 1 <= i <= 7 and not last:
                    pe_next(pe, j, u, i - 1)
            t = turn(b, 0 if last else 8)
            pe.wait_ge(s["acc_out"], b + 3)
            pe.wait_ge(s["turn_out"], t + 1)
            pe_finish(u, 6 + u).then_inc(s["turn_ps"], 1)

        def act_batch(act, j, u):
            b = 2 * j + u
            for i in range(NB):
                n, par, rows = NB * b + i, (NB * u + i) % 2, KBL[i][1]
                act.wait_ge(s["score_ps"], n + 1)
                act.wait_ge(s["pv_done"], n + 1)
                A.activation(p_sb[par][0:rows, :].rearrange("p (a n) -> p a n", a=2),
                             ps[0:rows, 2 * par:2 * par + 2, :], ACT.Exp).then_inc(s["exp_done"], 1)

        def dve_batch(dve, j, u, last):
            b = 2 * j + u
            if not last:
                for i in range(8):
                    dve.wait_ge(s["turn_ps"], turn(b, i) + 1)
                    if i < 4:
                        dve_keys(dve, i, 6 + (u + i) % 2, 16 * NSTACK * (b + 1), 4 * (b + 1) + i + 1)
                    else:
                        dve_values(1 - u, i % 4, 6 + (u + i) % 2).then_inc(s["turn_out"], 1)
            dve.wait_ge(s["pv_done"], NB * b + NB + 2)
            V.tensor_copy(o_sb[u], ps[:, 4 + u, 0:2 * P]).then_inc(s["acc_out"], 1)
            t = turn(b, 0 if last else 8)
            dve.wait_ge(s["turn_ps"], t + 1)
            num, den = ps[:, 6 + u, 0:NQ], ps[:, 6 + u, NQ:2 * NQ]
            V.reciprocal(recip, den).then_inc(s["sum_step"], 1)
            V.tensor_scalar(okay_a, den, SUM_LOW, None, ALU.is_ge).then_inc(s["sum_step"], 1)
            dve.wait_ge(s["sum_step"], 4 * b + 2)
            V.scalar_tensor_tensor(okay_b, den, SUM_HIGH, okay_a, ALU.is_le, ALU.mult).then_inc(s["sum_step"], 1)
            dve.wait_ge(s["sum_step"], 4 * b + 3)
            V.tensor_tensor(okay, okay, okay_b, ALU.mult).then_inc(s["sum_step"], 1)
            V.tensor_tensor(AT[:, bass.ds(b * NQ, NQ)], num, recip, ALU.mult).then_inc(s["turn_out"], 1)
            dve.wait_ge(s["sum_step"], 4 * b + 4)
            dve.wait_ge(s["turn_out"], t + 3)

        def g_load(sp, b):
            sp.wait_ge(s["g_ctx_free"], b + 1)
            sp.dma_start(ctx_sb[0], ctx_t[bass.ds(b, 1), :, :].rearrange("a c k -> (a c) k")).then_inc(s["g_ctx"], 16)

        def g_pe(pe, b):
            pe.wait_ge(s["g_ctx"], 16 * (b + 1))
            pe.wait_ge(s["g_done"], b + 1)
            for c in range(4):
                pe_keys(0, c, c).then_inc(s["g_k_ps"], 1)
            for g in range(4):
                pe_values(0, g, 4 + g).then_inc(s["g_v_ps"], 1)
            pe.wait_ge(s["g_q"], b + 1)
            pe.wait_ge(s["g_kv_sb"], 8 * (b + 1))
            for h in range(PAIRS):
                n = PAIRS * b + h
                if h >= 1:
                    pe.wait_ge(s["g_pt"], 4 * n)
                for c, (k0, m) in enumerate(KCH):
                    PE.matmul(ps[:, c, 0:m], gq_bd[:, h * P:(h + 1) * P], gk_sb[:, k0:k0 + m],
                              start=True, stop=True).then_inc(s["g_s_ps"], 1)
                pe.wait_ge(s["g_exp"], n + 1)
                for i, (k0, rows) in enumerate(KBL):
                    bank, o = (4 + i // 4, (i % 4) * P) if i < 12 else (3, 0)
                    t = PE.transpose(ps[0:rows, bank, o:o + P], s_sb[:, k0:k0 + rows], w("ident"))
                t.then_inc(s["g_t_ps"], 1)
                pe.wait_ge(s["g_pt"], 4 * (n + 1))
                c, r = h % 4, h // 4
                for i, (k0, rows) in enumerate(KBL):
                    mm = PE.matmul(ps[32 * c:32 * c + 32, 7, r * P:(r + 1) * P], v_sb[0][0:rows, i, h, :],
                                   pt_sb[0:rows, i, :], start=(i == 0 and r == 0), stop=(i == NB - 1),
                                   skip_group_check=True)
                mm.then_inc(s["g_pv"], 1)
            pe.wait_ge(s["g_o"], b + 1)
            pe_finish(0, 6).then_inc(s["g_fin"], 1)

        def g_dve(dve, b):
            for c in range(4):
                dve.wait_ge(s["g_k_ps"], 4 * b + c + 1)
                g_keys(c).then_inc(s["g_kv_sb"], 1)
            for g in range(4):
                dve.wait_ge(s["g_v_ps"], 4 * b + g + 1)
                dve_values(0, g, 4 + g).then_inc(s["g_kv_sb"], 1)
            V.tensor_reduce(ctx_mean[:, bass.ds(b, 1)], ctx_sb[0], AX.X, ALU.add).then_inc(s["g_ctx_free"], 1)
            for h in range(PAIRS):
                n = PAIRS * b + h
                for c, (k0, m) in enumerate(KCH):
                    dve.wait_ge(s["g_s_ps"], 4 * n + c + 1)
                    V.tensor_scalar(s_sb[:, k0:k0 + m], ps[:, c, 0:m], CLAMP, -CLAMP, ALU.min, ALU.max)\
                        .then_inc(s["g_clip"], 1)
                dve.wait_ge(s["g_clip"], 4 * (n + 1))
                V.tensor_reduce(row_neg, s_sb, AX.X, ALU.max, negate=True).then_inc(s["g_max"], 1)
                dve.wait_ge(s["g_t_ps"], n + 1)
                for i in range(3):
                    V.tensor_copy(pt_sb[:, 4 * i:4 * i + 4, :],
                                  ps[:, 4 + i, :].rearrange("p (n q) -> p n q", n=4)).then_inc(s["g_pt"], 1)
                rows = KBL[-1][1]
                V.tensor_copy(pt_sb[0:rows, NB - 1, :], ps[0:rows, 3, 0:P]).then_inc(s["g_pt"], 1)
                dve.wait_ge(s["g_pv"], n + 1)
            V.tensor_copy(o_sb[0], ps[:, 7, 0:2 * P]).then_inc(s["g_o"], 1)
            dve.wait_ge(s["g_fin"], b + 1)
            num, den = ps[:, 6, 0:NQ], ps[:, 6, NQ:2 * NQ]
            V.reciprocal(recip, den).then_inc(s["g_step"], 1)
            V.tensor_scalar(real, den, 0.0, None, ALU.is_gt).then_inc(s["g_step"], 1)
            dve.wait_ge(s["g_step"], 3 * b + 2)
            V.tensor_tensor(real_all, real_all, real, ALU.mult).then_inc(s["g_step"], 1)
            dve.wait_ge(s["g_step"], 3 * b + 3)
            V.tensor_tensor(AT[:, bass.ds(b * NQ, NQ)], num, recip, ALU.mult).then_inc(s["g_done"], 1)
            dve.wait_ge(s["g_done"], b + 2)

        def all_rows(dve, values, worst, i):
            V.tensor_reduce(worst, values, AX.X, ALU.min).then_inc(s["worst"], 1)
            dve.wait_ge(s["count_ps"], i + 1)
            V.tensor_copy(flag[:, i:i + 1], ps[0:1, 5, i:i + 1]).then_inc(s["flag_ready"], 1)

        QS = [slot(1), AT[:, :]]

        def by_query(buf):
            return buf.rearrange("p (b t) -> p t b", t=B)

        def gemm(pe, weight, src, banks, done, ready=None, free=None, c0=0, rows=P):
            for c in range(NC):
                if ready is not None:
                    pe.wait_ge(*(ready(c) if callable(ready) else (s[ready], c + 1)))
                if free is not None:
                    pe.wait_ge(s[free], c + 1)
                PE.matmul(ps[0:rows, banks + c, :], weight, chunk(src, c), start=True, stop=True)\
                    .then_inc(s[done], 1)

        def pe_head_sum(pe, v):
            for c in range(NC):
                pe.wait_ge(s["qs"], NC * v + c + 1)
                if v == 0:
                    pe.wait_ge(s["og"], c + 1)
                PE.matmul(ps[:, 4 + c, :], w("head_sum")[:, v * P:(v + 1) * P], chunk(QS[v % 2], c),
                          start=(v == 0), stop=(v == D - 1)).then_inc(s["osum_ps"], 1)

        hidden = lambda c: slot(4 + c % 2)
        gates = lambda k: slot(7)[:, (k % 4) * CH:(k % 4 + 1) * CH]
        tiles = lambda buf, half, n=64: buf[:, half * 1024:half * 1024 + NT * n].rearrange("p (i s) -> p i s", i=NT)
        logits, replaced = tiles(slot(4), 0), tiles(slot(4), 1)
        expo, mask = tiles(slot(5), 0), tiles(slot(5), 1)
        alpha, top = tiles(slot(6), 0), tiles(slot(6), 1, 8)
        xtok = slot(7).rearrange("p (i d) -> p i d", i=NT)
        att = tiles(slot(11), 0)
        att_in = tiles(slot(11), 1)
        vs = slot(1, 2)[0:64, :].rearrange("p (b d) -> p b d", b=B)
        svp = slot(3, 2)[0:64, :].rearrange("p (b d) -> p b d", b=B)
        slot_sum = small[:, 460:461]
        tau_inv = small[:, 461:462]
        hid_bias = small[0:64, 462:463]
        gh = small[:, 512:704].rearrange("p (k s) -> p k s", k=3)
        row16 = small[:, 704:720]
        row16b = small[:, 720:736]

        def over_batches(tile):
            return tile.unsqueeze(1).broadcast_to([P, PB, SLOTS])

        block = stack.enter_context(nc.Block())
        HALF = B // 2

        @block.sync
        def _(sp):
            sp.dma_start(X[:, :], x_t).then_inc(s["x_in"], 16)
            sp.dma_start(WA[:, :], w_a).then_inc(s["wa_in"], 16)
            for u in range(2):
                sp.dma_start(ctx_sb[u], ctx_t[u, :, :]).then_inc(ctx_in[u], 16)
            sp.wait_ge(s["q_parted"], 2 * NC)
            for g in range(4):
                for c in range(4):
                    sp.dma_start(q_stack[32 * c:32 * c + 32, g, :], q_parts[32 * g:32 * g + 32, c // 2, :])\
                        .then_inc(s["q_stacked"], 16)
            sp.wait_ge(s["turn_out"], 4 + 2)
            sp_stack(0)
            sp.dma_start(WB[:, :], w_b).then_inc(s["wb_in"], 16)
            with sp.Fori(0, HALF - 1) as j:
                for u in range(2):
                    sp.wait_ge(s["turn_out"], UNITS * (2 * j + u) + 8 + 4 + 2)
                    sp_stack(1 - u)
                    sp.wait_ge(s["turn_ps"], UNITS * (2 * j + u) + 8)
                    sp.dma_start(ctx_sb[u], ctx_t[bass.ds(2 * j + u + 2, 1), :, :].rearrange("a c k -> (a c) k"))\
                        .then_inc(ctx_in[u], 16)
            sp.wait_ge(s["turn_out"], UNITS * (B - 2) + 8 + 4 + 2)
            sp_stack(1)
            sp.wait_ge(s["flag_ready"], 1)
            f = sp.value_load(flag[0:1, 0:1])
            with sp.If(f < P):
                with sp.Fori(0, B) as b:
                    g_load(sp, b)
            for c in range(NC):
                sp.wait_ge(s["final"], c + 1)
                sp.dma_start(out_t[:, c * CH:(c + 1) * CH], chunk(AT, c)).then_inc(s["out_done"], 16)
            sp.wait_ge(s["out_done"], 16 * NC)

        @block.gpsimd
        def _(pool):
            for u in range(2):
                G.memset(v_sb[u][:, :, :, 16:32], 1.0).then_inc(s["ones_set"], 1)
            pool.wait_ge(s["q_stacked"], 16 * NSTACK)
            with pool.Fori(0, HALF) as j:
                for u in range(2):
                    pool.wait_ge(s["q_free"], 2 * j + u + 1)
                    q_blocks(2 * j + u, u).then_inc(s["q_ready"], 1)
            pool.wait_ge(s["flag_ready"], 1)
            f = pool.value_load(flag[0:1, 0:1])
            with pool.If(f < P):
                with pool.Fori(0, B) as b:
                    pool.wait_ge(s["g_done"], b + 1)
                    g_q_blocks(b).then_inc(s["g_q"], 1)
            for v in range(D):
                for c in range(NC):
                    pool.wait_ge(s["scan"], v + 1)
                    if v >= 2:
                        pool.wait_ge(s["osum_ps"], NC * (v - 2) + c + 1)
                    G.tensor_tensor(chunk(QS[v % 2], c).rearrange("p (t b) -> p t b", b=NQ),
                                    chunk(slot(4), c).rearrange("p (t b) -> p t b", b=NQ),
                                    by_query(slot(11 + v % 2))[:, 8 * c:8 * c + 8, :], ALU.mult)\
                        .then_inc(s["qs"], 1)
            for c in range(NC):
                pool.wait_ge(s["x2"], c + 1)
                G.tensor_tensor(chunk(X, c), chunk(X, c), chunk(slot(10), c), ALU.add).then_inc(s["x12"], 1)

        @block.tensor
        def _(pe):
            PE.sem_inc(s["pv_done"], 2)
            PE.sem_inc(s["q_free"], 2)
            pe.wait_ge(s["wa_in"], 16)
            norm_pe(pe, "norm1", lambda c: pe.wait_ge(s["x_in"], 16))
            gemm(pe, w("x_wq"), AT, 4, "q_ps", ready=lambda c: norm_ready("norm1", c))
            pe.wait_ge(ctx_in[0], 16)
            pe.wait_ge(s["q_sb"], NC)
            for i in range(8):
                pe.wait_ge(s["turn_out"], i + 1)
                (pe_keys if i < 4 else pe_values)(0, i % 4, 6 + i % 2).then_inc(s["turn_ps"], 1)
            pe.wait_ge(s["ones_set"], 2)
            with pe.Fori(0, HALF - 1) as j:
                for u in range(2):
                    pe_batch(pe, j, u, False)
            for u in range(2):
                pe_batch(pe, HALF - 1, u, u == 1)
            pe.wait_ge(s["worst"], 1)
            PE.matmul(ps[0:1, 5, 0:1], okay_min, w("ones")[:, 0:1], start=True, stop=True).then_inc(s["count_ps"], 1)
            pe.wait_ge(s["flag_ready"], 1)
            f = pe.value_load(flag[0:1, 0:1])
            with pe.If(f < P):
                with pe.Fori(0, B) as b:
                    g_pe(pe, b)
                pe.wait_ge(s["worst"], 2)
                PE.matmul(ps[0:1, 5, 1:2], real_min, w("ones")[:, 0:1], start=True, stop=True)\
                    .then_inc(s["count_ps"], 1)
                PE.matmul(ps[:, 4, 0:B], w("x_wv"), ctx_mean, start=True, stop=True).then_inc(s["v_mean_ps"], 1)
            gemm(pe, w("x_wo"), AT, 4, "xo_ps", ready="ao")
            norm_pe(pe, "norm2", lambda c: pe.wait_ge(s["x1"], c + 1))
            pe.wait_ge(s["wb_in"], 16)
            rms_pe(pe, "rms1")
            gemm(pe, w("g_wq"), slot(3), 0, "gq_ps", ready=lambda c: (s["rms_ready"], c + 1))
            gemm(pe, w("g_wk"), slot(3), 4, "gk_ps")
            gemm(pe, w("g_wg1"), slot(3), 0, "g1_ps", free="gq", rows=16)
            gemm(pe, w("g_wog"), slot(3), 4, "og_ps", free="gk")
            gemm(pe, w("g_wg2"), slot(2)[0:16, :], 0, "g2_ps", ready="g1", free="g1")
            for v in range(D):
                for c in range(NC):
                    if v == 0:
                        pe.wait_ge(s["decay"], c + 1)
                    else:
                        pe.wait_ge(s["kv"], NC * (v - 1) + c + 1)
                    PE.matmul(ps[:, c, :], w("g_wv")[:, v * P:(v + 1) * P], chunk(slot(3), c),
                              start=True, stop=True).then_inc(s["vv_ps"], 1)
                if v >= 1:
                    pe_head_sum(pe, v - 1)
            pe_head_sum(pe, D - 1)
            norm_pe(pe, "normo", lambda c: pe.wait_ge(s["o"], c + 1))
            gemm(pe, w("g_wo"), slot(9), 4, "wo_ps", ready="gated")
            rms_pe(pe, "rms2")
            for c in range(NC):
                pe.wait_ge(s["rms_ready"], NC + c + 1)
                for m in range(4):
                    k = 4 * c + m
                    if k >= 2:
                        pe.wait_ge(s["hid"], k - 1)
                    PE.matmul(ps[:, k % 2, :], w("w_gate")[:, m * P:(m + 1) * P], chunk(slot(3), c),
                              start=True, stop=True).then_inc(s["gate_ps"], 1)
                    PE.matmul(ps[:, 2 + k % 2, :], w("w_up")[:, m * P:(m + 1) * P], chunk(slot(3), c),
                              start=True, stop=True).then_inc(s["up_ps"], 1)
                for m in range(4):
                    pe.wait_ge(s["hid"], 4 * c + m + 1)
                    mm = PE.matmul(ps[:, 4 + c, :], w("w_down")[:, m * C:(m + 1) * C],
                                   hidden(c)[:, m * CH:(m + 1) * CH], start=(m == 0), stop=(m == 3))
                mm.then_inc(s["down_ps"], 1)
            norm_pe(pe, "norm3", lambda c: pe.wait_ge(s["x3"], c + 1))
            pe.wait_ge(s["slot_sum"], 1)
            PE.matmul(ps[0:64, 4, 0:1], w("w1s"), slot_sum, start=True, stop=True).then_inc(s["hb_ps"], 1)
            pe.wait_ge(s["hb"], 1)
            gemm(pe, w("w1x"), slot(0), 4, "h_ps", ready=lambda c: norm_ready("norm3", c), rows=64)
            for i in range(NT):
                if i == 0:
                    pe.wait_ge(*norm_ready("norm3", NC - 1))
                pe.wait_ge(s["h"], i // 4 + 1)
                PE.matmul(ps[:, i // 8, (i % 8) * 64:(i % 8 + 1) * 64], slot(3)[0:64, i * P:(i + 1) * P], w("w2"),
                          start=True, stop=True).then_inc(s["logit_ps"], 1)
            for i in range(NT):
                PE.transpose(ps[:, 4 + i // 4, (i % 4) * P:(i % 4 + 1) * P], slot(0)[:, i * P:(i + 1) * P], w("ident"))\
                    .then_inc(s["xt_ps"], 1)
            pe.wait_ge(s["alpha"], 1)
            for i in range(NT):
                PE.transpose(ps[0:64, i // 4, (i % 4) * P:(i % 4 + 1) * P], alpha[:, i, :], w("ident"))\
                    .then_inc(s["at_ps"], 1)
            pe.wait_ge(s["xt"], NC)
            for u in range(2):
                for i in range(NT):
                    mm = PE.matmul(ps[:, 4 + 2 * u + i // 8, (i % 8) * 64:(i % 8 + 1) * 64],
                                   xtok[64 * u:64 * u + 64, i, :], alpha[64 * u:64 * u + 64, i, :],
                                   start=True, stop=True)
                mm.then_inc(s["si_ps"], 1)
            pe.wait_ge(s["at"], NC)
            for u in range(2):
                for i in range(NT):
                    mm = PE.matmul(ps[:, 2 * u + i // 8, (i % 8) * 64:(i % 8 + 1) * 64],
                                   w("ones")[64 * u:64 * u + 64, :], alpha[64 * u:64 * u + 64, i, :],
                                   start=True, stop=True)
                mm.then_inc(s["sd_ps"], 1)
            pe.wait_ge(s["sd"], 4)
            pe.wait_ge(s["si"], 4)
            for k in range(3):
                mm = PE.matmul(ps[:, 0, k * 64:(k + 1) * 64], w("whh")[:, k * P:(k + 1) * P], w("slots"),
                               start=True, stop=True)
            mm.then_inc(s["gh_ps"], 1)
            gemm(pe, w("wih")[:, 0:P], slot(9), 4, "gr_ps", free=None)
            pe.wait_ge(s["gh"], 3)
            gemm(pe, w("wih")[:, P:2 * P], slot(9), 0, "gz_ps")
            gemm(pe, w("wih")[:, 2 * P:3 * P], slot(9), 4, "gn_ps", free="r_in")
            gemm(pe, w("s_wq"), slot(5), 0, "sq_ps", ready="snew", rows=DQ)
            gemm(pe, w("s_wk"), slot(5), 4, "sk_ps", rows=DQ)
            pe.wait_ge(s["sk"], NC)
            pe.wait_ge(s["sq"], NC)
            for b in range(B):
                mm = PE.matmul(ps[64 * (b % 2):64 * (b % 2) + 64, b // 16, (b // 2 % 8) * 64:(b // 2 % 8 + 1) * 64],
                               slot(9)[0:DQ, b * 64:(b + 1) * 64], slot(10)[0:DQ, b * 64:(b + 1) * 64],
                               start=True, stop=True)
            mm.then_inc(s["sc_ps"], 1)
            for b in range(B):
                if b >= 16 and b % 4 == 0:
                    pe.wait_ge(s["sv"], (b - 16) // 4 + 1)
                mm = PE.matmul(ps[0:64, 4 + b // 4 % 4, (b % 4) * P:(b % 4 + 1) * P], slot(5)[:, b * 64:(b + 1) * 64],
                               w("s_wv"), start=True, stop=True)
                if b % 4 == 3:
                    mm.then_inc(s["sv_ps"], 1)
            pe.wait_ge(s["attn"], 1)
            for i in range(NT):
                t = PE.transpose(ps[0:64, i // 4, (i % 4) * P:(i % 4 + 1) * P], att[:, i, :], w("ident"))
                if i % 4 == 3:
                    t.then_inc(s["attt_ps"], 1)
            for b in range(B):
                if b % PB == 0:
                    pe.wait_ge(s["sv"], 8)
                    pe.wait_ge(s["attt"], b // PB + 1)
                mm = PE.matmul(ps[:, 4 + b // PB, (b % PB) * 64:(b % PB + 1) * 64], vs[:, b, :],
                               slot(12)[0:64, b * 64:(b + 1) * 64], start=True, stop=True)
                if b % PB == PB - 1:
                    mm.then_inc(s["comm_ps"], 1)
            norm_pe(pe, "norms", lambda c: pe.wait_ge(s["y"], c + 1))
            for b in range(B):
                if b % 4 == 0:
                    pe.wait_ge(s["y2"], b // PB + 1)
                    if b >= 16:
                        pe.wait_ge(s["svp"], (b - 16) // 4 + 1)
                mm = PE.matmul(ps[0:64, 4 + b // 4 % 4, (b % 4) * P:(b % 4 + 1) * P], slot(10)[:, b * 64:(b + 1) * 64],
                               w("s_wvp"), start=True, stop=True)
                if b % 4 == 3:
                    mm.then_inc(s["svp_ps"], 1)
            for b in range(B):
                if b % 4 == 0:
                    pe.wait_ge(s["svp"], b // 4 + 1)
                mm = PE.matmul(ps[:, b // PB, (b % PB) * 64:(b % PB + 1) * 64], svp[:, b, :],
                               slot(8)[0:64, b * 64:(b + 1) * 64], start=True, stop=True)
                if b % PB == PB - 1:
                    mm.then_inc(s["read_ps"], 1)
            pe.wait_ge(s["svp"], 8)
            gemm(pe, w("s_wo"), slot(11), 4, "fin_ps", ready="read")

        @block.scalar
        def _(act):
            A.sem_inc(s["exp_done"], 2)
            act.wait_ge(s["eps_set"], 1)
            norm_act(act, "norm1")
            with act.Fori(0, HALF) as j:
                for u in range(2):
                    act_batch(act, j, u)
            act.wait_ge(s["flag_ready"], 1)
            f = act.value_load(flag[0:1, 0:1])
            with act.If(f < P):
                with act.Fori(0, B) as b:
                    for h in range(PAIRS):
                        act.wait_ge(s["g_max"], PAIRS * b + h + 1)
                        A.activation(s_sb, s_sb, ACT.Exp, bias=row_neg).then_inc(s["g_exp"], 1)
            norm_act(act, "norm2")
            rms_act(act, "rms1", lambda c: norm_ready("norm2", c))
            for c in range(NC):
                act.wait_ge(s["gq_ps"], c + 1)
                A.copy(chunk(slot(4), c), ps[:, c, :]).then_inc(s["gq"], 1)
            for c in range(NC):
                act.wait_ge(s["g1_ps"], c + 1)
                A.activation(chunk(slot(2), c)[0:16, :], ps[0:16, c, :], ACT.Silu, bias=bias("bg1", 16))\
                    .then_inc(s["g1"], 1)
            for c in range(NC):
                act.wait_ge(s["og_ps"], c + 1)
                A.activation(chunk(slot(8), c), ps[:, 4 + c, :], ACT.Silu, bias=bias("bog")).then_inc(s["og"], 1)
            act.wait_ge(s["bg2_scaled"], 1)
            for c in range(NC):
                act.wait_ge(s["g2_ps"], c + 1)
                A.activation(by_query(slot(7))[:, 8 * c:8 * c + 8, :],
                             ps[:, c, :].rearrange("p (t b) -> p t b", b=NQ), ACT.Sigmoid,
                             bias=small[:, 463:464], scale=1.0 / 16.0).then_inc(s["decay"], 1)
            for c in range(NC):
                act.wait_ge(s["osum_ps"], NC * (D - 1) + c + 1)
                A.copy(chunk(slot(6), c), ps[:, 4 + c, :]).then_inc(s["o"], 1)
            norm_act(act, "normo")
            rms_act(act, "rms2", lambda c: (s["x2"], c + 1))
            for k in range(16):
                act.wait_ge(s["gate_ps"], k + 1)
                if k >= 4:
                    act.wait_ge(s["hid"], k - 3)
                A.activation(gates(k), ps[:, k % 2, :], ACT.Silu).then_inc(s["gate"], 1)
            norm_act(act, "norm3")
            act.wait_ge(s["hb"], 1)
            for c in range(NC):
                act.wait_ge(s["h_ps"], c + 1)
                A.activation(chunk(slot(3), c)[0:64, :], ps[0:64, 4 + c, :], ACT.Gelu, bias=hid_bias)\
                    .then_inc(s["h"], 1)
            for c in range(NC):
                act.wait_ge(s["xt_ps"], 4 * c + 4)
                A.copy(chunk(slot(7), c), ps[:, 4 + c, :]).then_inc(s["xt"], 1)
            act.wait_ge(s["shifted"], 1)
            A.activation(expo, expo, ACT.Exp).then_inc(s["expo"], 1)
            for c in range(NC):
                act.wait_ge(s["at_ps"], 4 * c + 4)
                A.copy(chunk(slot(8), c)[0:64, :], ps[0:64, c, :]).then_inc(s["at"], 1)
            for c in range(NC):
                act.wait_ge(s["r_in"], c + 1)
                A.activation(chunk(slot(1), c), chunk(slot(1), c), ACT.Sigmoid).then_inc(s["r"], 1)
            for c in range(NC):
                act.wait_ge(s["z_in"], c + 1)
                A.activation(chunk(slot(2), c), chunk(slot(2), c), ACT.Sigmoid).then_inc(s["z"], 1)
            for c in range(NC):
                act.wait_ge(s["n_in"], c + 1)
                A.activation(chunk(slot(3), c), chunk(slot(3), c), ACT.Tanh, bias=bias("bih_n")).then_inc(s["n"], 1)
            for c in range(NC):
                act.wait_ge(s["sq_ps"], c + 1)
                A.activation(chunk(slot(9), c)[0:DQ, :], ps[0:DQ, c, :], ACT.Identity, bias=bias("s_bq", DQ))\
                    .then_inc(s["sq"], 1)
            for c in range(NC):
                act.wait_ge(s["sk_ps"], c + 1)
                A.activation(chunk(slot(10), c)[0:DQ, :], ps[0:DQ, 4 + c, :], ACT.Identity, bias=bias("s_bk", DQ))\
                    .then_inc(s["sk"], 1)
            act.wait_ge(s["att_in"], 1)
            A.activation(att_in, att_in, ACT.Exp, scale=DQ ** -0.5).then_inc(s["att_exp"], 1)
            for g in range(8):
                act.wait_ge(s["sv_ps"], g + 1)
                A.copy(vs[:, 4 * g:4 * g + 4, :], ps[0:64, 4 + g % 4, :].rearrange("p (b d) -> p b d", b=4))\
                    .then_inc(s["sv"], 1)
            norm_act(act, "norms")
            for g in range(8):
                act.wait_ge(s["svp_ps"], g + 1)
                A.copy(svp[:, 4 * g:4 * g + 4, :], ps[0:64, 4 + g % 4, :].rearrange("p (b d) -> p b d", b=4))\
                    .then_inc(s["svp"], 1)
            for c in range(NC):
                act.wait_ge(s["read_ps"], c + 1)
                A.activation(chunk(slot(11), c), ps[:, c, :], ACT.Identity, bias=bias("s_bvp")).then_inc(s["read"], 1)

        @block.vector
        def _(dve):
            V.sem_inc(s["turn_out"], 2)
            V.sem_inc(s["acc_out"], 2)
            V.sem_inc(s["g_ctx_free"], 1)
            V.sem_inc(s["g_done"], 1)
            V.memset(eps[:, :], 1e-5).then_inc(s["eps_set"], 1)
            V.memset(okay, 1.0).then_inc(s["okay_set"], 1)
            V.memset(real_all, 1.0).then_inc(s["okay_set"], 1)
            norm_dve(dve, "norm1")
            for c in range(NC):
                dve.wait_ge(s["q_ps"], c + 1)
                V.tensor_scalar(chunk(QT, c), ps[:, 4 + c, :], bias("x_bq"), SCALE, ALU.add, ALU.mult)\
                    .then_inc(s["q_sb"], 1)
                dve.wait_ge(s["q_sb"], c + 1)
                V.tensor_copy(chunk(q_parts[:, 0, :], c), chunk(QT, c)).then_inc(s["q_parted"], 1)
                dve.wait_ge(s["q_parted"], 2 * c + 1)
                V.tensor_tensor(chunk(q_parts[:, 1, :], c), chunk(QT, c), chunk(q_parts[:, 0, :], c), ALU.subtract)\
                    .then_inc(s["q_parted"], 1)
            for i in range(8):
                dve.wait_ge(s["turn_ps"], i + 1)
                if i < 4:
                    dve_keys(dve, i, 6 + i % 2, None, i + 1)
                else:
                    dve_values(0, i % 4, 6 + i % 2).then_inc(s["turn_out"], 1)
            dve.wait_ge(s["okay_set"], 2)
            with dve.Fori(0, HALF - 1) as j:
                for u in range(2):
                    dve_batch(dve, j, u, False)
            for u in range(2):
                dve_batch(dve, HALF - 1, u, u == 1)
            all_rows(dve, okay, okay_min, 0)
            dve.wait_ge(s["flag_ready"], 1)
            f = dve.value_load(flag[0:1, 0:1])
            with dve.If(f < P):
                with dve.Fori(0, B) as b:
                    g_dve(dve, b)
                all_rows(dve, real_all, real_min, 1)
                dve.wait_ge(s["v_mean_ps"], 1)
                V.tensor_scalar(v_mean, ps[:, 4, 0:B], 1.0 / NKV, None, ALU.mult).then_inc(s["v_mean"], 1)
                dve.wait_ge(s["v_mean"], 1)
                dve.wait_ge(s["flag_ready"], 2)
                nan = dve.value_load(flag[0:1, 1:2])
                with dve.If(nan < P):
                    V.tensor_copy(AT[:, :].rearrange("p (b q) -> p b q", b=B),
                                  v_mean.unsqueeze(2).broadcast_to([P, B, NQ])).then_inc(s["v_mean"], 1)
                    dve.wait_ge(s["v_mean"], 2)
                V.sem_inc(s["g_end"], 1)
            for c in range(NC):
                V.tensor_scalar(chunk(AT, c), chunk(AT, c), bias("x_bv"), None, ALU.add).then_inc(s["ao"], 1)
            for c in range(NC):
                dve.wait_ge(s["xo_ps"], c + 1)
                V.scalar_tensor_tensor(chunk(X, c), ps[:, 4 + c, :], bias("x_bo"), chunk(X, c), ALU.add, ALU.add)\
                    .then_inc(s["x1"], 1)
            norm_dve(dve, "norm2")
            dve.wait_ge(s["wb_in"], 16)
            V.tensor_scalar(small[:, 463:464], bias("bg2"), 1.0 / 16.0, None, ALU.mult).then_inc(s["bg2_scaled"], 1)
            rms_dve(dve, "rms1")
            for c in range(NC):
                dve.wait_ge(s["gk_ps"], c + 1)
                V.tensor_copy(chunk(slot(5), c), ps[:, 4 + c, :]).then_inc(s["gk"], 1)
            dve.wait_ge(s["decay"], NC)
            dve.wait_ge(s["gk"], NC)
            V.memset(slot(7).rearrange("p (b t) -> p b t", t=B)[:, :, 0:1], 0.0).then_inc(s["decay_set"], 1)
            dve.wait_ge(s["decay_set"], 1)
            for v in range(D):
                for c in range(NC):
                    dve.wait_ge(s["vv_ps"], NC * v + c + 1)
                    if v >= 2:
                        dve.wait_ge(s["scan"], v - 1)
                    V.tensor_tensor(by_query(slot(9 + v % 2))[:, 8 * c:8 * c + 8, :],
                                    ps[:, c, :].rearrange("p (t b) -> p t b", b=NQ),
                                    chunk(slot(5), c).rearrange("p (t b) -> p t b", b=NQ), ALU.mult)\
                        .then_inc(s["kv"], 1)
                dve.wait_ge(s["kv"], NC * (v + 1))
                if v >= 2:
                    dve.wait_ge(s["qs"], NC * (v - 1))
                V.tensor_tensor_scan(slot(11 + v % 2), slot(7), slot(9 + v % 2), 0.0, ALU.mult, ALU.add)\
                    .then_inc(s["scan"], 1)
            norm_dve(dve, "normo")
            for c in range(NC):
                dve.wait_ge(*norm_ready("normo", c))
                V.tensor_tensor(chunk(slot(9), c), chunk(slot(6), c), chunk(slot(8), c), ALU.mult)\
                    .then_inc(s["gated"], 1)
            for c in range(NC):
                dve.wait_ge(s["wo_ps"], c + 1)
                V.tensor_tensor(chunk(slot(10), c), chunk(slot(0), c), ps[:, 4 + c, :], ALU.add).then_inc(s["x2"], 1)
            rms_dve(dve, "rms2")
            for c in range(NC):
                for m in range(4):
                    k = 4 * c + m
                    dve.wait_ge(s["gate"], k + 1)
                    dve.wait_ge(s["up_ps"], k + 1)
                    if c >= 2:
                        dve.wait_ge(s["down_ps"], c - 1)
                    V.tensor_tensor(hidden(c)[:, m * CH:(m + 1) * CH], gates(k), ps[:, 2 + k % 2, :], ALU.mult)\
                        .then_inc(s["hid"], 1)
                dve.wait_ge(s["down_ps"], c + 1)
                dve.wait_ge(s["x12"], c + 1)
                V.tensor_tensor(chunk(X, c), chunk(X, c), ps[:, 4 + c, :], ALU.add).then_inc(s["x3"], 1)
            norm_dve(dve, "norm3")
            V.tensor_reduce(slot_sum, w("slots"), AX.X, ALU.add).then_inc(s["slot_sum0"], 1)
            V.scalar_tensor_tensor(tau_inv, bias("tau"), -1.0, bias("tau"), ALU.mult, ALU.max).then_inc(s["tau"], 1)
            dve.wait_ge(s["tau"], 1)
            V.tensor_scalar(tau_inv, tau_inv, 0.1, None, ALU.add).then_inc(s["tau"], 1)
            dve.wait_ge(s["tau"], 2)
            V.reciprocal(tau_inv, tau_inv).then_inc(s["tau"], 1)
            dve.wait_ge(s["slot_sum0"], 1)
            V.tensor_scalar(slot_sum, slot_sum, 1.0 / SLOTS, None, ALU.mult).then_inc(s["slot_sum"], 1)
            dve.wait_ge(s["hb_ps"], 1)
            V.tensor_tensor(hid_bias, ps[0:64, 4, 0:1], bias("b1", 64), ALU.add).then_inc(s["hb"], 1)
            dve.wait_ge(s["logit_ps"], NT)
            V.tensor_tensor(logits, ps[:, 0:2, :].rearrange("p a (i s) -> p (a i) s", s=64),
                            w("b2").unsqueeze(1).broadcast_to([P, NT, SLOTS]), ALU.add).then_inc(s["route"], 1)
            dve.wait_ge(s["route"], 1)
            dve.wait_ge(s["tau"], 3)
            V.tensor_scalar(logits, logits, tau_inv, None, ALU.mult).then_inc(s["route"], 1)
            dve.wait_ge(s["route"], 2)
            for i in range(NT):
                V.max(top[:, i, :], logits[:, i, :]).then_inc(s["top"], 1)
            for i in range(NT):
                dve.wait_ge(s["top"], i + 1)
                V.match_replace(replaced[:, i, :], top[:, i, :], logits[:, i, :], -3.0e38).then_inc(s["picked"], 1)
            dve.wait_ge(s["top"], NT)
            V.tensor_tensor(expo, logits, top[:, :, 0:1].broadcast_to([P, NT, SLOTS]), ALU.subtract)\
                .then_inc(s["shifted"], 1)
            dve.wait_ge(s["picked"], NT)
            V.tensor_tensor(mask, logits, replaced, ALU.not_equal).then_inc(s["mask"], 1)
            dve.wait_ge(s["mask"], 1)
            dve.wait_ge(s["expo"], 1)
            V.tensor_tensor(expo, expo, mask, ALU.mult).then_inc(s["mask"], 1)
            dve.wait_ge(s["mask"], 2)
            V.tensor_reduce(row16, expo, AX.X, ALU.add).then_inc(s["mask"], 1)
            dve.wait_ge(s["mask"], 3)
            V.reciprocal(row16b, row16).then_inc(s["mask"], 1)
            dve.wait_ge(s["mask"], 4)
            V.tensor_tensor(alpha, expo, row16b.unsqueeze(2).broadcast_to([P, NT, SLOTS]), ALU.mult)\
                .then_inc(s["alpha"], 1)
            spread = lambda buf: buf.rearrange("p (i u s) -> p u i s", u=2, s=64)
            for u in range(2):
                for g in range(2):
                    dve.wait_ge(s["sd_ps"], u + 1)
                    V.tensor_scalar(spread(slot(10))[:, u, 8 * g:8 * g + 8, :],
                                    ps[:, 2 * u + g, :].rearrange("p (i s) -> p i s", s=64), 1e-8, None, ALU.add)\
                        .then_inc(s["sd"], 1)
            dve.wait_ge(s["sd"], 4)
            V.reciprocal(slot(10), slot(10)).then_inc(s["sd_inv"], 1)
            dve.wait_ge(s["sd_inv"], 1)
            for u in range(2):
                for g in range(2):
                    dve.wait_ge(s["si_ps"], u + 1)
                    V.tensor_tensor(spread(slot(9))[:, u, 8 * g:8 * g + 8, :],
                                    ps[:, 4 + 2 * u + g, :].rearrange("p (i s) -> p i s", s=64),
                                    spread(slot(10))[:, u, 8 * g:8 * g + 8, :], ALU.mult).then_inc(s["si"], 1)
            dve.wait_ge(s["gh_ps"], 1)
            for k, names in enumerate((("bhh_r", "bih_r"), ("bhh_z", "bih_z"), ("bhh_n", "zero"))):
                V.tensor_scalar(gh[:, k, :], ps[:, 0, k * 64:(k + 1) * 64], bias(names[0]), bias(names[1]),
                                ALU.add, ALU.add).then_inc(s["gh"], 1)
            dve.wait_ge(s["gh"], 3)
            rows = lambda c, bank: ps[:, bank + c, :].rearrange("p (b s) -> p b s", b=PB)
            part = lambda k, c: chunk(slot(k), c).rearrange("p (b s) -> p b s", b=PB)
            for c in range(NC):
                dve.wait_ge(s["gr_ps"], c + 1)
                V.tensor_tensor(part(1, c), rows(c, 4), over_batches(gh[:, 0, :]), ALU.add).then_inc(s["r_in"], 1)
            for c in range(NC):
                dve.wait_ge(s["gz_ps"], c + 1)
                V.tensor_tensor(part(2, c), rows(c, 0), over_batches(gh[:, 1, :]), ALU.add).then_inc(s["z_in"], 1)
            for c in range(NC):
                dve.wait_ge(s["r"], c + 1)
                V.tensor_tensor(part(3, c), part(1, c), over_batches(gh[:, 2, :]), ALU.mult).then_inc(s["rn"], 1)
                dve.wait_ge(s["rn"], c + 1)
                dve.wait_ge(s["gn_ps"], c + 1)
                V.tensor_tensor(part(3, c), part(3, c), rows(c, 4), ALU.add).then_inc(s["n_in"], 1)
            for c in range(NC):
                dve.wait_ge(s["n"], c + 1)
                V.tensor_tensor(part(4, c), over_batches(w("slots")), part(3, c), ALU.subtract).then_inc(s["mix"], 1)
                dve.wait_ge(s["mix"], 2 * c + 1)
                dve.wait_ge(s["z"], c + 1)
                V.tensor_tensor(part(4, c), part(4, c), part(2, c), ALU.mult).then_inc(s["mix"], 1)
                dve.wait_ge(s["mix"], 2 * c + 2)
                V.tensor_tensor(part(5, c), part(4, c), part(3, c), ALU.add).then_inc(s["snew"], 1)
            dve.wait_ge(s["sc_ps"], 1)
            scores = ps[:, 0:2, :].rearrange("p a (i s) -> p (a i) s", s=64)
            V.tensor_reduce(row16, scores, AX.X, ALU.max).then_inc(s["att_step"], 1)
            dve.wait_ge(s["att_step"], 1)
            V.tensor_tensor(att_in, scores, row16.unsqueeze(2).broadcast_to([P, NT, SLOTS]), ALU.subtract)\
                .then_inc(s["att_in"], 1)
            dve.wait_ge(s["att_exp"], 1)
            V.tensor_reduce(row16, att_in, AX.X, ALU.add).then_inc(s["att_step"], 1)
            dve.wait_ge(s["att_step"], 2)
            V.reciprocal(row16b, row16).then_inc(s["att_step"], 1)
            dve.wait_ge(s["att_step"], 3)
            V.tensor_tensor(att, att_in, row16b.unsqueeze(2).broadcast_to([P, NT, SLOTS]), ALU.mult)\
                .then_inc(s["attn"], 1)
            for c in range(NC):
                dve.wait_ge(s["attt_ps"], c + 1)
                V.tensor_copy(chunk(slot(12), c)[0:64, :], ps[0:64, c, :]).then_inc(s["attt"], 1)
            for c in range(NC):
                dve.wait_ge(s["comm_ps"], c + 1)
                V.scalar_tensor_tensor(chunk(slot(9), c), ps[:, 4 + c, :], bias("s_bv"), chunk(slot(5), c),
                                       ALU.add, ALU.add).then_inc(s["y"], 1)
            norm_dve(dve, "norms")
            for c in range(NC):
                dve.wait_ge(*norm_ready("norms", c))
                V.tensor_scalar(chunk(slot(10), c), chunk(slot(9), c), bias("ln_g"), bias("ln_b"),
                                ALU.mult, ALU.add).then_inc(s["y2"], 1)
            for c in range(NC):
                dve.wait_ge(s["fin_ps"], c + 1)
                V.scalar_tensor_tensor(chunk(AT, c), ps[:, 4 + c, :], bias("s_bo"), chunk(X, c), ALU.add, ALU.add)\
                    .then_inc(s["final"], 1)


def kernel(**inputs):
    import concourse.bacc as _bacc
    from concourse.bass_utils import run_bass_kernel_spmd as _run

    i = {k: np.asarray(v) for k, v in inputs.items()}
    a, f = (lambda k: i["L0_attn_" + k]), (lambda k: i["L0_ffn_" + k])
    one = np.ones((1, 1), np.float32)
    zero = np.zeros((1,), np.float32)
    head = np.arange(P) // D
    same = (head[:, None] == head[None, :]).astype(np.float32)
    mask = (head[:, None] == np.arange(H)[None, :]).astype(np.float32)
    sel_num, sel_den = np.zeros((P, 4, P), np.float32), np.zeros((P, 4, P), np.float32)
    for c in range(4):
        for r in range(2):
            for e in range(2):
                out = (2 * (c + 4 * r) + e) * D + np.arange(D)
                sel_num[32 * c + e * D + np.arange(D), 2 * r + e, out] = 1
                sel_den[32 * c + 16, 2 * r + e, out] = 1
    head_sum = np.zeros((P, D, P), np.float32)
    for v in range(D):
        head_sum[np.arange(P), v, head * D + v] = 1
    wv = a("wv").T
    wv_rep = np.stack([wv[:, head * D + v] for v in range(D)], 1).reshape(C, D * C)
    bih, bhh = f("bih").reshape(3, C), f("bhh").reshape(3, C)
    cols = dict(x_bq=i["L0_xattn_bq"], x_bk=i["L0_xattn_bk"], x_bv=i["L0_xattn_bv"], x_bo=i["L0_xattn_bo"],
                scale1=a("scale1"), scale2=a("scale2"), bg1=a("bg1"), bg2=a("bg2"), bog=a("bog"), b1=f("b1"),
                bih_r=bih[0], bih_z=bih[1], bih_n=bih[2], bhh_r=bhh[0], bhh_z=bhh[1], bhh_n=bhh[2],
                s_bq=f("bq"), s_bk=f("bk"), s_bv=f("bv"), ln_g=f("ln_g"), ln_b=f("ln_b"), s_bvp=f("bvp"),
                s_bo=f("bo"), tau=np.broadcast_to(f("tau"), (P,)), zero=np.broadcast_to(zero, (P,)))

    def columns(names):
        m = np.zeros((P, len(names)), np.float32)
        for n, name in enumerate(names):
            m[:len(cols[name]), n] = cols[name]
        return m

    mats = dict(
        x_wq=i["L0_xattn_Wq"], x_wk=i["L0_xattn_Wk"], x_wv=i["L0_xattn_Wv"], x_wo=i["L0_xattn_Wo"],
        mean=np.full((P, P), 1.0 / C, np.float32), head_mask=mask, row_mask=mask[:32, :4][np.arange(P) % 32], bias_a=columns(BIAS_A),
        sel_num=sel_num.reshape(P, -1), sel_den=sel_den.reshape(P, -1), ident=np.eye(P, dtype=np.float32),
        ones=np.ones((P, P), np.float32), g_wq=a("wq").T, g_wk=a("wk").T, g_wv=wv_rep, g_wg1=a("wg1").T,
        g_wg2=a("wg2").T, g_wog=a("wog").T, g_wo=a("wo").T, w_gate=a("w_gate").T, w_up=a("w_up").T,
        w_down=a("w_down").T.reshape(4, P, C).transpose(1, 0, 2).reshape(P, 4 * C),
        head_sum=head_sum.reshape(P, -1), head_mean=np.where(same > 0, np.float32(1.0 / D), np.float32(0)),
        bias_b=columns(BIAS_B), w1x=f("w1")[:C], w1s=f("w1")[C:], w2=f("w2"),
        b2=np.broadcast_to(f("b2"), (P, SLOTS)), wih=f("Wih").T, whh=f("Whh").T, s_wq=f("wq"), s_wk=f("wk"),
        s_wv=f("wv"), s_wvp=f("wvp"), s_wo=f("wo"), slots=f("slot_init").T)
    packed = [np.zeros((P, n), np.float32) for n in WIDTHS]
    for name, (g, col, rows, width) in WHERE.items():
        packed[g][0:rows, col:col + width] = mats[name]
    arrays = {
        "x_t": np.ascontiguousarray(i["x"].reshape(TOK, C).T),
        "ctx_t": np.ascontiguousarray(i["ctx_768"].transpose(0, 2, 1)),
        "w_a": packed[0], "w_b": packed[1],
    }
    nc = _bacc.Bacc("TRN2", target_bir_lowering=False, num_devices=1)
    args = [nc.dram_tensor(k, v.shape, F32, kind="ExternalInput").ap() for k, v in arrays.items()]
    out = nc.dram_tensor("out_t", (C, TOK), F32, kind="ExternalOutput").ap()
    perceiver(nc, *args, out)
    r = _run(nc, [arrays], core_ids=[0])
    return np.ascontiguousarray(r.results[0]["out_t"].T).reshape(B, NQ, C)
```

```python
from contextlib import ExitStack

import numpy as np

import concourse.bass as bass
from concourse import mybir

F32 = mybir.dt.float32
F16 = mybir.dt.float16
I32 = mybir.dt.int32
ALU = mybir.AluOpType
ACT = mybir.ActivationFunctionType
AX = mybir.AxisListType

P = 128
B, NQ, C = 32, 64, 128
NKV, CKV = 1601, 96
H, D = 16, 8
TOK = B * NQ
CH = 512
NC = TOK // CH
NB = -(-NKV // P)
PAIRS = H // 2
SCALE = D ** -0.5
CLAMP = 10000.0
HID = 4 * C
SLOTS = 64
TOPK = 8
DQ = C // 4
NT = TOK // P
PB = CH // NQ
KCH = [(c * CH, min(CH, NKV - c * CH)) for c in range(-(-NKV // CH))]
KBL = [(i * P, min(P, NKV - i * P)) for i in range(NB)]
NSTACK = 16
UNITS = len(KCH) + 4
TURNS = {0: [(0, None), (1, None)], 1: [(2, None)], 2: [(3, None)], 4: [(4, 0)], 5: [(4, 1)], 6: [(5, 0)],
         7: [(5, 1)], 8: [(6, 0)], 9: [(6, 1)], 10: [(7, None)]}
GATHERS = (3, 11)
SUM_LOW, SUM_HIGH = 1e-10, 1e30


def pack():
    first = [("x_wq", C, C), ("x_wk", CKV, C), ("x_wv", CKV, C), ("centre", P, P), ("mean", P, 32), ("back", P, 4 * P),
             ("head_mask", P, H), ("row_mask", P, 4),
             ("bias_a", P, 4),]
    second = [("sel_num", P, 4 * P), ("sel_den", P, 4 * P), ("ident", P, P), ("ones", P, P), ("x_wo", C, C),
              ("g_wq", C, C), ("g_wk", C, C), ("g_wv", C, D * C), ("g_wg1", C, P), ("g_wg2", P, C),
              ("g_wog", C, C), ("g_wo", C, C), ("w_gate", C, HID), ("w_up", C, HID), ("w_down", C, 4 * C),
              ("head_sum", P, D * P), ("head_centre", P, P), ("head_mean", P, 32), ("head_back", P, 4 * P),
              ("bias_b", P, 21), ("w1x", C, P),
              ("w1s", C, P), ("w2", P, SLOTS), ("b2", P, SLOTS), ("wih", C, 3 * C), ("whh", C, 3 * C),
              ("s_wq", C, P), ("s_wk", C, P), ("s_wv", C, C), ("s_wvp", C, C), ("s_wo", C, C),
              ("slots", C, SLOTS)]
    where, widths = {}, []
    for a, group in enumerate((first, second)):
        col = 0
        for name, rows, cols in group:
            where[name] = (a, col, rows, cols)
            col += cols
        widths.append(col)
    return where, widths


WHERE, WIDTHS = pack()
BIAS_A = ["x_bq", "x_bk", "x_bv", "x_bo"]
BIAS_B = ["scale1", "scale2", "bg1", "bg2", "bog", "b1", "bih_r", "bih_z", "bih_n", "bhh_r", "bhh_z",
          "bhh_n", "s_bq", "s_bk", "s_bv", "ln_g", "ln_b", "s_bvp", "s_bo", "tau", "zero"]


def perceiver(nc, x_t, ctx_t, w_a, w_b, out_t, force_general=False):
    with ExitStack() as stack:
        def sb(name, shape, dt=F32):
            return stack.enter_context(nc.sbuf_tensor(name, shape, dt))

        def sem(name):
            return stack.enter_context(nc.semaphore(name))

        WA = sb("WA", [P, WIDTHS[0]])
        WB = sb("WB", [P, WIDTHS[1]])
        X = sb("X", [P, TOK])
        AT = sb("AT", [P, TOK])
        QT = sb("QT", [P, TOK])
        arena = sb("arena", [P, 14 * TOK])
        small = sb("small", [P, 1024])
        stat = [sb("stat0", [P, CH]), sb("stat1", [P, CH])]
        flag = sb("flag", [1, 2], I32)
        PS = stack.enter_context(nc.psum_tensor("PS", [P, 8, CH], F32))

        def w(name):
            a, col, rows, cols = WHERE[name]
            return (WA, WB)[a][0:rows, col:col + cols]

        def bias(name, rows=P):
            group, array, names = (("bias_a", WA, BIAS_A) if name in BIAS_A else ("bias_b", WB, BIAS_B))
            col = WHERE[group][1] + names.index(name)
            return array[0:rows, col:col + 1]

        def slot(k, n=1):
            return arena[:, k * TOK:(k + n) * TOK]

        def chunk(buf, c):
            return buf[:, c * CH:(c + 1) * CH]

        used = [0]

        def carve(cols):
            used[0] += cols
            assert used[0] <= 14 * TOK
            return arena[:, used[0] - cols:used[0]]

        def halves(cols):
            return carve(cols // 2).bitcast(F16)

        ctx_sb = [carve(NKV)[0:CKV, :] for _ in range(2)]
        k_parts = halves(2 * NKV).rearrange("p (a k) -> p a k", a=2)
        k_stack0 = used[0]
        k_stack = [halves(4 * NKV).rearrange("p (g k) -> p g k", g=4) for _ in range(2)]
        k_stack1 = used[0]
        v_sb = [carve(NB * PAIRS * 32).rearrange("p (n h m) -> p n h m", n=NB, h=PAIRS) for _ in range(2)]
        q_stack = halves(4 * TOK).rearrange("p (g t) -> p g t", g=4)
        q_bd = [halves(H * NQ).rearrange("p (g h q) -> p g h q", g=4, h=4) for _ in range(2)]
        p_start = used[0]
        p_sb = [carve(H * NQ) for _ in range(2)]
        o_sb = carve(4 * P)
        fast_end = used[0]
        q_parts = halves(2 * TOK).rearrange("p (a t) -> p a t", a=2)
        used[0] = p_start
        first_squares = carve(TOK)
        used[0] = k_stack0
        gk_sb = carve(NKV)
        gq_bd = carve(H * NQ)
        s_sb = carve(NKV)
        pt_sb = carve(NB * P).rearrange("p (n q) -> p n q", n=NB)
        assert used[0] <= k_stack1
        okay = small[:, 780:908]
        okay_a = small[:, 0:128]
        okay_b = small[:, 128:256]
        recip = small[:, 320:448]
        okay_min = small[:, 256:257]
        g_recip = recip[:, 0:NQ]
        row_neg = small[:, 258:259]
        ctx_mean = small[0:CKV, 260:292]
        v_mean = small[:, 908:940]
        real = small[:, 0:64]
        real_all = small[:, 940:1004]
        real_min = small[:, 452:453]

        class Signals(dict):

            def __missing__(self, name):
                self[name] = sem(name)
                return self[name]

        s = Signals()
        ctx_in = [sem("ctx_in0"), sem("ctx_in1")]
        PE, V, A, G = nc.tensor, nc.vector, nc.scalar, nc.gpsimd
        eps = sb("eps", [P, 1])
        ps = PS

        NORMS = {
            "norm1": (X, AT, AT, first_squares, ""),
            "norm2": (X, slot(0), slot(1), slot(2), ""),
            "normo": (slot(6), slot(6), slot(7), slot(11), "head_"),
            "norm3": (X, slot(0), slot(1), slot(2), ""),
            "norms": (slot(9), slot(9), slot(10), slot(11), ""),
        }
        ORDER = list(NORMS)

        def base(tag):
            return NC * ORDER.index(tag)

        def norm_ready(tag, c):
            return s["norm_ready"], base(tag) + c + 1

        def spread_back(stats, kind, bank, c):
            return PE.matmul(ps[:, bank, :], w(kind + "back")[:, c * P:(c + 1) * P], stats[:, :], start=True, stop=True)

        def norm_pe(pe, tag, src_ready):
            src, dst, centred, square, kind = NORMS[tag]
            for c in range(NC):
                src_ready(c)
                PE.matmul(ps[:, c, :], w(kind + "centre"), chunk(src, c), start=True, stop=True)\
                    .then_inc(s["norm_mean"], 1)
            for c in range(NC):
                pe.wait_ge(s["norm_squared"], base(tag) + c + 1)
                mm = PE.matmul(ps[32 * c:32 * c + 32, 4, :], w(kind + "mean"), chunk(square, c), start=True, stop=True)
            mm.then_inc(s["norm_var"], 1)
            pe.wait_ge(s["norm_inverse"], ORDER.index(tag) + 1)
            for c in range(NC):
                spread_back(stat[0], kind, c, c).then_inc(s["norm_back"], 1)

        def norm_act(act, tag):
            src, dst, centred, square, kind = NORMS[tag]
            for c in range(NC):
                act.wait_ge(s["norm_centred"], base(tag) + c + 1)
                A.activation(chunk(square, c), chunk(centred, c), ACT.Square).then_inc(s["norm_squared"], 1)
            act.wait_ge(s["norm_var"], ORDER.index(tag) + 1)
            A.activation(stat[0][:, :], ps[:, 4, :], ACT.Sqrt, bias=eps[:, 0:1]).then_inc(s["norm_root"], 1)

        def norm_dve(dve, tag, between=None):
            src, dst, centred, square, kind = NORMS[tag]
            for c in range(NC):
                dve.wait_ge(s["norm_mean"], base(tag) + c + 1)
                V.tensor_copy(chunk(centred, c), ps[:, c, :]).then_inc(s["norm_centred"], 1)
            dve.wait_ge(s["norm_root"], ORDER.index(tag) + 1)
            V.reciprocal(stat[0][:, :], stat[0][:, :]).then_inc(s["norm_inverse"], 1)
            if between is not None:
                between()
            for c in range(NC):
                dve.wait_ge(s["norm_back"], base(tag) + c + 1)
                V.tensor_tensor(chunk(dst, c), chunk(centred, c), ps[:, c, :], ALU.mult).then_inc(s["norm_ready"], 1)

        def rms1_pe(pe):
            pe.wait_ge(s["rms_inverse"], 1)
            for c in range(NC):
                spread_back(stat[1], "", 4 + c, c).then_inc(s["rms_back"], 1)

        def rms1_act(act):
            A.activation(stat[1][:, :], ps[:, 4, :], ACT.Sqrt).then_inc(s["rms_root"], 1)

        def rms1_stats(dve):
            dve.wait_ge(s["rms_root"], 1)
            dve.wait_ge(s["norm_inverse"], 2)
            V.tensor_tensor(stat[1][:, :], stat[1][:, :], stat[0][:, :], ALU.mult).then_inc(s["rms_step"], 1)
            dve.wait_ge(s["rms_step"], 1)
            V.tensor_scalar(stat[1][:, :], stat[1][:, :], 1e-6, None, ALU.add).then_inc(s["rms_step"], 1)
            dve.wait_ge(s["rms_step"], 2)
            V.reciprocal(stat[1][:, :], stat[1][:, :]).then_inc(s["rms_step"], 1)
            dve.wait_ge(s["rms_step"], 3)
            V.tensor_tensor(stat[1][:, :], stat[1][:, :], stat[0][:, :], ALU.mult).then_inc(s["rms_inverse"], 1)

        def rms1_dve(dve):
            for c in range(NC):
                dve.wait_ge(s["rms_back"], c + 1)
                V.scalar_tensor_tensor(chunk(slot(3), c), chunk(slot(1), c), bias("scale1"), ps[:, 4 + c, :],
                                       ALU.mult, ALU.mult).then_inc(s["rms_ready"], 1)

        def rms2_pe(pe):
            for c in range(NC):
                pe.wait_ge(s["rms_squared"], c + 1)
                mm = PE.matmul(ps[32 * c:32 * c + 32, 0, :], w("mean"), chunk(slot(1), c), start=True, stop=True)
            mm.then_inc(s["rms_mean"], 1)
            pe.wait_ge(s["rms_inverse"], 2)
            for c in range(NC):
                spread_back(stat[1], "", 4 + c, c).then_inc(s["rms_back"], 1)

        def rms2_act(act):
            for c in range(NC):
                act.wait_ge(s["x2"], c + 1)
                A.activation(chunk(slot(1), c), chunk(slot(10), c), ACT.Square).then_inc(s["rms_squared"], 1)
            act.wait_ge(s["rms_mean"], 1)
            A.activation(stat[1][:, :], ps[:, 0, :], ACT.Sqrt).then_inc(s["rms_root"], 1)

        def rms2_dve(dve):
            dve.wait_ge(s["rms_root"], 2)
            V.tensor_scalar(stat[1][:, :], stat[1][:, :], 1e-6, None, ALU.add).then_inc(s["rms_step"], 1)
            dve.wait_ge(s["rms_step"], 4)
            V.reciprocal(stat[1][:, :], stat[1][:, :]).then_inc(s["rms_inverse"], 1)
            for c in range(NC):
                dve.wait_ge(s["rms_back"], NC + c + 1)
                V.scalar_tensor_tensor(chunk(slot(3), c), chunk(slot(10), c), bias("scale2"), ps[:, 4 + c, :],
                                       ALU.mult, ALU.mult).then_inc(s["rms_ready"], 1)

        def turn(b, i):
            return UNITS * b + 8 + i

        def pe_keys(u, c, bank):
            k0, n = KCH[c]
            return PE.matmul(ps[:, bank, 0:n], w("x_wk"), ctx_sb[u][:, k0:k0 + n], start=True, stop=True)

        def pe_values(u, g, bank, half=None):
            blocks = list(range(4 * g, min(4 * g + 4, NB)))
            for i in blocks if half is None else blocks[2 * half:2 * half + 2]:
                k0, n = KBL[i]
                o = (i - 4 * g) * P
                mm = PE.matmul(ps[0:n, bank, o:o + P], ctx_sb[u][:, k0:k0 + n], w("x_wv"), start=True, stop=True)
            return mm

        def dve_keys(dve, c, bank, stacked, high):
            k0, n = KCH[c]
            hi, lo = k_parts[:, 0, k0:k0 + n], k_parts[:, 1, k0:k0 + n]
            if stacked is not None and c == 0:
                dve.wait_ge(s["k_stacked"], stacked)
            V.tensor_scalar(hi, ps[:, bank, 0:n], bias("x_bk"), None, ALU.add).then_inc(s["k_high"], 1)
            dve.wait_ge(s["k_high"], high)
            V.scalar_tensor_tensor(lo, ps[:, bank, 0:n], bias("x_bk"), hi, ALU.add, ALU.subtract)\
                .then_inc(s["turn_out"], 1)

        def g_keys(c):
            k0, n = KCH[c]
            return V.tensor_scalar(gk_sb[:, k0:k0 + n], ps[:, c, 0:n], bias("x_bk"), None, ALU.add)

        def stack_keys(queue, u):
            for g in range(4):
                for c in range(4):
                    queue.dma_start(k_stack[u][32 * c:32 * c + 32, g, :], k_parts[32 * g:32 * g + 32, c % 2, :])\
                        .then_inc(s["k_stacked"], 16)

        def stack_queries(queue, g):
            for c in range(4):
                queue.dma_start(q_stack[32 * c:32 * c + 32, g, :], q_parts[32 * g:32 * g + 32, c // 2, :])\
                    .then_inc(s["q_stacked"], 16)

        def dve_values(u, g, bank):
            n, rows = (4, P) if g < 3 else (1, KBL[-1][1])
            return V.tensor_copy(v_sb[u][0:rows, 4 * g:4 * g + n, :, 0:16],
                                 ps[0:rows, bank, 0:n * P].rearrange("p (n h m) -> p n h m", n=n, h=PAIRS))

        def pe_finish(o, width, bank, col, kinds=(0, 1)):
            for k in kinds:
                for i in range(4):
                    at = col + k * width
                    mm = PE.matmul(ps[:, bank, at:at + width], w(("sel_num", "sel_den")[k])[:, i * P:(i + 1) * P],
                                   o[:, i * width:(i + 1) * width], start=(i == 0), stop=(i == 3))
            return mm

        def q_blocks(b, u):
            return G.tensor_tensor(q_bd[u], q_stack[:, :, bass.ds(b * NQ, NQ)].unsqueeze(2).broadcast_to([P, 4, 4, NQ]),
                                   w("row_mask").unsqueeze(1).unsqueeze(3).broadcast_to([P, 4, 4, NQ]), ALU.mult)

        def g_q_blocks(b):
            return G.tensor_tensor(gq_bd.rearrange("p (h q) -> p h q", h=H),
                                   QT[:, bass.ds(b * NQ, NQ)].unsqueeze(1).broadcast_to([P, H, NQ]),
                                   w("head_mask").unsqueeze(2).broadcast_to([P, H, NQ]), ALU.mult)

        def pe_pv(pe, j, u, i):
            b = 2 * j + u
            n, par, rows = NB * b + i, (NB * u + i) % 2, KBL[i][1]
            pe.wait_ge(s["exp_done"], n + 3)
            if i == 0:
                pe.wait_ge(s["turn_out"], turn(b, 0) + 2)
                pe.wait_ge(s["acc_out"], b + 1)
                if u == 1:
                    pe.wait_ge(s["fin_out"], j + 1)
            for h in range(PAIRS):
                c, r = h % 4, h // 4
                mm = PE.matmul(ps[32 * c:32 * c + 32, 4 + u, r * P:(r + 1) * P], v_sb[u][0:rows, i, h, :],
                               p_sb[par][0:rows, h * P:(h + 1) * P], start=(i == 0 and r == 0),
                               stop=(i == NB - 1), skip_group_check=True)
                if i == NB - 1 and h == 0:
                    mm.then_inc(s["q_free"], 1)
            mm.then_inc(s["pv_done"], 1)

        def pe_next(pe, j, u, t, half):
            b = 2 * j + u
            if t == 0:
                pe.wait_ge(ctx_in[1 - u], 16 * (j + 1 + u))
            if half != 1:
                pe.wait_ge(s["turn_out"], turn(b, t) + 1)
            if t < 4:
                mm = pe_keys(1 - u, t, 6 + t % 2)
            else:
                mm = pe_values(1 - u, t - 4, 6 + t % 2, half)
            if half != 0:
                mm.then_inc(s["turn_ps"], 1)

        def pe_scores(pe, b, u, i):
            n, par = NB * b + i, (NB * u + i) % 2
            if i == 0:
                pe.wait_ge(s["q_ready"], b + 1)
                pe.wait_ge(s["k_stacked"], 16 * NSTACK * (b + 1))
            pe.wait_ge(s["exp_done"], n + 1)
            k0, rows = KBL[i]
            for g in range(4):
                mm = PE.matmul(ps[0:rows, 2 * par + g // 2, (g % 2) * 256:(g % 2 + 1) * 256],
                               k_stack[u][:, g, k0:k0 + rows],
                               q_bd[u][:, g, :, :].rearrange("p h q -> p (h q)"), start=True, stop=True)
            mm.then_inc(s["score_ps"], 1)

        def pe_gather(pe, j, kind):
            if kind == 0:
                pe.wait_ge(s["acc_out"], 2 * j + 4)
            pe_finish(o_sb, P, 5, 2 * P, (kind,)).then_inc(s["gather_ps"], 1)

        def pe_body(pe, j, first=False, last=False):
            for u in range(2):
                b = 2 * j + u
                final = last and u == 1
                for i in range(NB):
                    if i < NB - 1:
                        pe_scores(pe, b, u, i + 1)
                    elif not final:
                        pe_scores(pe, b + 1, 1 - u, 0)
                    for t, half in TURNS.get(i, ()):
                        if not final:
                            pe_next(pe, j, u, t, half)
                    if u == 0 and i in GATHERS and not first:
                        pe_gather(pe, j - 1, GATHERS.index(i))
                    pe_pv(pe, j, u, i)
            if last:
                for kind in range(2):
                    pe_gather(pe, j, kind)

        def act_batch(act, j, u):
            b = 2 * j + u
            for i in range(NB):
                n, par, rows = NB * b + i, (NB * u + i) % 2, KBL[i][1]
                act.wait_ge(s["score_ps"], n + 1)
                act.wait_ge(s["pv_done"], n + 1)
                A.activation(p_sb[par][0:rows, :].rearrange("p (a n) -> p a n", a=2),
                             ps[0:rows, 2 * par:2 * par + 2, :], ACT.Exp).then_inc(s["exp_done"], 1)

        def dve_gather(dve, j):
            dve.wait_ge(s["gather_ps"], 2 * j + 2)
            num, den = ps[:, 5, 2 * P:3 * P], ps[:, 5, 3 * P:4 * P]
            V.reciprocal(recip, den).then_inc(s["sum_step"], 1)
            V.tensor_scalar(okay_a, den, SUM_LOW, None, ALU.is_ge).then_inc(s["sum_step"], 1)
            dve.wait_ge(s["sum_step"], 4 * j + 2)
            V.scalar_tensor_tensor(okay_b, den, SUM_HIGH, okay_a, ALU.is_le, ALU.mult).then_inc(s["sum_step"], 1)
            dve.wait_ge(s["sum_step"], 4 * j + 3)
            V.tensor_tensor(okay, okay, okay_b, ALU.mult).then_inc(s["sum_step"], 1)
            V.tensor_tensor(AT[:, bass.ds(j * P, P)], num, recip, ALU.mult).then_inc(s["fin_out"], 1)
            dve.wait_ge(s["sum_step"], 4 * j + 4)
            dve.wait_ge(s["fin_out"], j + 2)

        def dve_body(dve, j, first=False, last=False):
            for u in range(2):
                b = 2 * j + u
                for i in range(UNITS):
                    if last and u == 1:
                        break
                    dve.wait_ge(s["turn_ps"], turn(b, i) + 1)
                    if i < 4:
                        dve_keys(dve, i, 6 + i % 2, 16 * NSTACK * (b + 1), 4 * (b + 1) + i + 1)
                    else:
                        dve_values(1 - u, i % 4, 6 + i % 2).then_inc(s["turn_out"], 1)
                if u == 0 and not first:
                    dve_gather(dve, j - 1)
                dve.wait_ge(s["pv_done"], NB * b + NB + 2)
                V.tensor_copy(o_sb.rearrange("p (i u q) -> p i u q", i=4, u=2)[:, :, u, :],
                              ps[:, 4 + u, 0:2 * P].rearrange("p (i q) -> p i q", i=4)).then_inc(s["acc_out"], 1)
            if last:
                dve_gather(dve, j)

        def g_load(sp, b):
            sp.wait_ge(s["g_ctx_free"], b + 1)
            sp.dma_start(ctx_sb[0], ctx_t[bass.ds(b, 1), :, :].rearrange("a c k -> (a c) k")).then_inc(s["g_ctx"], 16)

        def g_pe(pe, b):
            pe.wait_ge(s["g_ctx"], 16 * (b + 1))
            pe.wait_ge(s["g_done"], b + 1)
            for c in range(4):
                pe_keys(0, c, c).then_inc(s["g_k_ps"], 1)
            for g in range(4):
                pe_values(0, g, 4 + g).then_inc(s["g_v_ps"], 1)
            pe.wait_ge(s["g_q"], b + 1)
            pe.wait_ge(s["g_kv_sb"], 8 * (b + 1))
            for h in range(PAIRS):
                n = PAIRS * b + h
                if h >= 1:
                    pe.wait_ge(s["g_pt"], 4 * n)
                for c, (k0, m) in enumerate(KCH):
                    PE.matmul(ps[:, c, 0:m], gq_bd[:, h * P:(h + 1) * P], gk_sb[:, k0:k0 + m],
                              start=True, stop=True).then_inc(s["g_s_ps"], 1)
                pe.wait_ge(s["g_exp"], n + 1)
                for i, (k0, rows) in enumerate(KBL):
                    bank, o = (4 + i // 4, (i % 4) * P) if i < 12 else (3, 0)
                    t = PE.transpose(ps[0:rows, bank, o:o + P], s_sb[:, k0:k0 + rows], w("ident"))
                t.then_inc(s["g_t_ps"], 1)
                pe.wait_ge(s["g_pt"], 4 * (n + 1))
                c, r = h % 4, h // 4
                for i, (k0, rows) in enumerate(KBL):
                    mm = PE.matmul(ps[32 * c:32 * c + 32, 7, r * P:(r + 1) * P], v_sb[0][0:rows, i, h, :],
                                   pt_sb[0:rows, i, :], start=(i == 0 and r == 0), stop=(i == NB - 1),
                                   skip_group_check=True)
                mm.then_inc(s["g_pv"], 1)
            pe.wait_ge(s["g_o"], b + 1)
            pe_finish(o_sb, NQ, 6, 0).then_inc(s["g_fin"], 1)

        def g_dve(dve, b):
            for c in range(4):
                dve.wait_ge(s["g_k_ps"], 4 * b + c + 1)
                g_keys(c).then_inc(s["g_kv_sb"], 1)
            for g in range(4):
                dve.wait_ge(s["g_v_ps"], 4 * b + g + 1)
                dve_values(0, g, 4 + g).then_inc(s["g_kv_sb"], 1)
            V.tensor_reduce(ctx_mean[:, bass.ds(b, 1)], ctx_sb[0], AX.X, ALU.add).then_inc(s["g_ctx_free"], 1)
            for h in range(PAIRS):
                n = PAIRS * b + h
                for c, (k0, m) in enumerate(KCH):
                    dve.wait_ge(s["g_s_ps"], 4 * n + c + 1)
                    V.tensor_scalar(s_sb[:, k0:k0 + m], ps[:, c, 0:m], CLAMP, -CLAMP, ALU.min, ALU.max)\
                        .then_inc(s["g_clip"], 1)
                dve.wait_ge(s["g_clip"], 4 * (n + 1))
                V.tensor_reduce(row_neg, s_sb, AX.X, ALU.max, negate=True).then_inc(s["g_max"], 1)
                dve.wait_ge(s["g_t_ps"], n + 1)
                for i in range(3):
                    V.tensor_copy(pt_sb[:, 4 * i:4 * i + 4, :],
                                  ps[:, 4 + i, :].rearrange("p (n q) -> p n q", n=4)).then_inc(s["g_pt"], 1)
                rows = KBL[-1][1]
                V.tensor_copy(pt_sb[0:rows, NB - 1, :], ps[0:rows, 3, 0:P]).then_inc(s["g_pt"], 1)
                dve.wait_ge(s["g_pv"], n + 1)
            V.tensor_copy(o_sb[:, 0:2 * P], ps[:, 7, 0:2 * P]).then_inc(s["g_o"], 1)
            dve.wait_ge(s["g_fin"], b + 1)
            num, den = ps[:, 6, 0:NQ], ps[:, 6, NQ:2 * NQ]
            V.reciprocal(g_recip, den).then_inc(s["g_step"], 1)
            V.tensor_scalar(real, den, 0.0, None, ALU.is_gt).then_inc(s["g_step"], 1)
            dve.wait_ge(s["g_step"], 3 * b + 2)
            V.tensor_tensor(real_all, real_all, real, ALU.mult).then_inc(s["g_step"], 1)
            dve.wait_ge(s["g_step"], 3 * b + 3)
            V.tensor_tensor(AT[:, bass.ds(b * NQ, NQ)], num, g_recip, ALU.mult).then_inc(s["g_done"], 1)
            dve.wait_ge(s["g_done"], b + 2)

        def all_rows(dve, values, worst, i):
            V.tensor_reduce(worst, values, AX.X, ALU.min).then_inc(s["worst"], 1)
            dve.wait_ge(s["count_ps"], i + 1)
            V.tensor_copy(flag[:, i:i + 1], ps[0:1, 5, i:i + 1]).then_inc(s["flag_ready"], 1)

        QS = [slot(1), AT[:, :]]

        def by_query(buf):
            return buf.rearrange("p (b t) -> p t b", t=B)

        def gemm(pe, weight, src, banks, done, ready=None, free=None, c0=0, rows=P):
            for c in range(NC):
                if ready is not None:
                    pe.wait_ge(*(ready(c) if callable(ready) else (s[ready], c + 1)))
                if free is not None:
                    pe.wait_ge(s[free], c + 1)
                PE.matmul(ps[0:rows, banks + c, :], weight, chunk(src, c), start=True, stop=True)\
                    .then_inc(s[done], 1)

        def pe_head_sum(pe, v):
            for c in range(NC):
                pe.wait_ge(s["qs"], NC * v + c + 1)
                if v == 0:
                    pe.wait_ge(s["og"], c + 1)
                PE.matmul(ps[:, 4 + c, :], w("head_sum")[:, v * P:(v + 1) * P], chunk(QS[v % 2], c),
                          start=(v == 0), stop=(v == D - 1)).then_inc(s["osum_ps"], 1)

        hidden = lambda c: slot(4 + c % 2)
        gates = lambda k: slot(7)[:, (k % 4) * CH:(k % 4 + 1) * CH]
        tiles = lambda buf, half, n=64: buf[:, half * 1024:half * 1024 + NT * n].rearrange("p (i s) -> p i s", i=NT)
        logits, replaced = tiles(slot(4), 0), tiles(slot(4), 1)
        expo, mask = tiles(slot(5), 0), tiles(slot(5), 1)
        top = tiles(slot(6), 1, 8)
        alphas = slot(12)
        alpha = alphas.rearrange("p (i s) -> p i s", i=NT)
        xtok = slot(7).rearrange("p (i d) -> p i d", i=NT)
        att = slot(7).rearrange("p (i t) -> p i t", i=NT)
        att_in = tiles(slot(11), 1)
        vs = slot(1).rearrange("p (i d) -> p i d", i=NT)
        svp = slot(3).rearrange("p (i d) -> p i d", i=NT)

        def diagonal(dst, src, done):
            for u in range(2):
                rows = slice(64 * u, 64 * u + 64)
                V.tensor_tensor(dst[rows, :, 64 * u:64 * u + 64], src[rows, :, :],
                                row16b[rows, :].unsqueeze(2).broadcast_to([64, NT, SLOTS]), ALU.mult)\
                    .then_inc(s[done], 1)
        slot_sum = small[:, 460:461]
        tau_inv = small[:, 461:462]
        hid_bias = small[:, 462:463]
        gh = small[:, 512:704].rearrange("p (k s) -> p k s", k=3)
        row16 = small[:, 704:720]
        row16b = small[:, 720:736]

        def over_batches(tile):
            return tile.unsqueeze(1).broadcast_to([P, PB, SLOTS])

        block = stack.enter_context(nc.Block())
        HALF = B // 2

        @block.sync
        def _(sp):
            sp.dma_start(WA[:, :], w_a).then_inc(s["wa_in"], 16)
            for u in range(2):
                sp.dma_start(ctx_sb[u], ctx_t[u, :, :]).then_inc(ctx_in[u], 16)
            sp.wait_ge(s["turn_out"], 4 + 2)
            stack_keys(nc.sync, 0)
            sp.wait_ge(s["q_low"], NC)
            for g in range(2):
                stack_queries(nc.sync, g)
            sp.dma_start(WB[:, :], w_b).then_inc(s["wb_in"], 16)
            with sp.Fori(0, HALF - 1) as j:
                for u in range(2):
                    sp.wait_ge(s["turn_ps"], UNITS * (2 * j + u) + 8)
                    sp.dma_start(ctx_sb[u], ctx_t[bass.ds(2 * j + u + 2, 1), :, :].rearrange("a c k -> (a c) k"))\
                        .then_inc(ctx_in[u], 16)
                    sp.wait_ge(s["turn_out"], UNITS * (2 * j + u) + 8 + 4 + 2)
                    stack_keys(nc.sync, 1 - u)
            sp.wait_ge(s["turn_out"], UNITS * (B - 2) + 8 + 4 + 2)
            stack_keys(nc.sync, 1)
            sp.wait_ge(s["flag_ready"], 1)
            f = sp.value_load(flag[0:1, 0:1])
            with sp.If(f < P):
                with sp.Fori(0, B) as b:
                    g_load(sp, b)
            for c in range(NC):
                sp.wait_ge(s["final"], c + 1)
                sp.dma_start(out_t[:, c * CH:(c + 1) * CH], chunk(AT, c)).then_inc(s["out_done"], 16)
            sp.wait_ge(s["out_done"], 16 * NC)

        @block.gpsimd
        def _(pool):
            for u in range(2):
                G.memset(v_sb[u][:, :, :, 16:32], 1.0).then_inc(s["ones_set"], 1)
            pool.wait_ge(s["q_stacked"], 16 * NSTACK)
            with pool.Fori(0, HALF) as j:
                for u in range(2):
                    pool.wait_ge(s["q_free"], 2 * j + u + 1)
                    q_blocks(2 * j + u, u).then_inc(s["q_ready"], 1)
            pool.wait_ge(s["flag_ready"], 1)
            f = pool.value_load(flag[0:1, 0:1])
            with pool.If(f < P):
                with pool.Fori(0, B) as b:
                    pool.wait_ge(s["g_done"], b + 1)
                    g_q_blocks(b).then_inc(s["g_q"], 1)
            for v in range(D):
                for c in range(NC):
                    pool.wait_ge(s["scan"], v + 1)
                    if v >= 2:
                        pool.wait_ge(s["osum_ps"], NC * (v - 2) + c + 1)
                    G.tensor_tensor(chunk(QS[v % 2], c).rearrange("p (t b) -> p t b", b=NQ),
                                    chunk(slot(4), c).rearrange("p (t b) -> p t b", b=NQ),
                                    by_query(slot(11 + v % 2))[:, 8 * c:8 * c + 8, :], ALU.mult)\
                        .then_inc(s["qs"], 1)
            for c in range(NC):
                pool.wait_ge(s["x2"], c + 1)
                G.tensor_tensor(chunk(X, c), chunk(X, c), chunk(slot(10), c), ALU.add).then_inc(s["x12"], 1)
            pool.wait_ge(s["qs"], NC * D)
            G.memset(alphas, 0.0).then_inc(s["zeroed"], 1)
            pool.wait_ge(s["si_ps"], NC)
            G.memset(slot(7), 0.0).then_inc(s["zeroed"], 1)

        @block.tensor
        def _(pe):
            PE.sem_inc(s["pv_done"], 2)
            PE.sem_inc(s["q_free"], 2)
            pe.wait_ge(s["wa_in"], 16)
            pe.wait_ge(ctx_in[0], 16)
            for i in range(4):
                pe.wait_ge(s["turn_out"], i + 1)
                pe_keys(0, i, 6 + i % 2).then_inc(s["turn_ps"], 1)
            norm_pe(pe, "norm1", lambda c: pe.wait_ge(s["x_in"], 16))
            pe.wait_ge(s["turn_out"], 6)
            gemm(pe, w("x_wq"), AT, 4, "q_ps", ready=lambda c: norm_ready("norm1", c))
            pe.wait_ge(s["q_sb"], NC)
            for i in range(4, 8):
                pe.wait_ge(s["turn_out"], i + 1)
                pe_values(0, i % 4, 6 + i % 2).then_inc(s["turn_ps"], 1)
            pe.wait_ge(s["ones_set"], 2)
            pe_scores(pe, 0, 0, 0)
            pe_body(pe, 0, first=True)
            pe.wait_ge(s["wb_in"], 16)
            with pe.Fori(1, HALF - 1) as j:
                pe_body(pe, j)
            pe_body(pe, HALF - 1, last=True)
            pe.wait_ge(s["wb_in"], 16)
            pe.wait_ge(s["worst"], 1)
            PE.matmul(ps[0:1, 5, 0:1], okay_min, w("ones")[:, 0:1], start=True, stop=True).then_inc(s["count_ps"], 1)
            pe.wait_ge(s["flag_ready"], 1)
            f = pe.value_load(flag[0:1, 0:1])
            with pe.If(f < P):
                with pe.Fori(0, B) as b:
                    g_pe(pe, b)
                pe.wait_ge(s["worst"], 2)
                PE.matmul(ps[0:1, 5, 1:2], real_min, w("ones")[:, 0:1], start=True, stop=True)\
                    .then_inc(s["count_ps"], 1)
                PE.matmul(ps[:, 4, 0:B], w("x_wv"), ctx_mean, start=True, stop=True).then_inc(s["v_mean_ps"], 1)
            gemm(pe, w("x_wo"), AT, 4, "xo_ps", ready="ao")
            norm_pe(pe, "norm2", lambda c: pe.wait_ge(s["x1"], c + 1))
            pe.wait_ge(s["wb_in"], 16)
            rms1_pe(pe)
            gemm(pe, w("g_wq"), slot(3), 0, "gq_ps", ready=lambda c: (s["rms_ready"], c + 1))
            gemm(pe, w("g_wk"), slot(3), 4, "gk_ps")
            gemm(pe, w("g_wg1"), slot(3), 0, "g1_ps", free="gq")
            gemm(pe, w("g_wog"), slot(3), 4, "og_ps", free="gk")
            gemm(pe, w("g_wg2"), slot(2), 0, "g2_ps", ready="g1", free="g1")
            for v in range(D):
                for c in range(NC):
                    if v == 0:
                        pe.wait_ge(s["decay"], c + 1)
                    else:
                        pe.wait_ge(s["kv"], NC * (v - 1) + c + 1)
                    PE.matmul(ps[:, c, :], w("g_wv")[:, v * P:(v + 1) * P], chunk(slot(3), c),
                              start=True, stop=True).then_inc(s["vv_ps"], 1)
                if v >= 1:
                    pe_head_sum(pe, v - 1)
            pe_head_sum(pe, D - 1)
            norm_pe(pe, "normo", lambda c: pe.wait_ge(s["o"], c + 1))
            gemm(pe, w("g_wo"), slot(9), 4, "wo_ps", ready="gated")
            rms2_pe(pe)
            for c in range(NC):
                pe.wait_ge(s["rms_ready"], NC + c + 1)
                for m in range(4):
                    k = 4 * c + m
                    if k >= 2:
                        pe.wait_ge(s["hid"], k - 1)
                    PE.matmul(ps[:, k % 2, :], w("w_gate")[:, m * P:(m + 1) * P], chunk(slot(3), c),
                              start=True, stop=True).then_inc(s["gate_ps"], 1)
                    PE.matmul(ps[:, 2 + k % 2, :], w("w_up")[:, m * P:(m + 1) * P], chunk(slot(3), c),
                              start=True, stop=True).then_inc(s["up_ps"], 1)
                for m in range(4):
                    pe.wait_ge(s["hid"], 4 * c + m + 1)
                    mm = PE.matmul(ps[:, 4 + c, :], w("w_down")[:, m * C:(m + 1) * C],
                                   hidden(c)[:, m * CH:(m + 1) * CH], start=(m == 0), stop=(m == 3))
                mm.then_inc(s["down_ps"], 1)
            norm_pe(pe, "norm3", lambda c: pe.wait_ge(s["x3"], c + 1))
            pe.wait_ge(s["slot_sum"], 1)
            PE.matmul(ps[:, 4, 0:1], w("w1s"), slot_sum, start=True, stop=True).then_inc(s["hb_ps"], 1)
            pe.wait_ge(s["hb"], 1)
            gemm(pe, w("w1x"), slot(0), 4, "h_ps", ready=lambda c: norm_ready("norm3", c))
            for i in range(NT):
                if i == 0:
                    pe.wait_ge(*norm_ready("norm3", NC - 1))
                pe.wait_ge(s["h"], i // 4 + 1)
                PE.matmul(ps[:, i // 8, (i % 8) * 64:(i % 8 + 1) * 64], slot(3)[:, i * P:(i + 1) * P], w("w2"),
                          start=True, stop=True).then_inc(s["logit_ps"], 1)
            for i in range(NT):
                PE.transpose(ps[:, 4 + i // 4, (i % 4) * P:(i % 4 + 1) * P], slot(0)[:, i * P:(i + 1) * P], w("ident"))\
                    .then_inc(s["xt_ps"], 1)

            pe.wait_ge(s["alpha"], 2)
            for i in range(NT):
                PE.transpose(ps[:, i // 4, (i % 4) * P:(i % 4 + 1) * P], alpha[:, i, :], w("ident"))\
                    .then_inc(s["at_ps"], 1)
            pe.wait_ge(s["xt"], NC)
            for i in range(NT):
                mm = PE.matmul(ps[:, 4 + i // 4, (i % 4) * P:(i % 4 + 1) * P], xtok[:, i, :], alpha[:, i, :],
                               start=True, stop=True)
                if i % 4 == 3:
                    mm.then_inc(s["si_ps"], 1)
            for c in range(NC):
                pe.wait_ge(s["at"], c + 1)
                PE.matmul(ps[:, c, :], w("ones"), chunk(alphas, c), start=True, stop=True).then_inc(s["sd_ps"], 1)
            pe.wait_ge(s["sd"], NC)
            pe.wait_ge(s["si"], NC)
            for k in range(3):
                mm = PE.matmul(ps[:, 0, k * 64:(k + 1) * 64], w("whh")[:, k * P:(k + 1) * P], w("slots"),
                               start=True, stop=True)
            mm.then_inc(s["gh_ps"], 1)
            gemm(pe, w("wih")[:, 0:P], slot(9), 4, "gr_ps", free=None)
            pe.wait_ge(s["gh"], 3)
            gemm(pe, w("wih")[:, P:2 * P], slot(9), 0, "gz_ps")
            gemm(pe, w("wih")[:, 2 * P:3 * P], slot(9), 4, "gn_ps", free="r_in")
            gemm(pe, w("s_wq"), slot(5), 0, "sq_ps", ready="snew")
            gemm(pe, w("s_wk"), slot(5), 4, "sk_ps")
            pe.wait_ge(s["sk"], NC)
            pe.wait_ge(s["sq"], NC)
            for i in range(NT):
                mm = PE.matmul(ps[:, i // 4, (i % 4) * P:(i % 4 + 1) * P], slot(9)[:, i * P:(i + 1) * P],
                               slot(10)[:, i * P:(i + 1) * P], start=True, stop=True)
            mm.then_inc(s["sc_ps"], 1)
            for i in range(NT):
                mm = PE.matmul(ps[:, 4 + i // 4, (i % 4) * P:(i % 4 + 1) * P], slot(5)[:, i * P:(i + 1) * P],
                               w("s_wv"), start=True, stop=True)
                if i % 4 == 3:
                    mm.then_inc(s["sv_ps"], 1)
            pe.wait_ge(s["attn"], 2)
            for i in range(NT):
                t = PE.transpose(ps[:, i // 4, (i % 4) * P:(i % 4 + 1) * P], att[:, i, :], w("ident"))
                if i % 4 == 3:
                    t.then_inc(s["attt_ps"], 1)
            for i in range(NT):
                if i % 4 == 0:
                    pe.wait_ge(s["sv"], NC)
                    pe.wait_ge(s["attt"], i // 4 + 1)
                mm = PE.matmul(ps[:, 4 + i // 4, (i % 4) * P:(i % 4 + 1) * P], vs[:, i, :],
                               slot(12)[:, i * P:(i + 1) * P], start=True, stop=True)
                if i % 4 == 3:
                    mm.then_inc(s["comm_ps"], 1)
            norm_pe(pe, "norms", lambda c: pe.wait_ge(s["y"], c + 1))
            for i in range(NT):
                if i % 4 == 0:
                    pe.wait_ge(s["y2"], i // 4 + 1)
                mm = PE.matmul(ps[:, 4 + i // 4, (i % 4) * P:(i % 4 + 1) * P], slot(10)[:, i * P:(i + 1) * P],
                               w("s_wvp"), start=True, stop=True)
                if i % 4 == 3:
                    mm.then_inc(s["svp_ps"], 1)
            for i in range(NT):
                if i % 4 == 0:
                    pe.wait_ge(s["svp"], i // 4 + 1)
                mm = PE.matmul(ps[:, i // 4, (i % 4) * P:(i % 4 + 1) * P], svp[:, i, :],
                               slot(8)[:, i * P:(i + 1) * P], start=True, stop=True)
                if i % 4 == 3:
                    mm.then_inc(s["read_ps"], 1)
            gemm(pe, w("s_wo"), slot(11), 4, "fin_ps", ready="read")

        @block.scalar
        def _(act):
            A.sem_inc(s["exp_done"], 2)
            act.dma_start(X[:, :], x_t).then_inc(s["x_in"], 16)
            act.wait_ge(s["eps_set"], 1)
            norm_act(act, "norm1")
            for c in range(NC):
                act.wait_ge(s["q_sb"], c + 1)
                A.copy(chunk(q_parts[:, 0, :], c), chunk(QT, c)).then_inc(s["q_high"], 1)
            act.wait_ge(s["q_low"], NC)
            for g in range(2, 4):
                stack_queries(nc.scalar, g)
            with act.Fori(0, HALF) as j:
                for u in range(2):
                    act_batch(act, j, u)
            act.wait_ge(s["flag_ready"], 1)
            f = act.value_load(flag[0:1, 0:1])
            with act.If(f < P):
                with act.Fori(0, B) as b:
                    for h in range(PAIRS):
                        act.wait_ge(s["g_max"], PAIRS * b + h + 1)
                        A.activation(s_sb, s_sb, ACT.Exp, bias=row_neg).then_inc(s["g_exp"], 1)
            norm_act(act, "norm2")
            rms1_act(act)
            for c in range(NC):
                act.wait_ge(s["gq_ps"], c + 1)
                A.copy(chunk(slot(4), c), ps[:, c, :]).then_inc(s["gq"], 1)
            for c in range(NC):
                act.wait_ge(s["g1_ps"], c + 1)
                A.activation(chunk(slot(2), c), ps[:, c, :], ACT.Silu, bias=bias("bg1"))\
                    .then_inc(s["g1"], 1)
            for c in range(NC):
                act.wait_ge(s["og_ps"], c + 1)
                A.activation(chunk(slot(8), c), ps[:, 4 + c, :], ACT.Silu, bias=bias("bog")).then_inc(s["og"], 1)
            act.wait_ge(s["bg2_scaled"], 1)
            for c in range(NC):
                act.wait_ge(s["g2_ps"], c + 1)
                A.activation(by_query(slot(7))[:, 8 * c:8 * c + 8, :],
                             ps[:, c, :].rearrange("p (t b) -> p t b", b=NQ), ACT.Sigmoid,
                             bias=small[:, 463:464], scale=1.0 / 16.0).then_inc(s["decay"], 1)
            for c in range(NC):
                act.wait_ge(s["osum_ps"], NC * (D - 1) + c + 1)
                A.copy(chunk(slot(6), c), ps[:, 4 + c, :]).then_inc(s["o"], 1)
            norm_act(act, "normo")
            rms2_act(act)
            for k in range(16):
                act.wait_ge(s["gate_ps"], k + 1)
                if k >= 4:
                    act.wait_ge(s["hid"], k - 3)
                A.activation(gates(k), ps[:, k % 2, :], ACT.Silu).then_inc(s["gate"], 1)
            norm_act(act, "norm3")
            act.wait_ge(s["hb"], 1)
            for c in range(NC):
                act.wait_ge(s["h_ps"], c + 1)
                A.activation(chunk(slot(3), c), ps[:, 4 + c, :], ACT.Gelu, bias=hid_bias)\
                    .then_inc(s["h"], 1)
            for c in range(NC):
                act.wait_ge(s["xt_ps"], 4 * c + 4)
                A.copy(chunk(slot(7), c), ps[:, 4 + c, :]).then_inc(s["xt"], 1)
            act.wait_ge(s["shifted"], 1)
            A.activation(expo, expo, ACT.Exp).then_inc(s["expo"], 1)
            for c in range(NC):
                act.wait_ge(s["at_ps"], 4 * c + 4)
                A.copy(chunk(slot(8), c), ps[:, c, :]).then_inc(s["at"], 1)
            for c in range(NC):
                act.wait_ge(s["r_in"], c + 1)
                A.activation(chunk(slot(1), c), chunk(slot(1), c), ACT.Sigmoid).then_inc(s["r"], 1)
            for c in range(NC):
                act.wait_ge(s["z_in"], c + 1)
                A.activation(chunk(slot(2), c), chunk(slot(2), c), ACT.Sigmoid).then_inc(s["z"], 1)
            for c in range(NC):
                act.wait_ge(s["n_in"], c + 1)
                A.activation(chunk(slot(3), c), chunk(slot(3), c), ACT.Tanh, bias=bias("bih_n")).then_inc(s["n"], 1)
            for c in range(NC):
                act.wait_ge(s["sq_ps"], c + 1)
                A.activation(chunk(slot(9), c), ps[:, c, :], ACT.Identity, bias=bias("s_bq"))\
                    .then_inc(s["sq"], 1)
            for c in range(NC):
                act.wait_ge(s["sk_ps"], c + 1)
                A.activation(chunk(slot(10), c), ps[:, 4 + c, :], ACT.Identity, bias=bias("s_bk"))\
                    .then_inc(s["sk"], 1)
            act.wait_ge(s["att_in"], 2)
            A.activation(att_in, att_in, ACT.Exp, scale=DQ ** -0.5).then_inc(s["att_exp"], 1)
            for c in range(NC):
                act.wait_ge(s["sv_ps"], c + 1)
                A.copy(chunk(slot(1), c), ps[:, 4 + c, :]).then_inc(s["sv"], 1)
            norm_act(act, "norms")
            for c in range(NC):
                act.wait_ge(s["svp_ps"], c + 1)
                A.copy(chunk(slot(3), c), ps[:, 4 + c, :]).then_inc(s["svp"], 1)
            for c in range(NC):
                act.wait_ge(s["read_ps"], c + 1)
                A.activation(chunk(slot(11), c), ps[:, c, :], ACT.Identity, bias=bias("s_bvp")).then_inc(s["read"], 1)

        @block.vector
        def _(dve):
            V.sem_inc(s["turn_out"], 2)
            V.sem_inc(s["acc_out"], 2)
            V.sem_inc(s["fin_out"], 1)
            V.sem_inc(s["g_ctx_free"], 1)
            V.sem_inc(s["g_done"], 1)
            V.memset(eps[:, :], 1e-5).then_inc(s["eps_set"], 1)
            V.memset(okay, 1.0).then_inc(s["okay_set"], 1)
            V.memset(real_all, 1.0).then_inc(s["okay_set"], 1)
            for i in range(4):
                dve.wait_ge(s["turn_ps"], i + 1)
                dve_keys(dve, i, 6 + i % 2, None, i + 1)
            norm_dve(dve, "norm1")

            def q_low(c):
                dve.wait_ge(s["q_high"], c + 1)
                V.tensor_tensor(chunk(q_parts[:, 1, :], c), chunk(QT, c), chunk(q_parts[:, 0, :], c), ALU.subtract)\
                    .then_inc(s["q_low"], 1)

            for c in range(NC):
                dve.wait_ge(s["q_ps"], c + 1)
                V.tensor_scalar(chunk(QT, c), ps[:, 4 + c, :], bias("x_bq"), SCALE, ALU.add, ALU.mult)\
                    .then_inc(s["q_sb"], 1)
                if c >= 1:
                    q_low(c - 1)
            q_low(NC - 1)
            for i in range(4, 8):
                dve.wait_ge(s["turn_ps"], i + 1)
                dve_values(0, i % 4, 6 + i % 2).then_inc(s["turn_out"], 1)
            dve.wait_ge(s["okay_set"], 2)
            dve_body(dve, 0, first=True)
            with dve.Fori(1, HALF - 1) as j:
                dve_body(dve, j)
            dve_body(dve, HALF - 1, last=True)
            all_rows(dve, okay, okay_min, 0)
            dve.wait_ge(s["flag_ready"], 1)
            f = dve.value_load(flag[0:1, 0:1])
            with dve.If(f < P):
                with dve.Fori(0, B) as b:
                    g_dve(dve, b)
                all_rows(dve, real_all, real_min, 1)
                dve.wait_ge(s["v_mean_ps"], 1)
                V.tensor_scalar(v_mean, ps[:, 4, 0:B], 1.0 / NKV, None, ALU.mult).then_inc(s["v_mean"], 1)
                dve.wait_ge(s["v_mean"], 1)
                dve.wait_ge(s["flag_ready"], 2)
                nan = dve.value_load(flag[0:1, 1:2])
                with dve.If(nan < P):
                    V.tensor_copy(AT[:, :].rearrange("p (b q) -> p b q", b=B),
                                  v_mean.unsqueeze(2).broadcast_to([P, B, NQ])).then_inc(s["v_mean"], 1)
                    dve.wait_ge(s["v_mean"], 2)
                V.sem_inc(s["g_end"], 1)
            for c in range(NC):
                V.tensor_scalar(chunk(AT, c), chunk(AT, c), bias("x_bv"), None, ALU.add).then_inc(s["ao"], 1)
            for c in range(NC):
                dve.wait_ge(s["xo_ps"], c + 1)
                V.scalar_tensor_tensor(chunk(X, c), ps[:, 4 + c, :], bias("x_bo"), chunk(X, c), ALU.add, ALU.add)\
                    .then_inc(s["x1"], 1)
            norm_dve(dve, "norm2", between=lambda: rms1_stats(dve))
            dve.wait_ge(s["wb_in"], 16)
            V.tensor_scalar(small[:, 463:464], bias("bg2"), 1.0 / 16.0, None, ALU.mult).then_inc(s["bg2_scaled"], 1)
            rms1_dve(dve)
            for c in range(NC):
                dve.wait_ge(s["gk_ps"], c + 1)
                V.tensor_copy(chunk(slot(5), c), ps[:, 4 + c, :]).then_inc(s["gk"], 1)
            dve.wait_ge(s["decay"], NC)
            dve.wait_ge(s["gk"], NC)
            V.memset(slot(7).rearrange("p (b t) -> p b t", t=B)[:, :, 0:1], 0.0).then_inc(s["decay_set"], 1)
            dve.wait_ge(s["decay_set"], 1)
            for v in range(D):
                for c in range(NC):
                    dve.wait_ge(s["vv_ps"], NC * v + c + 1)
                    if v >= 2:
                        dve.wait_ge(s["scan"], v - 1)
                    V.tensor_tensor(by_query(slot(9 + v % 2))[:, 8 * c:8 * c + 8, :],
                                    ps[:, c, :].rearrange("p (t b) -> p t b", b=NQ),
                                    chunk(slot(5), c).rearrange("p (t b) -> p t b", b=NQ), ALU.mult)\
                        .then_inc(s["kv"], 1)
                dve.wait_ge(s["kv"], NC * (v + 1))
                if v >= 2:
                    dve.wait_ge(s["qs"], NC * (v - 1))
                V.tensor_tensor_scan(slot(11 + v % 2), slot(7), slot(9 + v % 2), 0.0, ALU.mult, ALU.add)\
                    .then_inc(s["scan"], 1)
            norm_dve(dve, "normo")
            for c in range(NC):
                dve.wait_ge(*norm_ready("normo", c))
                V.tensor_tensor(chunk(slot(9), c), chunk(slot(6), c), chunk(slot(8), c), ALU.mult)\
                    .then_inc(s["gated"], 1)
            for c in range(NC):
                dve.wait_ge(s["wo_ps"], c + 1)
                V.tensor_tensor(chunk(slot(10), c), chunk(slot(0), c), ps[:, 4 + c, :], ALU.add).then_inc(s["x2"], 1)
            rms2_dve(dve)
            for c in range(NC):
                for m in range(4):
                    k = 4 * c + m
                    dve.wait_ge(s["gate"], k + 1)
                    dve.wait_ge(s["up_ps"], k + 1)
                    if c >= 2:
                        dve.wait_ge(s["down_ps"], c - 1)
                    V.tensor_tensor(hidden(c)[:, m * CH:(m + 1) * CH], gates(k), ps[:, 2 + k % 2, :], ALU.mult)\
                        .then_inc(s["hid"], 1)
                dve.wait_ge(s["down_ps"], c + 1)
                dve.wait_ge(s["x12"], c + 1)
                V.tensor_tensor(chunk(X, c), chunk(X, c), ps[:, 4 + c, :], ALU.add).then_inc(s["x3"], 1)
            norm_dve(dve, "norm3")
            V.tensor_reduce(slot_sum, w("slots"), AX.X, ALU.add).then_inc(s["slot_sum0"], 1)
            V.scalar_tensor_tensor(tau_inv, bias("tau"), -1.0, bias("tau"), ALU.mult, ALU.max).then_inc(s["tau"], 1)
            dve.wait_ge(s["tau"], 1)
            V.tensor_scalar(tau_inv, tau_inv, 0.1, None, ALU.add).then_inc(s["tau"], 1)
            dve.wait_ge(s["tau"], 2)
            V.reciprocal(tau_inv, tau_inv).then_inc(s["tau"], 1)
            dve.wait_ge(s["slot_sum0"], 1)
            V.tensor_scalar(slot_sum, slot_sum, 1.0 / SLOTS, None, ALU.mult).then_inc(s["slot_sum"], 1)
            dve.wait_ge(s["hb_ps"], 1)
            V.tensor_tensor(hid_bias, ps[:, 4, 0:1], bias("b1"), ALU.add).then_inc(s["hb"], 1)
            dve.wait_ge(s["logit_ps"], NT)
            V.tensor_tensor(logits, ps[:, 0:2, :].rearrange("p a (i s) -> p (a i) s", s=64),
                            w("b2").unsqueeze(1).broadcast_to([P, NT, SLOTS]), ALU.add).then_inc(s["route"], 1)
            dve.wait_ge(s["route"], 1)
            dve.wait_ge(s["tau"], 3)
            V.tensor_scalar(logits, logits, tau_inv, None, ALU.mult).then_inc(s["route"], 1)
            dve.wait_ge(s["route"], 2)
            for i in range(NT):
                V.max(top[:, i, :], logits[:, i, :]).then_inc(s["top"], 1)
            for i in range(NT):
                dve.wait_ge(s["top"], i + 1)
                V.match_replace(replaced[:, i, :], top[:, i, :], logits[:, i, :], -3.0e38).then_inc(s["picked"], 1)
            dve.wait_ge(s["top"], NT)
            V.tensor_tensor(expo, logits, top[:, :, 0:1].broadcast_to([P, NT, SLOTS]), ALU.subtract)\
                .then_inc(s["shifted"], 1)
            dve.wait_ge(s["picked"], NT)
            V.tensor_tensor(mask, logits, replaced, ALU.not_equal).then_inc(s["mask"], 1)
            dve.wait_ge(s["mask"], 1)
            dve.wait_ge(s["expo"], 1)
            V.tensor_tensor(expo, expo, mask, ALU.mult).then_inc(s["mask"], 1)
            dve.wait_ge(s["mask"], 2)
            V.tensor_reduce(row16, expo, AX.X, ALU.add).then_inc(s["mask"], 1)
            dve.wait_ge(s["mask"], 3)
            V.reciprocal(row16b, row16).then_inc(s["mask"], 1)
            dve.wait_ge(s["mask"], 4)
            dve.wait_ge(s["zeroed"], 1)
            diagonal(alpha, expo, "alpha")
            for c in range(NC):
                dve.wait_ge(s["sd_ps"], c + 1)
                V.tensor_scalar(chunk(slot(10), c), ps[:, c, :], 1e-8, None, ALU.add).then_inc(s["sd"], 1)
                dve.wait_ge(s["sd"], c + 1)
                V.reciprocal(chunk(slot(10), c), chunk(slot(10), c)).then_inc(s["sd_inv"], 1)
                dve.wait_ge(s["sd_inv"], c + 1)
                dve.wait_ge(s["si_ps"], c + 1)
                V.tensor_tensor(chunk(slot(9), c), ps[:, 4 + c, :], chunk(slot(10), c), ALU.mult).then_inc(s["si"], 1)
            dve.wait_ge(s["gh_ps"], 1)
            for k, names in enumerate((("bhh_r", "bih_r"), ("bhh_z", "bih_z"), ("bhh_n", "zero"))):
                V.tensor_scalar(gh[:, k, :], ps[:, 0, k * 64:(k + 1) * 64], bias(names[0]), bias(names[1]),
                                ALU.add, ALU.add).then_inc(s["gh"], 1)
            dve.wait_ge(s["gh"], 3)
            rows = lambda c, bank: ps[:, bank + c, :].rearrange("p (b s) -> p b s", b=PB)
            part = lambda k, c: chunk(slot(k), c).rearrange("p (b s) -> p b s", b=PB)
            for c in range(NC):
                dve.wait_ge(s["gr_ps"], c + 1)
                V.tensor_tensor(part(1, c), rows(c, 4), over_batches(gh[:, 0, :]), ALU.add).then_inc(s["r_in"], 1)
            for c in range(NC):
                dve.wait_ge(s["gz_ps"], c + 1)
                V.tensor_tensor(part(2, c), rows(c, 0), over_batches(gh[:, 1, :]), ALU.add).then_inc(s["z_in"], 1)
            for c in range(NC):
                dve.wait_ge(s["r"], c + 1)
                V.tensor_tensor(part(3, c), part(1, c), over_batches(gh[:, 2, :]), ALU.mult).then_inc(s["rn"], 1)
                dve.wait_ge(s["rn"], c + 1)
                dve.wait_ge(s["gn_ps"], c + 1)
                V.tensor_tensor(part(3, c), part(3, c), rows(c, 4), ALU.add).then_inc(s["n_in"], 1)
            for c in range(NC):
                dve.wait_ge(s["n"], c + 1)
                V.tensor_tensor(part(4, c), over_batches(w("slots")), part(3, c), ALU.subtract).then_inc(s["mix"], 1)
                dve.wait_ge(s["mix"], 2 * c + 1)
                dve.wait_ge(s["z"], c + 1)
                V.tensor_tensor(part(4, c), part(4, c), part(2, c), ALU.mult).then_inc(s["mix"], 1)
                dve.wait_ge(s["mix"], 2 * c + 2)
                V.tensor_tensor(part(5, c), part(4, c), part(3, c), ALU.add).then_inc(s["snew"], 1)
            dve.wait_ge(s["sc_ps"], 1)
            for u in range(2):
                rows = slice(64 * u, 64 * u + 64)
                scores = ps[rows, 0:4, :].rearrange("p a (i t) -> p (a i) t", t=P)[:, :, 64 * u:64 * u + 64]
                V.tensor_reduce(row16[rows, :], scores, AX.X, ALU.max).then_inc(s["att_step"], 1)
                dve.wait_ge(s["att_step"], u + 1)
                V.tensor_tensor(att_in[rows, :, :], scores, row16[rows, :].unsqueeze(2).broadcast_to([64, NT, SLOTS]),
                                ALU.subtract).then_inc(s["att_in"], 1)
            dve.wait_ge(s["att_exp"], 1)
            V.tensor_reduce(row16, att_in, AX.X, ALU.add).then_inc(s["att_step"], 1)
            dve.wait_ge(s["att_step"], 3)
            V.reciprocal(row16b, row16).then_inc(s["att_step"], 1)
            dve.wait_ge(s["att_step"], 4)
            dve.wait_ge(s["zeroed"], 2)
            diagonal(att, att_in, "attn")
            for c in range(NC):
                dve.wait_ge(s["attt_ps"], c + 1)
                V.tensor_copy(chunk(slot(12), c), ps[:, c, :]).then_inc(s["attt"], 1)
            for c in range(NC):
                dve.wait_ge(s["comm_ps"], c + 1)
                V.scalar_tensor_tensor(chunk(slot(9), c), ps[:, 4 + c, :], bias("s_bv"), chunk(slot(5), c),
                                       ALU.add, ALU.add).then_inc(s["y"], 1)
            norm_dve(dve, "norms")
            for c in range(NC):
                dve.wait_ge(*norm_ready("norms", c))
                V.tensor_scalar(chunk(slot(10), c), chunk(slot(9), c), bias("ln_g"), bias("ln_b"),
                                ALU.mult, ALU.add).then_inc(s["y2"], 1)
            for c in range(NC):
                dve.wait_ge(s["fin_ps"], c + 1)
                V.scalar_tensor_tensor(chunk(AT, c), ps[:, 4 + c, :], bias("s_bo"), chunk(X, c), ALU.add, ALU.add)\
                    .then_inc(s["final"], 1)


def kernel(**inputs):
    import concourse.bacc as _bacc
    from concourse.bass_utils import run_bass_kernel_spmd as _run

    i = {k: np.asarray(v) for k, v in inputs.items()}
    a, f = (lambda k: i["L0_attn_" + k]), (lambda k: i["L0_ffn_" + k])
    one = np.ones((1, 1), np.float32)
    zero = np.zeros((1,), np.float32)
    head = np.arange(P) // D
    same = (head[:, None] == head[None, :]).astype(np.float32)
    mask = (head[:, None] == np.arange(H)[None, :]).astype(np.float32)
    sel_num, sel_den = np.zeros((P, 4, P), np.float32), np.zeros((P, 4, P), np.float32)
    for c in range(4):
        for r in range(2):
            for e in range(2):
                out = (2 * (c + 4 * r) + e) * D + np.arange(D)
                sel_num[32 * c + e * D + np.arange(D), 2 * r + e, out] = 1
                sel_den[32 * c + 16, 2 * r + e, out] = 1
    back, head_back = np.zeros((P, 4, P), np.float32), np.zeros((P, 4, P), np.float32)
    for c in range(4):
        back[32 * c, c, :] = 1
        head_back[32 * c + head, c, np.arange(P)] = 1
    head_sum = np.zeros((P, D, P), np.float32)
    for v in range(D):
        head_sum[np.arange(P), v, head * D + v] = 1
    wv = a("wv").T
    wv_rep = np.stack([wv[:, head * D + v] for v in range(D)], 1).reshape(C, D * C)
    bih, bhh = f("bih").reshape(3, C), f("bhh").reshape(3, C)
    cols = dict(x_bq=i["L0_xattn_bq"], x_bk=i["L0_xattn_bk"], x_bv=i["L0_xattn_bv"], x_bo=i["L0_xattn_bo"],
                scale1=a("scale1"), scale2=a("scale2"), bg1=a("bg1"), bg2=a("bg2"), bog=a("bog"), b1=f("b1"),
                bih_r=bih[0], bih_z=bih[1], bih_n=bih[2], bhh_r=bhh[0], bhh_z=bhh[1], bhh_n=bhh[2],
                s_bq=f("bq"), s_bk=f("bk"), s_bv=f("bv"), ln_g=f("ln_g"), ln_b=f("ln_b"), s_bvp=f("bvp"),
                s_bo=f("bo"), tau=np.broadcast_to(f("tau"), (P,)), zero=np.broadcast_to(zero, (P,)))

    def columns(names):
        m = np.zeros((P, len(names)), np.float32)
        for n, name in enumerate(names):
            m[:len(cols[name]), n] = cols[name]
        return m

    mats = dict(
        x_wq=i["L0_xattn_Wq"], x_wk=i["L0_xattn_Wk"], x_wv=i["L0_xattn_Wv"], x_wo=i["L0_xattn_Wo"],
        centre=np.eye(P, dtype=np.float32) - np.float32(1.0 / C), mean=np.full((P, 32), 1.0 / C, np.float32),
        back=back.reshape(P, -1), head_centre=np.eye(P, dtype=np.float32) - same * np.float32(1.0 / D),
        head_mean=np.tile(mask * np.float32(1.0 / D), (1, 2)), head_back=head_back.reshape(P, -1), head_mask=mask, row_mask=mask[:32, :4][np.arange(P) % 32], bias_a=columns(BIAS_A),
        sel_num=sel_num.reshape(P, -1), sel_den=sel_den.reshape(P, -1), ident=np.eye(P, dtype=np.float32),
        ones=np.ones((P, P), np.float32), g_wq=a("wq").T, g_wk=a("wk").T, g_wv=wv_rep, g_wg1=a("wg1").T,
        g_wg2=a("wg2").T, g_wog=a("wog").T, g_wo=a("wo").T, w_gate=a("w_gate").T, w_up=a("w_up").T,
        w_down=a("w_down").T.reshape(4, P, C).transpose(1, 0, 2).reshape(P, 4 * C),
        head_sum=head_sum.reshape(P, -1),
        bias_b=columns(BIAS_B), w1x=f("w1")[:C], w1s=f("w1")[C:], w2=f("w2"),
        b2=np.broadcast_to(f("b2"), (P, SLOTS)), wih=f("Wih").T, whh=f("Whh").T, s_wq=f("wq"), s_wk=f("wk"),
        s_wv=f("wv"), s_wvp=f("wvp"), s_wo=f("wo"), slots=f("slot_init").T)
    packed = [np.zeros((P, n), np.float32) for n in WIDTHS]
    for name, (g, col, rows, width) in WHERE.items():
        m = mats[name]
        packed[g][0:m.shape[0], col:col + m.shape[1]] = m
    arrays = {
        "x_t": np.ascontiguousarray(i["x"].reshape(TOK, C).T),
        "ctx_t": np.ascontiguousarray(i["ctx_768"].transpose(0, 2, 1)),
        "w_a": packed[0], "w_b": packed[1],
    }
    nc = _bacc.Bacc("TRN2", target_bir_lowering=False, num_devices=1)
    args = [nc.dram_tensor(k, v.shape, F32, kind="ExternalInput").ap() for k, v in arrays.items()]
    out = nc.dram_tensor("out_t", (C, TOK), F32, kind="ExternalOutput").ap()
    perceiver(nc, *args, out)
    r = _run(nc, [arrays], core_ids=[0])
    return np.ascontiguousarray(r.results[0]["out_t"].T).reshape(B, NQ, C)
```

```python
from contextlib import ExitStack

import numpy as np

import concourse.bass as bass
from concourse import mybir

F32 = mybir.dt.float32
BF16 = mybir.dt.bfloat16
F16 = mybir.dt.float16
I32 = mybir.dt.int32
ALU = mybir.AluOpType
ACT = mybir.ActivationFunctionType
AX = mybir.AxisListType

P = 128
B, NQ, C = 32, 64, 128
NKV, CKV = 1601, 96
H, D = 16, 8
TOK = B * NQ
CH = 512
NC = TOK // CH
NB = -(-NKV // P)
PAIRS = H // 2
SCALE = D ** -0.5
CLAMP = 10000.0
HID = 4 * C
SLOTS = 64
DQ = C // 4
NT = TOK // P
PB = CH // NQ
KCH = [(c * CH, min(CH, NKV - c * CH)) for c in range(-(-NKV // CH))]
KBL = [(i * P, min(P, NKV - i * P)) for i in range(NB)]
V_COPIES = 12
NSTACK = 16
UNITS = len(KCH) + 4
TURNS = {0: [(0, None), (1, None)], 1: [(2, None)], 2: [(3, None)], 4: [(4, 0)], 5: [(4, 1)], 6: [(5, 0)],
         7: [(5, 1)], 8: [(6, 0)], 9: [(6, 1)], 10: [(7, None)]}
GATHERS = (3, 11)
SUBS = {"": 4, "head_": 2}
QS_POOL = NC - 1
PICKED = -3.0e38
SUM_LOW, SUM_HIGH = 1e-10, 1e30


def pack():
    first = [("x_wq", C, C), ("x_wk", CKV, C), ("x_wv", CKV, C), ("centre", P, P), ("mean", P, SUBS[""] * 32),
             ("pick", P, NC * SUBS[""]),
             ("head_mask", P, H), ("row_mask", P, 4), ("bias_a", P, 4)]
    second = [("sel_num", P, 4 * P), ("sel_den", P, 4 * P), ("ident", P, P), ("ones", P, P), ("x_wo", C, C),
              ("g_wq", C, C), ("g_wk", C, C), ("g_wv", C, C), ("spread", 3 * 2 * H, 2 * P),
              ("g_wg1", C, P), ("g_wg2", P, C),
              ("g_wog", C, C), ("g_wo", C, C), ("w_gate", C, HID), ("w_up", C, HID), ("w_down", C, 4 * C),
              ("head_sum", P, D * P), ("head_centre", P, P), ("head_mean", P, SUBS["head_"] * 32),
              ("head_back", P, NC * SUBS["head_"] * P),
              ("bias_b", P, 21), ("w1x", C, P),
              ("w1s", C, P), ("w2", P, SLOTS), ("b2", P, SLOTS), ("wih", C, 3 * C), ("whh", C, 3 * C),
              ("s_wq", C, P), ("s_wk", C, P), ("s_wv", C, C), ("s_wvp", C, C), ("s_wo", C, C),
              ("slots", C, SLOTS)]
    where, widths = {}, []
    for a, group in enumerate((first, second)):
        col = 0
        for name, rows, cols in group:
            where[name] = (a, col, rows, cols)
            col += cols
        widths.append(col)
    return where, widths


WHERE, WIDTHS = pack()
BIAS_A = ["x_bq", "x_bk", "x_bv", "x_bo"]
BIAS_B = ["scale1", "scale2", "bg1", "bg2", "bog", "b1", "bih_r", "bih_z", "bih_n", "bhh_r", "bhh_z",
          "bhh_n", "s_bq", "s_bk", "s_bv", "ln_g", "ln_b", "s_bvp", "s_bo", "tau", "zero"]


def perceiver(nc, x_t, ctx_t, w_a, w_b, out_t):
    with ExitStack() as stack:
        def sb(name, shape, dt=F32):
            return stack.enter_context(nc.sbuf_tensor(name, shape, dt))

        def sem(name):
            return stack.enter_context(nc.semaphore(name))

        WA = sb("WA", [P, WIDTHS[0]])
        WB = sb("WB", [P, WIDTHS[1]])
        X = sb("X", [P, TOK])
        AT = sb("AT", [P, TOK])
        QT = sb("QT", [P, TOK])
        arena = sb("arena", [P, 14 * TOK])
        small = sb("small", [P, 1024])
        stat = [sb("stat0", [P, CH // 2]), sb("stat1", [P, CH // 4])]
        back = sb("back", [P, NC * SUBS[""] * P])
        spread = sb("spread", [6 * H, 2 * P], BF16)
        flag = sb("flag", [1, 2], I32)
        PS = stack.enter_context(nc.psum_tensor("PS", [P, 8, CH], F32))

        def w(name):
            a, col, rows, cols = WHERE[name]
            return (WA, WB)[a][0:rows, col:col + cols]

        def bias(name, rows=P):
            group, array, names = (("bias_a", WA, BIAS_A) if name in BIAS_A else ("bias_b", WB, BIAS_B))
            col = WHERE[group][1] + names.index(name)
            return array[0:rows, col:col + 1]

        def slot(k, n=1):
            return arena[:, k * TOK:(k + n) * TOK]

        def chunk(buf, c):
            return buf[:, c * CH:(c + 1) * CH]

        used = [0]

        def carve(cols):
            used[0] += cols
            assert used[0] <= 14 * TOK
            return arena[:, used[0] - cols:used[0]]

        def halves(cols):
            return carve(cols // 2).bitcast(F16)

        ctx_sb = [carve(NKV)[0:CKV, :] for _ in range(2)]
        k_parts = halves(2 * NKV).rearrange("p (a k) -> p a k", a=2)
        k_stack0 = used[0]
        k_stack = [halves(4 * NKV).rearrange("p (g k) -> p g k", g=4) for _ in range(2)]
        k_stack1 = used[0]
        v_sb = [carve(NB * PAIRS * 32).rearrange("p (n h m) -> p n h m", n=NB, h=PAIRS) for _ in range(2)]
        q_stack = halves(4 * TOK).rearrange("p (g t) -> p g t", g=4)
        q_bd = [halves(H * NQ).rearrange("p (g h q) -> p g h q", g=4, h=4) for _ in range(2)]
        p_start = used[0]
        p_sb = [carve(H * NQ) for _ in range(2)]
        o_sb = carve(4 * P)
        fast_end = used[0]
        q_parts = halves(2 * TOK).rearrange("p (a t) -> p a t", a=2)
        used[0] = p_start
        first_squares = carve(TOK)
        used[0] = k_stack0
        gk_sb = carve(NKV)
        gq_bd = carve(H * NQ)
        s_sb = carve(NKV)
        pt_sb = carve(NB * P).rearrange("p (n q) -> p n q", n=NB)
        assert used[0] <= k_stack1
        okay = small[:, 780:908]
        okay_a = small[:, 0:128]
        okay_b = small[:, 128:256]
        recip = small[:, 320:448]
        roots = small[:, 470:480]
        okay_min = small[:, 256:257]
        g_recip = recip[:, 0:NQ]
        row_neg = small[:, 258:259]
        ctx_mean = small[0:CKV, 260:292]
        v_mean = small[:, 908:940]
        real = small[:, 0:64]
        real_all = small[:, 940:1004]
        real_min = small[:, 452:453]

        class Signals(dict):

            def __missing__(self, name):
                self[name] = sem(name)
                return self[name]

        s = Signals()
        ctx_in = [sem("ctx_in0"), sem("ctx_in1")]
        PE, V, A, G = nc.tensor, nc.vector, nc.scalar, nc.gpsimd
        eps = sb("eps", [P, 1])
        ps = PS

        NORMS = {
            "norm1": (X, AT, AT, first_squares, ""),
            "norm2": (X, slot(0), slot(1), slot(2), ""),
            "normo": (slot(6), slot(6), slot(7), slot(11), "head_"),
            "norm3": (X, slot(0), slot(1), slot(2), ""),
            "norms": (slot(9), slot(9), slot(10), slot(11), ""),
        }
        ORDER = list(NORMS)

        def base(tag):
            return NC * ORDER.index(tag)

        def stat_rows(kind):
            return CH // SUBS[kind]

        def mean_of(squares, c, kind, bank):
            n = stat_rows(kind)
            for k in range(SUBS[kind]):
                mm = PE.matmul(ps[32 * c:32 * c + 32, bank, 0:n], w(kind + "mean")[:, k * 32:(k + 1) * 32],
                               squares[:, c * CH + k * n:c * CH + (k + 1) * n],
                               start=(k == 0), stop=(k == SUBS[kind] - 1))
            return mm

        def norm_ready(tag, c):
            return s["norm_ready"], base(tag) + c + 1

        def spread_back(stats, kind, bank, c):
            n, matrix = stat_rows(kind), (w("head_back") if kind else back)
            for k in range(SUBS[kind]):
                at = (SUBS[kind] * c + k) * P
                mm = PE.matmul(ps[:, bank, k * n:(k + 1) * n], matrix[:, at:at + P], stats[:, 0:n],
                               start=True, stop=True)
            return mm

        def norm_pe(pe, tag, src_ready, between=None):
            src, dst, centred, square, kind = NORMS[tag]
            for c in range(NC):
                src_ready(c)
                PE.matmul(ps[:, c, :], w(kind + "centre"), chunk(src, c), start=True, stop=True)\
                    .then_inc(s["norm_mean"], 1)
            for c in range(NC):
                pe.wait_ge(s["norm_squared"], base(tag) + c + 1)
                mm = mean_of(square, c, kind, 4)
            mm.then_inc(s["norm_var"], 1)
            if between is not None:
                between()
            pe.wait_ge(s["norm_inverse"], ORDER.index(tag) + 1)
            if tag == ORDER[0]:
                pe.wait_ge(s["back_set"], 1)
            for c in range(NC):
                spread_back(stat[0], kind, c, c).then_inc(s["norm_back"], 1)

        def norm_act(act, tag):
            src, dst, centred, square, kind = NORMS[tag]
            A.activation(roots[:, ORDER.index(tag):ORDER.index(tag) + 1], eps[:, 0:1], ACT.Sqrt)
            for c in range(NC):
                act.wait_ge(s["norm_centred"], base(tag) + c + 1)
                A.activation(chunk(square, c), chunk(centred, c), ACT.Square).then_inc(s["norm_squared"], 1)
            act.wait_ge(s["norm_var"], ORDER.index(tag) + 1)
            n = stat_rows(kind)
            A.activation(stat[0][:, 0:n], ps[:, 4, 0:n], ACT.Sqrt, bias=eps[:, 0:1]).then_inc(s["norm_root"], 1)

        def norm_dve(dve, tag, between=None):
            src, dst, centred, square, kind = NORMS[tag]
            for c in range(NC):
                dve.wait_ge(s["norm_mean"], base(tag) + c + 1)
                V.tensor_copy(chunk(centred, c), ps[:, c, :]).then_inc(s["norm_centred"], 1)
            dve.wait_ge(s["norm_root"], ORDER.index(tag) + 1)
            n = stat_rows(kind)
            V.reciprocal(stat[0][:, 0:n], stat[0][:, 0:n]).then_inc(s["norm_inverse"], 1)
            if between is not None:
                between()
            for c in range(NC):
                dve.wait_ge(s["norm_back"], base(tag) + c + 1)
                V.tensor_tensor(chunk(dst, c), chunk(centred, c), ps[:, c, :], ALU.mult).then_inc(s["norm_ready"], 1)

        def rms1_pe(pe):
            pe.wait_ge(s["rms_inverse"], 1)
            for c in range(NC):
                spread_back(stat[1], "", 4 + c, c).then_inc(s["rms_back"], 1)

        def rms1_act(act):
            A.activation(stat[1][:, :], ps[:, 4, 0:CH // 4], ACT.Sqrt).then_inc(s["rms_root"], 1)

        def rms1_stats(dve):
            dve.wait_ge(s["rms_root"], 1)
            dve.wait_ge(s["norm_inverse"], 2)
            V.tensor_tensor(stat[1][:, :], stat[1][:, :], stat[0][:, 0:CH // 4], ALU.mult).then_inc(s["rms_step"], 1)
            dve.wait_ge(s["rms_step"], 1)
            V.tensor_scalar(stat[1][:, :], stat[1][:, :], 1e-6, None, ALU.add).then_inc(s["rms_step"], 1)
            dve.wait_ge(s["rms_step"], 2)
            V.reciprocal(stat[1][:, :], stat[1][:, :]).then_inc(s["rms_step"], 1)
            dve.wait_ge(s["rms_step"], 3)
            V.tensor_tensor(stat[1][:, :], stat[1][:, :], stat[0][:, 0:CH // 4], ALU.mult).then_inc(s["rms_inverse"], 1)

        def rms1_dve(dve):
            for c in range(NC):
                dve.wait_ge(s["rms_back"], c + 1)
                V.scalar_tensor_tensor(chunk(slot(3), c), chunk(slot(1), c), bias("scale1"), ps[:, 4 + c, :],
                                       ALU.mult, ALU.mult).then_inc(s["rms_ready"], 1)

        def rms2_pe(pe):
            for c in range(NC):
                pe.wait_ge(s["rms_squared"], c + 1)
                mm = mean_of(slot(1), c, "", 0)
            mm.then_inc(s["rms_mean"], 1)
            pe.wait_ge(s["rms_inverse"], 2)
            for c in range(NC):
                spread_back(stat[1][:, :], "", 4 + c, c).then_inc(s["rms_back"], 1)

        def rms2_act(act):
            A.activation(roots[:, 9:10], eps[:, 0:1], ACT.Sqrt)
            for c in range(NC):
                act.wait_ge(s["x2"], c + 1)
                A.activation(chunk(slot(1), c), chunk(slot(10), c), ACT.Square).then_inc(s["rms_squared"], 1)
            act.wait_ge(s["rms_mean"], 1)
            A.activation(stat[1][:, :], ps[:, 0, 0:CH // 4], ACT.Sqrt).then_inc(s["rms_root"], 1)

        def rms2_dve(dve):
            dve.wait_ge(s["rms_root"], 2)
            V.tensor_scalar(stat[1][:, :], stat[1][:, :], 1e-6, None, ALU.add).then_inc(s["rms_step"], 1)
            dve.wait_ge(s["rms_step"], 4)
            V.reciprocal(stat[1][:, :], stat[1][:, :]).then_inc(s["rms_inverse"], 1)
            for c in range(NC):
                dve.wait_ge(s["rms_back"], NC + c + 1)
                V.scalar_tensor_tensor(chunk(slot(3), c), chunk(slot(10), c), bias("scale2"), ps[:, 4 + c, :],
                                       ALU.mult, ALU.mult).then_inc(s["rms_ready"], 1)

        def turn(b, i):
            return UNITS * b + 8 + i

        def pe_keys(u, c, bank):
            k0, n = KCH[c]
            return PE.matmul(ps[:, bank, 0:n], w("x_wk"), ctx_sb[u][:, k0:k0 + n], start=True, stop=True)

        def pe_values(u, g, bank, half=None):
            blocks = list(range(4 * g, min(4 * g + 4, NB)))
            for i in blocks if half is None else blocks[2 * half:2 * half + 2]:
                k0, n = KBL[i]
                o = (i - 4 * g) * P
                mm = PE.matmul(ps[0:n, bank, o:o + P], ctx_sb[u][:, k0:k0 + n], w("x_wv"), start=True, stop=True)
            return mm

        def dve_keys(dve, c, bank, stacked, high):
            k0, n = KCH[c]
            hi, lo = k_parts[:, 0, k0:k0 + n], k_parts[:, 1, k0:k0 + n]
            if stacked is not None and c == 0:
                dve.wait_ge(s["k_stacked"], stacked)
            V.tensor_scalar(hi, ps[:, bank, 0:n], bias("x_bk"), None, ALU.add).then_inc(s["k_high"], 1)
            dve.wait_ge(s["k_high"], high)
            V.scalar_tensor_tensor(lo, ps[:, bank, 0:n], bias("x_bk"), hi, ALU.add, ALU.subtract)\
                .then_inc(s["turn_out"], 1)

        def g_keys(c):
            k0, n = KCH[c]
            return V.tensor_scalar(gk_sb[:, k0:k0 + n], ps[:, c, 0:n], bias("x_bk"), None, ALU.add)

        def stack_keys(queue, u):
            for g in range(4):
                for c in range(4):
                    queue.dma_start(k_stack[u][32 * c:32 * c + 32, g, :], k_parts[32 * g:32 * g + 32, c % 2, :])\
                        .then_inc(s["k_stacked"], 16)

        def stack_queries(queue, g):
            for c in range(4):
                queue.dma_start(q_stack[32 * c:32 * c + 32, g, :], q_parts[32 * g:32 * g + 32, c // 2, :])\
                    .then_inc(s["q_stacked"], 16)

        def dve_values(u, g, bank):
            n, rows = (4, P) if g < 3 else (1, KBL[-1][1])
            return V.tensor_copy(v_sb[u][0:rows, 4 * g:4 * g + n, :, 0:16],
                                 ps[0:rows, bank, 0:n * P].rearrange("p (n h m) -> p n h m", n=n, h=PAIRS))

        def pe_finish(o, width, bank, col, kinds=(0, 1)):
            for k in kinds:
                for i in range(4):
                    at = col + k * width
                    mm = PE.matmul(ps[:, bank, at:at + width], w(("sel_num", "sel_den")[k])[:, i * P:(i + 1) * P],
                                   o[:, i * width:(i + 1) * width], start=(i == 0), stop=(i == 3))
            return mm

        def q_blocks(b, u):
            return G.tensor_tensor(q_bd[u], q_stack[:, :, bass.ds(b * NQ, NQ)].unsqueeze(2).broadcast_to([P, 4, 4, NQ]),
                                   w("row_mask").unsqueeze(1).unsqueeze(3).broadcast_to([P, 4, 4, NQ]), ALU.mult)

        def g_q_blocks(b):
            return G.tensor_tensor(gq_bd.rearrange("p (h q) -> p h q", h=H),
                                   QT[:, bass.ds(b * NQ, NQ)].unsqueeze(1).broadcast_to([P, H, NQ]),
                                   w("head_mask").unsqueeze(2).broadcast_to([P, H, NQ]), ALU.mult)

        def pe_pv(pe, j, u, i):
            b = 2 * j + u
            n, par, rows = NB * b + i, (NB * u + i) % 2, KBL[i][1]
            pe.wait_ge(s["exp_done"], n + 3)
            if i == 0:
                pe.wait_ge(s["turn_out"], turn(b, 0) + 2)
                pe.wait_ge(s["acc_out"], b + 1)
                if u == 1:
                    pe.wait_ge(s["fin_out"], j + 1)
            for h in range(PAIRS):
                c, r = h % 4, h // 4
                mm = PE.matmul(ps[32 * c:32 * c + 32, 4 + u, r * P:(r + 1) * P], v_sb[u][0:rows, i, h, :],
                               p_sb[par][0:rows, h * P:(h + 1) * P], start=(i == 0 and r == 0),
                               stop=(i == NB - 1), skip_group_check=True)
                if i == NB - 1 and h == 0:
                    mm.then_inc(s["q_free"], 1)
            mm.then_inc(s["pv_done"], 1)

        def pe_next(pe, j, u, t, half):
            b = 2 * j + u
            if t == 0:
                pe.wait_ge(ctx_in[1 - u], 16 * (j + 1 + u))
            if half != 1:
                pe.wait_ge(s["turn_out"], turn(b, t) + 1)
            if t < 4:
                mm = pe_keys(1 - u, t, 6 + t % 2)
            else:
                mm = pe_values(1 - u, t - 4, 6 + t % 2, half)
            if half != 0:
                mm.then_inc(s["turn_ps"], 1)

        def pe_scores(pe, b, u, i):
            n, par = NB * b + i, (NB * u + i) % 2
            if i == 0:
                pe.wait_ge(s["q_ready"], b + 1)
                pe.wait_ge(s["k_stacked"], 16 * NSTACK * (b + 1))
            pe.wait_ge(s["exp_done"], n + 1)
            k0, rows = KBL[i]
            for g in range(4):
                mm = PE.matmul(ps[0:rows, 2 * par + g // 2, (g % 2) * 256:(g % 2 + 1) * 256],
                               k_stack[u][:, g, k0:k0 + rows],
                               q_bd[u][:, g, :, :].rearrange("p h q -> p (h q)"), start=True, stop=True)
            mm.then_inc(s["score_ps"], 1)

        def pe_gather(pe, j, kind):
            if kind == 0:
                pe.wait_ge(s["acc_out"], 2 * j + 4)
            pe_finish(o_sb, P, 5, 2 * P, (kind,)).then_inc(s["gather_ps"], 1)

        def pe_body(pe, j, first=False, last=False):
            for u in range(2):
                b = 2 * j + u
                final = last and u == 1
                for i in range(NB):
                    if i < NB - 1:
                        pe_scores(pe, b, u, i + 1)
                    elif not final:
                        pe_scores(pe, b + 1, 1 - u, 0)
                    for t, half in TURNS.get(i, ()):
                        if not final:
                            pe_next(pe, j, u, t, half)
                    if u == 0 and i in GATHERS and not first:
                        pe_gather(pe, j - 1, GATHERS.index(i))
                    pe_pv(pe, j, u, i)
            if last:
                for kind in range(2):
                    pe_gather(pe, j, kind)

        def act_batch(act, j, u):
            b = 2 * j + u
            for i in range(NB):
                n, par, rows = NB * b + i, (NB * u + i) % 2, KBL[i][1]
                act.wait_ge(s["score_ps"], n + 1)
                act.wait_ge(s["pv_done"], n + 1)
                A.activation(p_sb[par][0:rows, :].rearrange("p (a n) -> p a n", a=2),
                             ps[0:rows, 2 * par:2 * par + 2, :], ACT.Exp).then_inc(s["exp_done"], 1)

        def dve_gather(dve, j):
            dve.wait_ge(s["gather_ps"], 2 * j + 2)
            num, den = ps[:, 5, 2 * P:3 * P], ps[:, 5, 3 * P:4 * P]
            V.reciprocal(recip, den).then_inc(s["sum_step"], 1)
            V.tensor_scalar(okay_a, den, SUM_LOW, None, ALU.is_ge).then_inc(s["sum_step"], 1)
            dve.wait_ge(s["sum_step"], 4 * j + 2)
            V.scalar_tensor_tensor(okay_b, den, SUM_HIGH, okay_a, ALU.is_le, ALU.mult).then_inc(s["sum_step"], 1)
            dve.wait_ge(s["sum_step"], 4 * j + 3)
            V.tensor_tensor(okay, okay, okay_b, ALU.mult).then_inc(s["sum_step"], 1)
            V.tensor_tensor(AT[:, bass.ds(j * P, P)], num, recip, ALU.mult).then_inc(s["fin_out"], 1)
            dve.wait_ge(s["sum_step"], 4 * j + 4)
            dve.wait_ge(s["fin_out"], j + 2)

        def dve_body(dve, j, first=False, last=False):
            for u in range(2):
                b = 2 * j + u
                for i in range(UNITS):
                    if last and u == 1:
                        break
                    dve.wait_ge(s["turn_ps"], turn(b, i) + 1)
                    if i < 4:
                        dve_keys(dve, i, 6 + i % 2, 16 * NSTACK * (b + 1), 4 * (b + 1) + i + 1)
                    else:
                        dve_values(1 - u, i % 4, 6 + i % 2).then_inc(s["turn_out"], 1)
                if u == 0 and not first:
                    dve_gather(dve, j - 1)
                dve.wait_ge(s["pv_done"], NB * b + NB + 2)
                V.tensor_copy(o_sb.rearrange("p (i u q) -> p i u q", i=4, u=2)[:, :, u, :],
                              ps[:, 4 + u, 0:2 * P].rearrange("p (i q) -> p i q", i=4)).then_inc(s["acc_out"], 1)
            if last:
                dve_gather(dve, j)

        def g_load(sp, b):
            sp.wait_ge(s["g_ctx_free"], b + 1)
            sp.dma_start(ctx_sb[0], ctx_t[bass.ds(b, 1), :, :].rearrange("a c k -> (a c) k")).then_inc(s["g_ctx"], 16)

        def g_pe(pe, b):
            pe.wait_ge(s["g_ctx"], 16 * (b + 1))
            pe.wait_ge(s["g_done"], b + 1)
            for c in range(4):
                pe_keys(0, c, c).then_inc(s["g_k_ps"], 1)
            for g in range(4):
                pe_values(0, g, 4 + g).then_inc(s["g_v_ps"], 1)
            pe.wait_ge(s["g_q"], b + 1)
            pe.wait_ge(s["g_kv_sb"], 8 * (b + 1))
            for h in range(PAIRS):
                n = PAIRS * b + h
                if h >= 1:
                    pe.wait_ge(s["g_pt"], 4 * n)
                for c, (k0, m) in enumerate(KCH):
                    PE.matmul(ps[:, c, 0:m], gq_bd[:, h * P:(h + 1) * P], gk_sb[:, k0:k0 + m],
                              start=True, stop=True).then_inc(s["g_s_ps"], 1)
                pe.wait_ge(s["g_exp"], n + 1)
                for i, (k0, rows) in enumerate(KBL):
                    bank, o = (4 + i // 4, (i % 4) * P) if i < 12 else (3, 0)
                    t = PE.transpose(ps[0:rows, bank, o:o + P], s_sb[:, k0:k0 + rows], w("ident"))
                t.then_inc(s["g_t_ps"], 1)
                pe.wait_ge(s["g_pt"], 4 * (n + 1))
                c, r = h % 4, h // 4
                for i, (k0, rows) in enumerate(KBL):
                    mm = PE.matmul(ps[32 * c:32 * c + 32, 7, r * P:(r + 1) * P], v_sb[0][0:rows, i, h, :],
                                   pt_sb[0:rows, i, :], start=(i == 0 and r == 0), stop=(i == NB - 1),
                                   skip_group_check=True)
                mm.then_inc(s["g_pv"], 1)
            pe.wait_ge(s["g_o"], b + 1)
            pe_finish(o_sb, NQ, 6, 0).then_inc(s["g_fin"], 1)

        def g_dve(dve, b):
            for c in range(4):
                dve.wait_ge(s["g_k_ps"], 4 * b + c + 1)
                g_keys(c).then_inc(s["g_kv_sb"], 1)
            for g in range(4):
                dve.wait_ge(s["g_v_ps"], 4 * b + g + 1)
                dve_values(0, g, 4 + g).then_inc(s["g_kv_sb"], 1)
            V.tensor_reduce(ctx_mean[:, bass.ds(b, 1)], ctx_sb[0], AX.X, ALU.add).then_inc(s["g_ctx_free"], 1)
            for h in range(PAIRS):
                n = PAIRS * b + h
                for c, (k0, m) in enumerate(KCH):
                    dve.wait_ge(s["g_s_ps"], 4 * n + c + 1)
                    V.tensor_scalar(s_sb[:, k0:k0 + m], ps[:, c, 0:m], CLAMP, -CLAMP, ALU.min, ALU.max)\
                        .then_inc(s["g_clip"], 1)
                dve.wait_ge(s["g_clip"], 4 * (n + 1))
                V.tensor_reduce(row_neg, s_sb, AX.X, ALU.max, negate=True).then_inc(s["g_max"], 1)
                dve.wait_ge(s["g_t_ps"], n + 1)
                for i in range(3):
                    V.tensor_copy(pt_sb[:, 4 * i:4 * i + 4, :],
                                  ps[:, 4 + i, :].rearrange("p (n q) -> p n q", n=4)).then_inc(s["g_pt"], 1)
                rows = KBL[-1][1]
                V.tensor_copy(pt_sb[0:rows, NB - 1, :], ps[0:rows, 3, 0:P]).then_inc(s["g_pt"], 1)
                dve.wait_ge(s["g_pv"], n + 1)
            V.tensor_copy(o_sb[:, 0:2 * P], ps[:, 7, 0:2 * P]).then_inc(s["g_o"], 1)
            dve.wait_ge(s["g_fin"], b + 1)
            num, den = ps[:, 6, 0:NQ], ps[:, 6, NQ:2 * NQ]
            V.reciprocal(g_recip, den).then_inc(s["g_step"], 1)
            V.tensor_scalar(real, den, 0.0, None, ALU.is_gt).then_inc(s["g_step"], 1)
            dve.wait_ge(s["g_step"], 3 * b + 2)
            V.tensor_tensor(real_all, real_all, real, ALU.mult).then_inc(s["g_step"], 1)
            dve.wait_ge(s["g_step"], 3 * b + 3)
            V.tensor_tensor(AT[:, bass.ds(b * NQ, NQ)], num, g_recip, ALU.mult).then_inc(s["g_done"], 1)
            dve.wait_ge(s["g_done"], b + 2)

        def all_rows(dve, values, worst, i):
            V.tensor_reduce(worst, values, AX.X, ALU.min).then_inc(s["worst"], 1)
            dve.wait_ge(s["count_ps"], i + 1)
            V.tensor_copy(flag[:, i:i + 1], ps[0:1, 5, i:i + 1]).then_inc(s["flag_ready"], 1)

        QS = [slot(1), AT[:, :]]
        bf = lambda at: arena[:, at:at + TOK // 2].bitcast(BF16)
        v_parts = [bf(9 * TOK), bf(9 * TOK + TOK // 2), bf(10 * TOK)]
        v_rest = slot(11)
        v_stack = [bf(at)[0:6 * H, :] for at in (6 * TOK, 6 * TOK + TOK // 2, 13 * TOK, 13 * TOK + TOK // 2)]

        def by_query(buf):
            return buf.rearrange("p (b t) -> p t b", t=B)

        def query_state(engine, v, c):
            return engine.tensor_tensor(chunk(QS[v % 2], c).rearrange("p (t b) -> p t b", b=NQ),
                                        chunk(slot(4), c).rearrange("p (t b) -> p t b", b=NQ),
                                        by_query(slot(11 + v % 2))[:, 8 * c:8 * c + 8, :], ALU.mult)

        def gemm(pe, weight, src, banks, done, ready=None, free=None, c0=0, rows=P):
            for c in range(NC):
                if ready is not None:
                    pe.wait_ge(*(ready(c) if callable(ready) else (s[ready], c + 1)))
                if free is not None:
                    pe.wait_ge(s[free], c + 1)
                PE.matmul(ps[0:rows, banks + c, :], weight, chunk(src, c), start=True, stop=True)\
                    .then_inc(s[done], 1)

        def summed(v, c):
            return NC * v + (c + 1) % NC + 1

        def pe_values_out(pe, v):
            for c in range(NC):
                if v == 0:
                    pe.wait_ge(s["decay"], c + 1)
                else:
                    pe.wait_ge(s["kv"], NC * (v - 1) + c + 1)
                PE.matmul(ps[:, c, :], spread[:, (v % 2) * P:(v % 2 + 1) * P], chunk(v_stack[v // 2], c),
                          start=True, stop=True).then_inc(s["vv_ps"], 1)

        def pe_head_sum(pe, v, c):
            if c < QS_POOL:
                pe.wait_ge(s["qs"], QS_POOL * v + c + 1)
            else:
                pe.wait_ge(s["qs_dve"], v + 1)
            if v == 0:
                pe.wait_ge(s["og"], c + 1)
            PE.matmul(ps[:, 4 + c, :], w("head_sum")[:, v * P:(v + 1) * P], chunk(QS[v % 2], c),
                      start=(v == 0), stop=(v == D - 1)).then_inc(s["osum_ps"], 1)

        hidden = lambda c: slot(4 + c % 2)
        gates = lambda k: slot(7)[:, (k % 4) * CH:(k % 4 + 1) * CH]
        tiles = lambda buf, half, n=64: buf[:, half * 1024:half * 1024 + NT * n].rearrange("p (i s) -> p i s", i=NT)
        logits, replaced = tiles(slot(4), 0), tiles(slot(4), 1)
        expo = tiles(slot(5), 0)
        top = tiles(slot(6), 1, 8)
        alphas = slot(12)
        alpha = alphas.rearrange("p (i s) -> p i s", i=NT)
        xtok = slot(7).rearrange("p (i d) -> p i d", i=NT)
        att = slot(7).rearrange("p (i t) -> p i t", i=NT)
        att_in = tiles(slot(11), 1)
        vs = slot(1).rearrange("p (i d) -> p i d", i=NT)
        svp = slot(3).rearrange("p (i d) -> p i d", i=NT)

        def diagonal(dst, src, done):
            for u in range(2):
                rows = slice(64 * u, 64 * u + 64)
                V.tensor_tensor(dst[rows, :, 64 * u:64 * u + 64], src[rows, :, :],
                                row16b[rows, :].unsqueeze(2).broadcast_to([64, NT, SLOTS]), ALU.mult)\
                    .then_inc(s[done], 1)
        bg2_scaled = small[:, 463:464]
        slot_sum = small[:, 460:461]
        tau_inv = small[:, 461:462]
        cool_b2 = small[:, 0:SLOTS]
        hid_bias = small[:, 462:463]
        gh_n = small[:, 512:512 + SLOTS]
        gate_bias = small[:, 576:578]
        row16 = small[:, 704:720]
        row16b = small[:, 720:736]

        def over_batches(tile):
            return tile.unsqueeze(1).broadcast_to([P, PB, SLOTS])

        block = stack.enter_context(nc.Block())
        HALF = B // 2

        @block.sync
        def _(sp):
            sp.dma_start(WA[:, :], w_a).then_inc(s["wa_in"], 16)
            sp.dma_start(ctx_sb[0], ctx_t[0, :, :]).then_inc(ctx_in[0], 16)
            sp.dma_start(X[:, :], x_t).then_inc(s["x_in"], 16)
            sp.dma_start(ctx_sb[1], ctx_t[1, :, :]).then_inc(ctx_in[1], 16)
            sp.wait_ge(s["turn_out"], 4 + 2)
            stack_keys(nc.sync, 0)
            sp.wait_ge(s["q_low"], NC)
            for g in range(2):
                stack_queries(nc.sync, g)
            sp.dma_start(WB[:, :], w_b).then_inc(s["wb_in"], 16)
            with sp.Fori(0, HALF - 1) as j:
                for u in range(2):
                    sp.wait_ge(s["turn_ps"], UNITS * (2 * j + u) + 8)
                    sp.dma_start(ctx_sb[u], ctx_t[bass.ds(2 * j + u + 2, 1), :, :].rearrange("a c k -> (a c) k"))\
                        .then_inc(ctx_in[u], 16)
                    sp.wait_ge(s["turn_out"], UNITS * (2 * j + u) + 8 + 4 + 2)
                    stack_keys(nc.sync, 1 - u)
            sp.wait_ge(s["turn_out"], UNITS * (B - 2) + 8 + 4 + 2)
            stack_keys(nc.sync, 1)
            sp.wait_ge(s["flag_ready"], 1)
            f = sp.value_load(flag[0:1, 0:1])
            with sp.If(f < P):
                with sp.Fori(0, B) as b:
                    g_load(sp, b)
            sp.wait_ge(s["gla_step"], 2 + 3 * NC)
            for k in range(4):
                for a in range(3):
                    sp.dma_start(v_stack[k][32 * a:32 * a + 32, :], v_parts[a][32 * k:32 * k + 32, :])\
                        .then_inc(s["v_stacked"], 16)
            for c in range(NC):
                sp.wait_ge(s["final"], c + 1)
                sp.dma_start(out_t[:, c * CH:(c + 1) * CH], chunk(AT, c)).then_inc(s["out_done"], 16)
            sp.wait_ge(s["out_done"], 16 * NC)

        @block.gpsimd
        def _(pool):
            for u in range(2):
                G.memset(v_sb[u][:, :, :, 16:32], 1.0).then_inc(s["ones_set"], 1)
            pool.wait_ge(s["wa_in"], 16)
            G.tensor_copy(back.rearrange("p (k n) -> p k n", n=P),
                          w("pick").unsqueeze(2).broadcast_to([P, NC * SUBS[""], P])).then_inc(s["back_set"], 1)
            pool.wait_ge(s["q_stacked"], 16 * NSTACK)
            with pool.Fori(0, HALF) as j:
                for u in range(2):
                    pool.wait_ge(s["q_free"], 2 * j + u + 1)
                    q_blocks(2 * j + u, u).then_inc(s["q_ready"], 1)
            pool.wait_ge(s["flag_ready"], 1)
            f = pool.value_load(flag[0:1, 0:1])
            with pool.If(f < P):
                with pool.Fori(0, B) as b:
                    pool.wait_ge(s["g_done"], b + 1)
                    g_q_blocks(b).then_inc(s["g_q"], 1)
            for v in range(D):
                for c in range(QS_POOL):
                    pool.wait_ge(s["scan"], v + 1)
                    if v >= 2:
                        pool.wait_ge(s["osum_ps"], summed(v - 2, c))
                    query_state(G, v, c).then_inc(s["qs"], 1)
            for c in range(NC):
                pool.wait_ge(s["x2"], c + 1)
                G.tensor_tensor(chunk(X, c), chunk(X, c), chunk(slot(10), c), ALU.add).then_inc(s["x12"], 1)
            pool.wait_ge(s["qs"], QS_POOL * D)
            pool.wait_ge(s["qs_dve"], D)
            G.memset(alphas, 0.0).then_inc(s["zeroed"], 1)
            pool.wait_ge(s["top"], NT)
            G.tensor_tensor(expo, logits, top[:, :, 0:1].broadcast_to([P, NT, SLOTS]), ALU.subtract)\
                .then_inc(s["shifted"], 1)
            pool.wait_ge(s["si_ps"], NC)
            G.memset(slot(7), 0.0).then_inc(s["zeroed"], 1)

        @block.tensor
        def _(pe):
            PE.sem_inc(s["pv_done"], 2)
            PE.sem_inc(s["q_free"], 2)
            pe.wait_ge(s["wa_in"], 16)
            pe.wait_ge(ctx_in[0], 16)
            for i in range(4):
                pe.wait_ge(s["turn_out"], i + 1)
                pe_keys(0, i, 6 + i % 2).then_inc(s["turn_ps"], 1)
            norm_pe(pe, "norm1", lambda c: pe.wait_ge(s["x_in"], 16))
            pe.wait_ge(s["turn_out"], 6)
            gemm(pe, w("x_wq"), AT, 4, "q_ps", ready=lambda c: norm_ready("norm1", c))
            pe.wait_ge(s["q_sb"], NC)
            for i in range(4, 8):
                pe.wait_ge(s["turn_out"], i + 1)
                pe_values(0, i % 4, 6 + i % 2).then_inc(s["turn_ps"], 1)
            pe.wait_ge(s["ones_set"], 2)
            pe_scores(pe, 0, 0, 0)
            pe_body(pe, 0, first=True)
            pe.wait_ge(s["wb_in"], 16)
            with pe.Fori(1, HALF - 1) as j:
                pe_body(pe, j)
            pe_body(pe, HALF - 1, last=True)
            pe.wait_ge(s["wb_in"], 16)
            pe.wait_ge(s["worst"], 1)
            PE.matmul(ps[0:1, 5, 0:1], okay_min, w("ones")[:, 0:1], start=True, stop=True).then_inc(s["count_ps"], 1)
            pe.wait_ge(s["flag_ready"], 1)
            f = pe.value_load(flag[0:1, 0:1])
            with pe.If(f < P):
                with pe.Fori(0, B) as b:
                    g_pe(pe, b)
                pe.wait_ge(s["worst"], 2)
                PE.matmul(ps[0:1, 5, 1:2], real_min, w("ones")[:, 0:1], start=True, stop=True)\
                    .then_inc(s["count_ps"], 1)
                PE.matmul(ps[:, 4, 0:B], w("x_wv"), ctx_mean, start=True, stop=True).then_inc(s["v_mean_ps"], 1)
            gemm(pe, w("x_wo"), AT, 4, "xo_ps", ready="ao")
            norm_pe(pe, "norm2", lambda c: pe.wait_ge(s["x1"], c + 1))
            pe.wait_ge(s["wb_in"], 16)
            rms1_pe(pe)
            gemm(pe, w("g_wv"), slot(3), 4, "v_ps", ready=lambda c: (s["rms_ready"], c + 1))
            gemm(pe, w("g_wq"), slot(3), 0, "gq_ps")
            gemm(pe, w("g_wk"), slot(3), 4, "gk_ps", ready=lambda c: (s["gla_step"], 3 + 3 * c))
            gemm(pe, w("g_wg1"), slot(3), 0, "g1_ps", free="gq")
            gemm(pe, w("g_wog"), slot(3), 4, "og_ps", free="gk")
            gemm(pe, w("g_wg2"), slot(2), 0, "g2_ps", ready="g1", free="g1")
            pe.wait_ge(s["v_stacked"], 16 * V_COPIES)
            pe_values_out(pe, 0)
            pe_values_out(pe, 1)
            for v in range(D):
                for c in (NC - 1, 0, 1):
                    pe_head_sum(pe, v, c)
                if v + 2 < D:
                    pe_values_out(pe, v + 2)
                pe_head_sum(pe, v, 2)
            norm_pe(pe, "normo", lambda c: pe.wait_ge(s["o"], c + 1))
            gemm(pe, w("g_wo"), slot(9), 4, "wo_ps", ready="gated")
            rms2_pe(pe)
            for c in range(NC):
                pe.wait_ge(s["rms_ready"], NC + c + 1)
                for m in range(4):
                    k = 4 * c + m
                    if k >= 2:
                        pe.wait_ge(s["hid"], k - 1)
                    PE.matmul(ps[:, k % 2, :], w("w_gate")[:, m * P:(m + 1) * P], chunk(slot(3), c),
                              start=True, stop=True).then_inc(s["gate_ps"], 1)
                    PE.matmul(ps[:, 2 + k % 2, :], w("w_up")[:, m * P:(m + 1) * P], chunk(slot(3), c),
                              start=True, stop=True).then_inc(s["up_ps"], 1)
                for m in range(4):
                    pe.wait_ge(s["hid"], 4 * c + m + 1)
                    mm = PE.matmul(ps[:, 4 + c, :], w("w_down")[:, m * C:(m + 1) * C],
                                   hidden(c)[:, m * CH:(m + 1) * CH], start=(m == 0), stop=(m == 3))
                mm.then_inc(s["down_ps"], 1)

            def slot_part():
                pe.wait_ge(s["router_step"], 6)
                PE.matmul(ps[:, 7, 0:1], w("w1s"), slot_sum, start=True, stop=True).then_inc(s["hb_ps"], 1)

            norm_pe(pe, "norm3", lambda c: pe.wait_ge(s["x3"], c + 1), between=slot_part)
            pe.wait_ge(s["hb"], 1)
            gemm(pe, w("w1x"), slot(0), 4, "h_ps", ready=lambda c: norm_ready("norm3", c))
            for i in range(NT):
                if i == 0:
                    pe.wait_ge(*norm_ready("norm3", NC - 1))
                pe.wait_ge(s["h"], i // 4 + 1)
                PE.matmul(ps[:, i // 8, (i % 8) * 64:(i % 8 + 1) * 64], slot(3)[:, i * P:(i + 1) * P], w("w2"),
                          start=True, stop=True).then_inc(s["logit_ps"], 1)
            for i in range(NT):
                PE.transpose(ps[:, 4 + i // 4, (i % 4) * P:(i % 4 + 1) * P], slot(0)[:, i * P:(i + 1) * P], w("ident"))\
                    .then_inc(s["xt_ps"], 1)

            pe.wait_ge(s["alpha"], 2)
            for i in range(NT):
                PE.transpose(ps[:, i // 4, (i % 4) * P:(i % 4 + 1) * P], alpha[:, i, :], w("ident"))\
                    .then_inc(s["at_ps"], 1)
            pe.wait_ge(s["xt"], NC)
            for i in range(NT):
                mm = PE.matmul(ps[:, 4 + i // 4, (i % 4) * P:(i % 4 + 1) * P], xtok[:, i, :], alpha[:, i, :],
                               start=True, stop=True)
                if i % 4 == 3:
                    mm.then_inc(s["si_ps"], 1)
            pe.wait_ge(s["at"], 1)
            for c in range(NC):
                mm = mean_of(alphas, c, "", 0)
            mm.then_inc(s["sd_ps"], 1)
            pe.wait_ge(s["sd"], 2)
            for c in range(NC):
                pe.wait_ge(s["at"], c + 1)
                spread_back(stat[0], "", c, c).then_inc(s["sd_back"], 1)
            def gate(k, banks, done, ready):
                for c in range(NC):
                    ready(c)
                    PE.matmul(ps[:, banks + c, :], w("wih")[:, k * P:(k + 1) * P], chunk(slot(9), c),
                              start=True, stop=False)
                    PE.matmul(ps[:, banks + c, :].rearrange("p (b s) -> p b s", b=PB), w("whh")[:, k * P:(k + 1) * P],
                              over_batches(w("slots")), start=False, stop=True).then_inc(s[done], 1)

            gate(0, 4, "gr_ps", lambda c: pe.wait_ge(s["si"], c + 1))
            PE.matmul(ps[:, 0, 0:SLOTS], w("whh")[:, 2 * P:3 * P], w("slots"), start=True, stop=True)\
                .then_inc(s["gh_ps"], 1)
            gemm(pe, w("wih")[:, 2 * P:3 * P], slot(9), 4, "gn_ps", free="r")
            pe.wait_ge(s["gh"], 2)
            gate(1, 0, "gz_ps", lambda c: None)
            gemm(pe, w("s_wq"), slot(5), 0, "sq_ps", ready="snew")
            gemm(pe, w("s_wk"), slot(5), 4, "sk_ps")
            pe.wait_ge(s["sk"], NC)
            pe.wait_ge(s["sq"], NC)
            for i in range(NT):
                mm = PE.matmul(ps[:, i // 4, (i % 4) * P:(i % 4 + 1) * P], slot(9)[:, i * P:(i + 1) * P],
                               slot(10)[:, i * P:(i + 1) * P], start=True, stop=True)
            mm.then_inc(s["sc_ps"], 1)
            for i in range(NT):
                mm = PE.matmul(ps[:, 4 + i // 4, (i % 4) * P:(i % 4 + 1) * P], slot(5)[:, i * P:(i + 1) * P],
                               w("s_wv"), start=True, stop=True)
                if i % 4 == 3:
                    mm.then_inc(s["sv_ps"], 1)
            pe.wait_ge(s["attn"], 2)
            for i in range(NT):
                t = PE.transpose(ps[:, i // 4, (i % 4) * P:(i % 4 + 1) * P], att[:, i, :], w("ident"))
                if i % 4 == 3:
                    t.then_inc(s["attt_ps"], 1)
            for i in range(NT):
                if i % 4 == 0:
                    pe.wait_ge(s["sv"], NC)
                    pe.wait_ge(s["attt"], i // 4 + 1)
                mm = PE.matmul(ps[:, 4 + i // 4, (i % 4) * P:(i % 4 + 1) * P], vs[:, i, :],
                               slot(12)[:, i * P:(i + 1) * P], start=True, stop=True)
                if i % 4 == 3:
                    mm.then_inc(s["comm_ps"], 1)
            norm_pe(pe, "norms", lambda c: pe.wait_ge(s["y"], c + 1))
            for i in range(NT):
                if i % 4 == 0:
                    pe.wait_ge(s["y2"], i // 4 + 1)
                mm = PE.matmul(ps[:, 4 + i // 4, (i % 4) * P:(i % 4 + 1) * P], slot(10)[:, i * P:(i + 1) * P],
                               w("s_wvp"), start=True, stop=True)
                if i % 4 == 3:
                    mm.then_inc(s["svp_ps"], 1)
            for i in range(NT):
                if i % 4 == 0:
                    pe.wait_ge(s["svp"], i // 4 + 1)
                mm = PE.matmul(ps[:, i // 4, (i % 4) * P:(i % 4 + 1) * P], svp[:, i, :],
                               slot(8)[:, i * P:(i + 1) * P], start=True, stop=True)
                if i % 4 == 3:
                    mm.then_inc(s["read_ps"], 1)
            gemm(pe, w("s_wo"), slot(11), 4, "fin_ps", ready="read")

        @block.scalar
        def _(act):
            A.sem_inc(s["exp_done"], 2)
            act.wait_ge(s["first_set"], 1)
            norm_act(act, "norm1")
            for c in range(NC):
                act.wait_ge(s["q_sb"], c + 1)
                A.copy(chunk(q_parts[:, 0, :], c), chunk(QT, c)).then_inc(s["q_high"], 1)
            act.wait_ge(s["q_low"], NC)
            for g in range(2, 4):
                stack_queries(nc.scalar, g)
            with act.Fori(0, HALF) as j:
                for u in range(2):
                    act_batch(act, j, u)
            act.wait_ge(s["flag_ready"], 1)
            f = act.value_load(flag[0:1, 0:1])
            with act.If(f < P):
                with act.Fori(0, B) as b:
                    for h in range(PAIRS):
                        act.wait_ge(s["g_max"], PAIRS * b + h + 1)
                        A.activation(s_sb, s_sb, ACT.Exp, bias=row_neg).then_inc(s["g_exp"], 1)
            norm_act(act, "norm2")
            rms1_act(act)
            for c in range(NC):
                act.wait_ge(s["v_ps"], c + 1)
                A.copy(chunk(v_parts[0], c), ps[:, 4 + c, :]).then_inc(s["v_high"], 1)
            for c in range(NC):
                act.wait_ge(s["gq_ps"], c + 1)
                A.copy(chunk(slot(4), c), ps[:, c, :]).then_inc(s["gq"], 1)
            for c in range(NC):
                act.wait_ge(s["g1_ps"], c + 1)
                A.activation(chunk(slot(2), c), ps[:, c, :], ACT.Silu, bias=bias("bg1"))\
                    .then_inc(s["g1"], 1)
            for c in range(NC):
                act.wait_ge(s["og_ps"], c + 1)
                A.activation(chunk(slot(8), c), ps[:, 4 + c, :], ACT.Silu, bias=bias("bog")).then_inc(s["og"], 1)
            act.wait_ge(s["gla_step"], 1)
            for c in range(NC):
                act.wait_ge(s["g2_ps"], c + 1)
                A.activation(by_query(slot(7))[:, 8 * c:8 * c + 8, :],
                             ps[:, c, :].rearrange("p (t b) -> p t b", b=NQ), ACT.Sigmoid,
                             bias=bg2_scaled, scale=1.0 / 16.0).then_inc(s["decay"], 1)
            for c in range(NC):
                act.wait_ge(s["osum_ps"], summed(D - 1, c))
                A.copy(chunk(slot(6), c), ps[:, 4 + c, :]).then_inc(s["o"], 1)
            norm_act(act, "normo")
            rms2_act(act)
            for k in range(16):
                act.wait_ge(s["gate_ps"], k + 1)
                if k >= 4:
                    act.wait_ge(s["hid"], k - 3)
                A.activation(gates(k), ps[:, k % 2, :], ACT.Silu).then_inc(s["gate"], 1)
            norm_act(act, "norm3")
            act.wait_ge(s["hb"], 1)
            for c in range(NC):
                act.wait_ge(s["h_ps"], c + 1)
                A.activation(chunk(slot(3), c), ps[:, 4 + c, :], ACT.Gelu, bias=hid_bias)\
                    .then_inc(s["h"], 1)
            for c in range(NC):
                act.wait_ge(s["xt_ps"], 4 * c + 4)
                A.copy(chunk(slot(7), c), ps[:, 4 + c, :]).then_inc(s["xt"], 1)
            act.wait_ge(s["shifted"], 1)
            A.activation(expo, expo, ACT.Exp).then_inc(s["expo"], 1)
            for c in range(NC):
                act.wait_ge(s["at_ps"], 4 * c + 4)
                A.copy(chunk(slot(8), c), ps[:, c, :]).then_inc(s["at"], 1)
            act.wait_ge(s["gh"], 1)
            for c in range(NC):
                act.wait_ge(s["gr_ps"], c + 1)
                A.activation(chunk(slot(1), c), ps[:, 4 + c, :], ACT.Sigmoid, bias=gate_bias[:, 0:1])\
                    .then_inc(s["r"], 1)
            for c in range(NC):
                act.wait_ge(s["n_in"], c + 1)
                A.activation(chunk(slot(3), c), chunk(slot(3), c), ACT.Tanh, bias=bias("bih_n")).then_inc(s["n"], 1)
            for c in range(NC):
                act.wait_ge(s["gz_ps"], c + 1)
                A.activation(chunk(slot(2), c), ps[:, c, :], ACT.Sigmoid, bias=gate_bias[:, 1:2]).then_inc(s["z"], 1)
            for c in range(NC):
                act.wait_ge(s["sq_ps"], c + 1)
                A.activation(chunk(slot(9), c), ps[:, c, :], ACT.Identity, bias=bias("s_bq"))\
                    .then_inc(s["sq"], 1)
            for c in range(NC):
                act.wait_ge(s["sk_ps"], c + 1)
                A.activation(chunk(slot(10), c), ps[:, 4 + c, :], ACT.Identity, bias=bias("s_bk"))\
                    .then_inc(s["sk"], 1)
            act.wait_ge(s["att_in"], 2)
            A.activation(att_in, att_in, ACT.Exp, scale=DQ ** -0.5).then_inc(s["att_exp"], 1)
            for c in range(NC):
                act.wait_ge(s["sv_ps"], c + 1)
                A.copy(chunk(slot(1), c), ps[:, 4 + c, :]).then_inc(s["sv"], 1)
            norm_act(act, "norms")
            for c in range(NC):
                act.wait_ge(s["svp_ps"], c + 1)
                A.copy(chunk(slot(3), c), ps[:, 4 + c, :]).then_inc(s["svp"], 1)
            for c in range(NC):
                act.wait_ge(s["read_ps"], c + 1)
                A.activation(chunk(slot(11), c), ps[:, c, :], ACT.Identity, bias=bias("s_bvp")).then_inc(s["read"], 1)

        @block.vector
        def _(dve):
            V.sem_inc(s["turn_out"], 2)
            V.sem_inc(s["acc_out"], 2)
            V.sem_inc(s["fin_out"], 1)
            V.sem_inc(s["g_ctx_free"], 1)
            V.sem_inc(s["g_done"], 1)
            V.memset(eps[:, :], 1e-5).then_inc(s["first_set"], 1)
            V.memset(okay, 1.0).then_inc(s["first_set"], 1)
            V.memset(real_all, 1.0).then_inc(s["first_set"], 1)
            for i in range(4):
                dve.wait_ge(s["turn_ps"], i + 1)
                dve_keys(dve, i, 6 + i % 2, None, i + 1)
            norm_dve(dve, "norm1")

            def q_low(c):
                dve.wait_ge(s["q_high"], c + 1)
                V.tensor_tensor(chunk(q_parts[:, 1, :], c), chunk(QT, c), chunk(q_parts[:, 0, :], c), ALU.subtract)\
                    .then_inc(s["q_low"], 1)

            for c in range(NC):
                dve.wait_ge(s["q_ps"], c + 1)
                V.tensor_scalar(chunk(QT, c), ps[:, 4 + c, :], bias("x_bq"), SCALE, ALU.add, ALU.mult)\
                    .then_inc(s["q_sb"], 1)
                if c >= 1:
                    q_low(c - 1)
            q_low(NC - 1)
            for i in range(4, 8):
                dve.wait_ge(s["turn_ps"], i + 1)
                dve_values(0, i % 4, 6 + i % 2).then_inc(s["turn_out"], 1)
            dve.wait_ge(s["first_set"], 3)
            dve_body(dve, 0, first=True)
            with dve.Fori(1, HALF - 1) as j:
                dve_body(dve, j)
            dve_body(dve, HALF - 1, last=True)
            all_rows(dve, okay, okay_min, 0)
            dve.wait_ge(s["flag_ready"], 1)
            f = dve.value_load(flag[0:1, 0:1])
            with dve.If(f < P):
                with dve.Fori(0, B) as b:
                    g_dve(dve, b)
                all_rows(dve, real_all, real_min, 1)
                dve.wait_ge(s["v_mean_ps"], 1)
                V.tensor_scalar(v_mean, ps[:, 4, 0:B], 1.0 / NKV, None, ALU.mult).then_inc(s["v_mean"], 1)
                dve.wait_ge(s["v_mean"], 1)
                dve.wait_ge(s["flag_ready"], 2)
                nan = dve.value_load(flag[0:1, 1:2])
                with dve.If(nan < P):
                    V.tensor_copy(AT[:, :].rearrange("p (b q) -> p b q", b=B),
                                  v_mean.unsqueeze(2).broadcast_to([P, B, NQ])).then_inc(s["v_mean"], 1)
                    dve.wait_ge(s["v_mean"], 2)
                V.sem_inc(s["g_end"], 1)
            for c in range(NC):
                V.tensor_scalar(chunk(AT, c), chunk(AT, c), bias("x_bv"), None, ALU.add).then_inc(s["ao"], 1)
            for c in range(NC):
                dve.wait_ge(s["xo_ps"], c + 1)
                V.scalar_tensor_tensor(chunk(X, c), ps[:, 4 + c, :], bias("x_bo"), chunk(X, c), ALU.add, ALU.add)\
                    .then_inc(s["x1"], 1)
            norm_dve(dve, "norm2", between=lambda: rms1_stats(dve))
            dve.wait_ge(s["wb_in"], 16)
            V.tensor_scalar(bg2_scaled, bias("bg2"), 1.0 / 16.0, None, ALU.mult).then_inc(s["gla_step"], 1)
            V.tensor_copy(spread[:, :], w("spread")).then_inc(s["gla_step"], 1)
            rms1_dve(dve)
            for c in range(NC):
                dve.wait_ge(s["v_high"], c + 1)
                V.tensor_tensor(chunk(v_rest, c), ps[:, 4 + c, :], chunk(v_parts[0], c), ALU.subtract)\
                    .then_inc(s["gla_step"], 1)
                dve.wait_ge(s["gla_step"], 3 + 3 * c)
                V.tensor_copy(chunk(v_parts[1], c), chunk(v_rest, c)).then_inc(s["gla_step"], 1)
                dve.wait_ge(s["gla_step"], 4 + 3 * c)
                V.tensor_tensor(chunk(v_parts[2], c), chunk(v_rest, c), chunk(v_parts[1], c), ALU.subtract)\
                    .then_inc(s["gla_step"], 1)
            for c in range(NC):
                dve.wait_ge(s["gk_ps"], c + 1)
                V.tensor_copy(chunk(slot(5), c), ps[:, 4 + c, :]).then_inc(s["gk"], 1)
            dve.wait_ge(s["decay"], NC)
            dve.wait_ge(s["gk"], NC)
            V.memset(slot(7).rearrange("p (b t) -> p b t", t=B)[:, :, 0:1], 0.0).then_inc(s["gla_step"], 1)
            dve.wait_ge(s["gla_step"], 3 + 3 * NC)
            for v in range(D):
                for c in range(NC):
                    dve.wait_ge(s["vv_ps"], NC * v + c + 1)
                    if v >= 2:
                        dve.wait_ge(s["scan"], v - 1)
                    V.tensor_tensor(by_query(slot(9 + v % 2))[:, 8 * c:8 * c + 8, :],
                                    ps[:, c, :].rearrange("p (t b) -> p t b", b=NQ),
                                    chunk(slot(5), c).rearrange("p (t b) -> p t b", b=NQ), ALU.mult)\
                        .then_inc(s["kv"], 1)
                dve.wait_ge(s["kv"], NC * (v + 1))
                if v >= 2:
                    dve.wait_ge(s["qs"], QS_POOL * (v - 1))
                    dve.wait_ge(s["qs_dve"], v - 1)
                V.tensor_tensor_scan(slot(11 + v % 2), slot(7), slot(9 + v % 2), 0.0, ALU.mult, ALU.add)\
                    .then_inc(s["scan"], 1)
                dve.wait_ge(s["scan"], v + 1)
                if v >= 2:
                    dve.wait_ge(s["osum_ps"], summed(v - 2, NC - 1))
                query_state(V, v, NC - 1).then_inc(s["qs_dve"], 1)
            norm_dve(dve, "normo")
            for c in range(NC):
                dve.wait_ge(*norm_ready("normo", c))
                V.tensor_tensor(chunk(slot(9), c), chunk(slot(6), c), chunk(slot(8), c), ALU.mult)\
                    .then_inc(s["gated"], 1)
            for c in range(NC):
                dve.wait_ge(s["wo_ps"], c + 1)
                V.tensor_tensor(chunk(slot(10), c), chunk(slot(0), c), ps[:, 4 + c, :], ALU.add).then_inc(s["x2"], 1)
            rms2_dve(dve)
            for c in range(NC):
                for m in range(4):
                    k = 4 * c + m
                    dve.wait_ge(s["gate"], k + 1)
                    dve.wait_ge(s["up_ps"], k + 1)
                    if c >= 2:
                        dve.wait_ge(s["down_ps"], c - 1)
                    V.tensor_tensor(hidden(c)[:, m * CH:(m + 1) * CH], gates(k), ps[:, 2 + k % 2, :], ALU.mult)\
                        .then_inc(s["hid"], 1)
                dve.wait_ge(s["down_ps"], c + 1)
                dve.wait_ge(s["x12"], c + 1)
                V.tensor_tensor(chunk(X, c), chunk(X, c), ps[:, 4 + c, :], ALU.add).then_inc(s["x3"], 1)
            V.tensor_reduce(slot_sum, w("slots"), AX.X, ALU.add).then_inc(s["router_step"], 1)
            V.scalar_tensor_tensor(tau_inv, bias("tau"), -1.0, bias("tau"), ALU.mult, ALU.max)\
                .then_inc(s["router_step"], 1)
            dve.wait_ge(s["router_step"], 2)
            V.tensor_scalar(tau_inv, tau_inv, 0.1, None, ALU.add).then_inc(s["router_step"], 1)
            dve.wait_ge(s["router_step"], 3)
            V.reciprocal(tau_inv, tau_inv).then_inc(s["router_step"], 1)
            dve.wait_ge(s["router_step"], 4)
            V.tensor_scalar(cool_b2, w("b2"), tau_inv, None, ALU.mult).then_inc(s["router_step"], 1)
            dve.wait_ge(s["router_step"], 1)
            V.tensor_scalar(slot_sum, slot_sum, 1.0 / SLOTS, None, ALU.mult).then_inc(s["router_step"], 1)

            def hidden_bias():
                dve.wait_ge(s["hb_ps"], 1)
                V.tensor_tensor(hid_bias, ps[:, 7, 0:1], bias("b1"), ALU.add).then_inc(s["hb"], 1)

            norm_dve(dve, "norm3", between=hidden_bias)
            dve.wait_ge(s["router_step"], 5)
            dve.wait_ge(s["logit_ps"], NT)
            V.scalar_tensor_tensor(logits, ps[:, 0:2, :].rearrange("p a (i s) -> p (a i) s", s=64), tau_inv,
                                   cool_b2.unsqueeze(1).broadcast_to([P, NT, SLOTS]), ALU.mult, ALU.add)\
                .then_inc(s["router_step"], 1)
            dve.wait_ge(s["router_step"], 7)
            for i in range(NT):
                V.max(top[:, i, :], logits[:, i, :]).then_inc(s["top"], 1)
            dve.wait_ge(s["top"], NT)
            for i in range(NT):
                V.match_replace(replaced[:, i, :], top[:, i, :], logits[:, i, :], PICKED).then_inc(s["picked"], 1)
            dve.wait_ge(s["picked"], NT)
            dve.wait_ge(s["expo"], 1)
            V.scalar_tensor_tensor(expo, replaced, PICKED, expo, ALU.is_le, ALU.mult).then_inc(s["router_step"], 1)
            dve.wait_ge(s["router_step"], 8)
            V.tensor_reduce(row16, expo, AX.X, ALU.add).then_inc(s["router_step"], 1)
            dve.wait_ge(s["router_step"], 9)
            V.reciprocal(row16b, row16).then_inc(s["router_step"], 1)
            dve.wait_ge(s["router_step"], 10)
            dve.wait_ge(s["zeroed"], 1)
            diagonal(alpha, expo, "alpha")
            gates_from = lambda name: WHERE["bias_b"][1] + BIAS_B.index(name)
            V.tensor_tensor(gate_bias, WB[:, gates_from("bih_r"):gates_from("bih_r") + 2],
                            WB[:, gates_from("bhh_r"):gates_from("bhh_r") + 2], ALU.add).then_inc(s["gh"], 1)
            dve.wait_ge(s["sd_ps"], 1)
            weight_sums = stat[0][:, 0:CH // 4]
            V.tensor_scalar(weight_sums, ps[:, 0, 0:CH // 4], 1e-8 / P, None, ALU.add).then_inc(s["sd"], 1)
            dve.wait_ge(s["sd"], 1)
            V.reciprocal(weight_sums, weight_sums).then_inc(s["sd"], 1)
            for c in range(NC):
                dve.wait_ge(s["sd_back"], c + 1)
                dve.wait_ge(s["si_ps"], c + 1)
                V.tensor_copy(chunk(slot(10), c), ps[:, c, :]).then_inc(s["sd"], 1)
                dve.wait_ge(s["sd"], c + 3)
                V.scalar_tensor_tensor(chunk(slot(9), c), ps[:, 4 + c, :], 1.0 / P, chunk(slot(10), c),
                                       ALU.mult, ALU.mult)\
                    .then_inc(s["si"], 1)
            dve.wait_ge(s["gh_ps"], 1)
            V.tensor_scalar(gh_n, ps[:, 0, 0:SLOTS], bias("bhh_n"), None, ALU.add).then_inc(s["gh"], 1)
            dve.wait_ge(s["gh"], 2)
            rows = lambda c, bank: ps[:, bank + c, :].rearrange("p (b s) -> p b s", b=PB)
            part = lambda k, c: chunk(slot(k), c).rearrange("p (b s) -> p b s", b=PB)
            for c in range(NC):
                dve.wait_ge(s["r"], c + 1)
                V.tensor_tensor(part(3, c), part(1, c), over_batches(gh_n), ALU.mult).then_inc(s["rn"], 1)
                dve.wait_ge(s["rn"], c + 1)
                dve.wait_ge(s["gn_ps"], c + 1)
                V.tensor_tensor(part(3, c), part(3, c), rows(c, 4), ALU.add).then_inc(s["n_in"], 1)

            def mix_difference(c):
                dve.wait_ge(s["n"], c + 1)
                V.tensor_tensor(part(4, c), over_batches(w("slots")), part(3, c), ALU.subtract).then_inc(s["mix"], 1)

            mix_difference(0)
            for c in range(NC):
                if c + 1 < NC:
                    mix_difference(c + 1)
                dve.wait_ge(s["mix"], max(2 * c, 1))
                dve.wait_ge(s["z"], c + 1)
                V.tensor_tensor(part(4, c), part(4, c), part(2, c), ALU.mult).then_inc(s["mix"], 1)
                dve.wait_ge(s["mix"], min(2 * c + 3, 2 * NC))
                V.tensor_tensor(part(5, c), part(4, c), part(3, c), ALU.add).then_inc(s["snew"], 1)
            dve.wait_ge(s["sc_ps"], 1)
            for u in range(2):
                rows = slice(64 * u, 64 * u + 64)
                scores = ps[rows, 0:4, :].rearrange("p a (i t) -> p (a i) t", t=P)[:, :, 64 * u:64 * u + 64]
                V.tensor_reduce(row16[rows, :], scores, AX.X, ALU.max).then_inc(s["att_step"], 1)
                dve.wait_ge(s["att_step"], u + 1)
                V.tensor_tensor(att_in[rows, :, :], scores, row16[rows, :].unsqueeze(2).broadcast_to([64, NT, SLOTS]),
                                ALU.subtract).then_inc(s["att_in"], 1)
            dve.wait_ge(s["att_exp"], 1)
            V.tensor_reduce(row16, att_in, AX.X, ALU.add).then_inc(s["att_step"], 1)
            dve.wait_ge(s["att_step"], 3)
            V.reciprocal(row16b, row16).then_inc(s["att_step"], 1)
            dve.wait_ge(s["att_step"], 4)
            dve.wait_ge(s["zeroed"], 2)
            diagonal(att, att_in, "attn")
            for c in range(NC):
                dve.wait_ge(s["attt_ps"], c + 1)
                V.tensor_copy(chunk(slot(12), c), ps[:, c, :]).then_inc(s["attt"], 1)
            for c in range(NC):
                dve.wait_ge(s["comm_ps"], c + 1)
                V.scalar_tensor_tensor(chunk(slot(9), c), ps[:, 4 + c, :], bias("s_bv"), chunk(slot(5), c),
                                       ALU.add, ALU.add).then_inc(s["y"], 1)
            norm_dve(dve, "norms")
            for c in range(NC):
                dve.wait_ge(*norm_ready("norms", c))
                V.tensor_scalar(chunk(slot(10), c), chunk(slot(9), c), bias("ln_g"), bias("ln_b"),
                                ALU.mult, ALU.add).then_inc(s["y2"], 1)
            for c in range(NC):
                dve.wait_ge(s["fin_ps"], c + 1)
                V.scalar_tensor_tensor(chunk(AT, c), ps[:, 4 + c, :], bias("s_bo"), chunk(X, c), ALU.add, ALU.add)\
                    .then_inc(s["final"], 1)


def kernel(**inputs):
    import concourse.bacc as _bacc
    from concourse.bass_utils import run_bass_kernel_spmd as _run

    i = {k: np.asarray(v) for k, v in inputs.items()}
    a, f = (lambda k: i["L0_attn_" + k]), (lambda k: i["L0_ffn_" + k])
    one = np.ones((1, 1), np.float32)
    zero = np.zeros((1,), np.float32)
    head = np.arange(P) // D
    same = (head[:, None] == head[None, :]).astype(np.float32)
    mask = (head[:, None] == np.arange(H)[None, :]).astype(np.float32)
    sel_num, sel_den = np.zeros((P, 4, P), np.float32), np.zeros((P, 4, P), np.float32)
    for c in range(4):
        for r in range(2):
            for e in range(2):
                out = (2 * (c + 4 * r) + e) * D + np.arange(D)
                sel_num[32 * c + e * D + np.arange(D), 2 * r + e, out] = 1
                sel_den[32 * c + 16, 2 * r + e, out] = 1
    parts, head_parts = SUBS[""], SUBS["head_"]
    mean, head_mean = np.zeros((P, parts, 32), np.float32), np.zeros((P, head_parts, 32), np.float32)
    pick, head_back = np.zeros((P, NC, parts), np.float32), np.zeros((P, NC, head_parts, P), np.float32)
    for k in range(parts):
        rows = 32 // parts
        mean[:, k, k * rows:(k + 1) * rows] = 1.0 / C
        pick[32 * np.arange(NC) + k * rows, np.arange(NC), k] = 1
    for k in range(head_parts):
        head_mean[:, k, k * H:(k + 1) * H] = mask * np.float32(1.0 / D)
        for c in range(NC):
            head_back[32 * c + k * H + head, c, k, np.arange(P)] = 1
    head_sum = np.zeros((P, D, P), np.float32)
    for v in range(D):
        head_sum[np.arange(P), v, head * D + v] = 1
    spread = np.zeros((3, 2, H, 2, P), np.float32)
    for e in range(2):
        spread[:, e, head, e, np.arange(P)] = 1
    bih, bhh = f("bih").reshape(3, C), f("bhh").reshape(3, C)
    cols = dict(x_bq=i["L0_xattn_bq"], x_bk=i["L0_xattn_bk"], x_bv=i["L0_xattn_bv"], x_bo=i["L0_xattn_bo"],
                scale1=a("scale1"), scale2=a("scale2"), bg1=a("bg1"), bg2=a("bg2"), bog=a("bog"), b1=f("b1"),
                bih_r=bih[0], bih_z=bih[1], bih_n=bih[2], bhh_r=bhh[0], bhh_z=bhh[1], bhh_n=bhh[2],
                s_bq=f("bq"), s_bk=f("bk"), s_bv=f("bv"), ln_g=f("ln_g"), ln_b=f("ln_b"), s_bvp=f("bvp"),
                s_bo=f("bo"), tau=np.broadcast_to(f("tau"), (P,)), zero=np.broadcast_to(zero, (P,)))

    def columns(names):
        m = np.zeros((P, len(names)), np.float32)
        for n, name in enumerate(names):
            m[:len(cols[name]), n] = cols[name]
        return m

    mats = dict(
        x_wq=i["L0_xattn_Wq"], x_wk=i["L0_xattn_Wk"], x_wv=i["L0_xattn_Wv"], x_wo=i["L0_xattn_Wo"],
        centre=np.eye(P, dtype=np.float32) - np.float32(1.0 / C), mean=mean.reshape(P, -1),
        pick=pick.reshape(P, -1), head_centre=np.eye(P, dtype=np.float32) - same * np.float32(1.0 / D),
        head_mean=head_mean.reshape(P, -1), head_back=head_back.reshape(P, -1), head_mask=mask,
        row_mask=mask[:32, :4][np.arange(P) % 32], bias_a=columns(BIAS_A),
        sel_num=sel_num.reshape(P, -1), sel_den=sel_den.reshape(P, -1), ident=np.eye(P, dtype=np.float32),
        ones=np.ones((P, P), np.float32), g_wq=a("wq").T, g_wk=a("wk").T,
        g_wv=a("wv").T.reshape(C, H, D).transpose(0, 2, 1).reshape(C, C), spread=spread.reshape(-1, 2 * P),
        g_wg1=a("wg1").T,
        g_wg2=a("wg2").T, g_wog=a("wog").T, g_wo=a("wo").T, w_gate=a("w_gate").T, w_up=a("w_up").T,
        w_down=a("w_down").T.reshape(4, P, C).transpose(1, 0, 2).reshape(P, 4 * C),
        head_sum=head_sum.reshape(P, -1),
        bias_b=columns(BIAS_B), w1x=f("w1")[:C], w1s=f("w1")[C:], w2=f("w2"),
        b2=np.broadcast_to(f("b2"), (P, SLOTS)), wih=f("Wih").T, whh=f("Whh").T, s_wq=f("wq"), s_wk=f("wk"),
        s_wv=f("wv"), s_wvp=f("wvp"), s_wo=f("wo"), slots=f("slot_init").T)
    packed = [np.zeros((P, n), np.float32) for n in WIDTHS]
    for name, (g, col, rows, width) in WHERE.items():
        m = mats[name]
        packed[g][0:m.shape[0], col:col + m.shape[1]] = m
    arrays = {
        "x_t": np.ascontiguousarray(i["x"].reshape(TOK, C).T),
        "ctx_t": np.ascontiguousarray(i["ctx_768"].transpose(0, 2, 1)),
        "w_a": packed[0], "w_b": packed[1],
    }
    nc = _bacc.Bacc("TRN2", target_bir_lowering=False, num_devices=1)
    args = [nc.dram_tensor(k, v.shape, F32, kind="ExternalInput").ap() for k, v in arrays.items()]
    out = nc.dram_tensor("out_t", (C, TOK), F32, kind="ExternalOutput").ap()
    perceiver(nc, *args, out)
    r = _run(nc, [arrays], core_ids=[0])
    return np.ascontiguousarray(r.results[0]["out_t"].T).reshape(B, NQ, C)
```
